# Optimizing a Trainium2 kernel written in Bass

```python
import numpy as np
import jax
import jax.numpy as jnp

def _softmax(x, axis=-1):
    return jax.nn.softmax(x, axis=axis)

def _gelu(x):
    return jax.nn.gelu(x, approximate=True)

def _silu(x):
    return jax.nn.silu(x)

def _sigmoid(x):
    return jax.nn.sigmoid(x)

def _layernorm(x, axis=-1, eps=1e-05):
    m = jnp.mean(x, axis=axis, keepdims=True)
    v = jnp.var(x, axis=axis, keepdims=True)
    return (x - m) / jnp.sqrt(v + eps)

def _scatter_add(tgt, idx, src, axis=0):
    return tgt.at[idx].add(src)

def _segment_sum(src, seg, n):
    return jax.ops.segment_sum(src, seg, n)
kernel_name = 'mk_xattn_ffn_d2_seqx_r4_4f4fe9'

def setup_inputs(seed: int=0):
    np.random.seed(seed)
    _w = jnp.asarray

    def _rec_inputs():
        import jax
        import jax.numpy as jnp
        _rk = jax.random.key(seed)
        x = 0.0002417 + 0.9998 * jax.random.normal(jax.random.fold_in(_rk, 1), (16, 256, 256), jnp.float32)
        _lenS = 256 - jax.random.randint(jax.random.fold_in(_rk, 7), (16,), 0, max(1, 256 // 4) + 1, jnp.int32)
        _lenS2 = 256 - jax.random.randint(jax.random.fold_in(_rk, 8), (16,), 0, max(1, 256 // 4) + 1, jnp.int32)
        _ctx_1024P = jax.random.normal(jax.random.fold_in(_rk, 11), (16, 16, 256), jnp.float32)
        _ctx_1024c = jax.random.dirichlet(jax.random.fold_in(_rk, 511), 0.3 * jnp.ones((16,), jnp.float32), (16, 256))
        _ctx_1024t = jnp.einsum('bsk,bkd->bsd', _ctx_1024c, _ctx_1024P)
        _ctx_1024t = _ctx_1024t * jax.lax.rsqrt(jnp.mean(jnp.square(_ctx_1024t)) + 1e-12) * 0.953939
        ctx_1024 = 7.22013e-05 + 1.00017 * (_ctx_1024t + 0.3 * jax.random.normal(jax.random.fold_in(_rk, 611), (16, 256, 256), jnp.float32))
        return (x, ctx_1024)
    x, ctx_1024 = _rec_inputs()

    def _L0_xattn_setup():
        import jax, jax.numpy as jnp
        import numpy as np
        D_MODEL = 256
        B, S = (4, 512)
        key = jax.random.key(seed)
        ks = jax.random.split(key, 10)
        s = 1.0 / np.sqrt(D_MODEL)
        return {'k': jax.random.normal(ks[0], (B, S, D_MODEL), jnp.float32), 'v': jax.random.normal(ks[1], (B, S, D_MODEL), jnp.float32), 'q': jax.random.normal(ks[2], (B, S, D_MODEL), jnp.float32), 'Wk': jax.random.normal(ks[3], (D_MODEL, D_MODEL), jnp.float32) * s, 'Wv': jax.random.normal(ks[4], (D_MODEL, D_MODEL), jnp.float32) * s, 'bv': jnp.zeros((D_MODEL,), jnp.float32), 'Wq': jax.random.normal(ks[5], (D_MODEL, D_MODEL), jnp.float32) * s, 'bq': jnp.zeros((D_MODEL,), jnp.float32), 'Wo': jax.random.normal(ks[6], (D_MODEL, D_MODEL), jnp.float32) * s, 'bo': jnp.zeros((D_MODEL,), jnp.float32)}
    _L0_xattn_all = _L0_xattn_setup()
    _L0_xattn_in = {k: v for k, v in _L0_xattn_all.items() if k in ('Wk', 'Wv', 'bv', 'Wq', 'bq', 'Wo', 'bo')}
    del _L0_xattn_all

    def _L0_ffn_setup():
        import jax, jax.numpy as jnp
        import numpy as np
        H = 32
        MB = 2
        TOP_K = 2
        key = jax.random.key(seed)
        ks = jax.random.split(key, 8)
        B, S, D, E = (8, 256, 256, 8)
        Fd = 4 * D

        def w(k, shape, fan):
            return jax.random.normal(k, shape, jnp.float32) / np.float32(np.sqrt(fan))
        return dict(x=jax.random.normal(ks[0], (B, S, D), jnp.float32), ln_g=jnp.ones((D,), jnp.float32), ln_b=jnp.zeros((D,), jnp.float32), wq=w(ks[1], (D, D), D), wk=w(ks[2], (D, D), D), wv=w(ks[3], (D, D), D), wo=w(ks[4], (D, D), D), gate_w=w(ks[5], (E, D), D), w1=w(ks[6], (E, D, Fd), D), b1=jnp.zeros((E, Fd), jnp.float32), w2=w(ks[7], (E, Fd, D), Fd), b2=jnp.zeros((E, D), jnp.float32))
    _L0_ffn_all = _L0_ffn_setup()
    _L0_ffn_in = {k: v for k, v in _L0_ffn_all.items() if k in ('ln_g', 'ln_b', 'wq', 'wk', 'wv', 'wo', 'gate_w', 'w1', 'b1', 'w2', 'b2')}
    del _L0_ffn_all

    def _L1_xattn_setup():
        import jax, jax.numpy as jnp
        import numpy as np
        B, S, E, H = (4, 512, 128, 256)
        key = jax.random.key(seed)
        ks = jax.random.split(key, 8)
        s = 1.0 / np.sqrt(H)
        return {'hidden_states': jax.random.normal(ks[0], (B, S, H), jnp.float32), 'external_embeddings': jax.random.normal(ks[1], (B, E, H), jnp.float32), 'Wq': jax.random.normal(ks[2], (H, H), jnp.float32) * s, 'bq': jax.random.normal(ks[3], (H,), jnp.float32) * 0.02, 'Wk': jax.random.normal(ks[4], (H, H), jnp.float32) * s, 'bk': jax.random.normal(ks[5], (H,), jnp.float32) * 0.02, 'Wv': jax.random.normal(ks[6], (H, H), jnp.float32) * s, 'bv': jax.random.normal(ks[7], (H,), jnp.float32) * 0.02}
    _L1_xattn_all = _L1_xattn_setup()
    _L1_xattn_in = {k: v for k, v in _L1_xattn_all.items() if k in ('Wq', 'bq', 'Wk', 'bk', 'Wv', 'bv')}
    del _L1_xattn_all

    def _L1_ffn_setup():
        import jax, jax.numpy as jnp
        import numpy as np
        D_MODEL = 256
        N_HEADS = 16
        HEAD_DIM = D_MODEL // N_HEADS
        FFN_DIM = 1024
        N_EXPERTS = 8
        CAP_FRAC = 0.25
        MOE_TOKEN_DROPOUT = 0.2
        LN_EPS = 1e-05
        B, S = (4, 128)

        def _layer_norm(x, g, b):
            mu = x.mean(-1, keepdims=True)
            var = ((x - mu) ** 2).mean(-1, keepdims=True)
            return (x - mu) * jax.lax.rsqrt(var + LN_EPS) * g + b

        def _self_attention(x, wq, bq, wk, bk, wv, bv, wo, bo):
            b, s, d = x.shape
            q = ((x @ wq + bq) * HEAD_DIM ** (-0.5)).reshape(b, s, N_HEADS, HEAD_DIM)
            k = (x @ wk + bk).reshape(b, s, N_HEADS, HEAD_DIM)
            v = (x @ wv + bv).reshape(b, s, N_HEADS, HEAD_DIM)
            scores = jnp.einsum('bqhd,bkhd->bhqk', q, k)
            p = jax.nn.softmax(scores, axis=-1)
            o = jnp.einsum('bhqk,bkhd->bqhd', p, v).reshape(b, s, d)
            return o @ wo + bo

        def _moe_ffn(x, wr, w1, b1, w2, b2):
            T, D = x.shape
            C = int(np.ceil(CAP_FRAC * T))
            logits = x @ wr
            probs = jax.nn.softmax(logits, axis=-1)
            top1 = jnp.argmax(probs, axis=-1)
            m1 = jax.nn.one_hot(top1, N_EXPERTS, dtype=x.dtype)
            top2 = jnp.argmax(jnp.where(m1 > 0, -jnp.inf, logits), axis=-1)
            m2 = jax.nn.one_hot(top2, N_EXPERTS, dtype=x.dtype)
            loc1 = jnp.cumsum(m1, axis=0) - 1.0
            loc2 = jnp.cumsum(m2, axis=0) - 1.0 + m1.sum(0, keepdims=True)
            m1 = m1 * (loc1 < C)
            m2 = m2 * (loc2 < C)
            t1 = (probs * m1).sum(-1)
            t2 = (probs * m2).sum(-1)
            denom = jnp.maximum(t1 + t2, jnp.finfo(x.dtype).eps)
            t1, t2 = (t1 / denom, t2 / denom)
            tok = jnp.arange(T)
            s1 = loc1[tok, top1].astype(jnp.int32)
            s2 = loc2[tok, top2].astype(jnp.int32)
            v1 = m1[tok, top1] > 0
            v2 = m2[tok, top2] > 0
            s1 = jnp.where(v1, s1, C)
            s2 = jnp.where(v2, s2, C)
            buf = jnp.zeros((N_EXPERTS, C, D), x.dtype)
            buf = buf.at[top1, s1].set(x, mode='drop')
            buf = buf.at[top2, s2].set(x, mode='drop')
            h = jax.nn.relu(jnp.einsum('ecd,edf->ecf', buf, w1) + b1[:, None, :])
            y = (jnp.einsum('ecf,efd->ecd', h, w2) + b2[:, None, :]) * (1.0 - MOE_TOKEN_DROPOUT)
            y1 = y[top1, jnp.minimum(s1, C - 1)]
            y2 = y[top2, jnp.minimum(s2, C - 1)]
            g1 = t1 * v1
            g2 = t2 * v2
            return g1[:, None] * y1 + g2[:, None] * y2
        key = jax.random.key(seed)
        ks = jax.random.split(key, 20)

        def w(k, shape, scale=0.02):
            return jax.random.normal(k, shape, jnp.float32) * scale
        return {'x': jax.random.normal(ks[0], (B, S, D_MODEL), jnp.float32), 'wq': w(ks[1], (D_MODEL, D_MODEL)), 'bq': w(ks[2], (D_MODEL,)), 'wk': w(ks[3], (D_MODEL, D_MODEL)), 'bk': w(ks[4], (D_MODEL,)), 'wv': w(ks[5], (D_MODEL, D_MODEL)), 'bv': w(ks[6], (D_MODEL,)), 'wo': w(ks[7], (D_MODEL, D_MODEL)), 'bo': w(ks[8], (D_MODEL,)), 'ln1_g': 1.0 + w(ks[9], (D_MODEL,)), 'ln1_b': w(ks[10], (D_MODEL,)), 'ln2_g': 1.0 + w(ks[11], (D_MODEL,)), 'ln2_b': w(ks[12], (D_MODEL,)), 'wr': w(ks[13], (D_MODEL, N_EXPERTS)), 'w1': w(ks[14], (N_EXPERTS, D_MODEL, FFN_DIM)), 'b1': w(ks[15], (N_EXPERTS, FFN_DIM)), 'w2': w(ks[16], (N_EXPERTS, FFN_DIM, D_MODEL)), 'b2': w(ks[17], (N_EXPERTS, D_MODEL))}
    _L1_ffn_all = _L1_ffn_setup()
    _L1_ffn_in = {k: v for k, v in _L1_ffn_all.items() if k in ('wq', 'bq', 'wk', 'bk', 'wv', 'bv', 'wo', 'bo', 'ln1_g', 'ln1_b', 'ln2_g', 'ln2_b', 'wr', 'w1', 'b1', 'w2', 'b2')}
    del _L1_ffn_all
    return {'x': x, 'ctx_1024': ctx_1024, 'L0_xattn_Wk': _L0_xattn_in['Wk'], 'L0_xattn_Wv': _L0_xattn_in['Wv'], 'L0_xattn_bv': _L0_xattn_in['bv'], 'L0_xattn_Wq': _L0_xattn_in['Wq'], 'L0_xattn_bq': _L0_xattn_in['bq'], 'L0_xattn_Wo': _L0_xattn_in['Wo'], 'L0_xattn_bo': _L0_xattn_in['bo'], 'L0_ffn_ln_g': _L0_ffn_in['ln_g'], 'L0_ffn_ln_b': _L0_ffn_in['ln_b'], 'L0_ffn_wq': _L0_ffn_in['wq'], 'L0_ffn_wk': _L0_ffn_in['wk'], 'L0_ffn_wv': _L0_ffn_in['wv'], 'L0_ffn_wo': _L0_ffn_in['wo'], 'L0_ffn_gate_w': _L0_ffn_in['gate_w'], 'L0_ffn_w1': _L0_ffn_in['w1'], 'L0_ffn_b1': _L0_ffn_in['b1'], 'L0_ffn_w2': _L0_ffn_in['w2'], 'L0_ffn_b2': _L0_ffn_in['b2'], 'L1_xattn_Wq': _L1_xattn_in['Wq'], 'L1_xattn_bq': _L1_xattn_in['bq'], 'L1_xattn_Wk': _L1_xattn_in['Wk'], 'L1_xattn_bk': _L1_xattn_in['bk'], 'L1_xattn_Wv': _L1_xattn_in['Wv'], 'L1_xattn_bv': _L1_xattn_in['bv'], 'L1_ffn_wq': _L1_ffn_in['wq'], 'L1_ffn_bq': _L1_ffn_in['bq'], 'L1_ffn_wk': _L1_ffn_in['wk'], 'L1_ffn_bk': _L1_ffn_in['bk'], 'L1_ffn_wv': _L1_ffn_in['wv'], 'L1_ffn_bv': _L1_ffn_in['bv'], 'L1_ffn_wo': _L1_ffn_in['wo'], 'L1_ffn_bo': _L1_ffn_in['bo'], 'L1_ffn_ln1_g': _L1_ffn_in['ln1_g'], 'L1_ffn_ln1_b': _L1_ffn_in['ln1_b'], 'L1_ffn_ln2_g': _L1_ffn_in['ln2_g'], 'L1_ffn_ln2_b': _L1_ffn_in['ln2_b'], 'L1_ffn_wr': _L1_ffn_in['wr'], 'L1_ffn_w1': _L1_ffn_in['w1'], 'L1_ffn_b1': _L1_ffn_in['b1'], 'L1_ffn_w2': _L1_ffn_in['w2'], 'L1_ffn_b2': _L1_ffn_in['b2']}

def reference(x, ctx_1024, L0_xattn_Wk, L0_xattn_Wv, L0_xattn_bv, L0_xattn_Wq, L0_xattn_bq, L0_xattn_Wo, L0_xattn_bo, L0_ffn_ln_g, L0_ffn_ln_b, L0_ffn_wq, L0_ffn_wk, L0_ffn_wv, L0_ffn_wo, L0_ffn_gate_w, L0_ffn_w1, L0_ffn_b1, L0_ffn_w2, L0_ffn_b2, L1_xattn_Wq, L1_xattn_bq, L1_xattn_Wk, L1_xattn_bk, L1_xattn_Wv, L1_xattn_bv, L1_ffn_wq, L1_ffn_bq, L1_ffn_wk, L1_ffn_bk, L1_ffn_wv, L1_ffn_bv, L1_ffn_wo, L1_ffn_bo, L1_ffn_ln1_g, L1_ffn_ln1_b, L1_ffn_ln2_g, L1_ffn_ln2_b, L1_ffn_wr, L1_ffn_w1, L1_ffn_b1, L1_ffn_w2, L1_ffn_b2):
    import jax
    import jax.numpy as jnp

    def _L0_xattn_ref(k, v, q, Wk, Wv, bv, Wq, bq, Wo, bo):
        import jax, jax.numpy as jnp
        import numpy as np
        D_MODEL = 256
        B, S = (4, 512)
        kp = jnp.einsum('bsd,ed->bse', k, Wk)
        vp = jnp.einsum('bsd,ed->bse', v, Wv) + bv
        qp = jnp.einsum('bsd,ed->bse', q, Wq) + bq
        scale = 1.0 / jnp.sqrt(jnp.float32(kp.shape[-1]))
        scores = jnp.einsum('bqd,bkd->bqk', qp, kp) * scale
        probs = jax.nn.softmax(scores, axis=-1)
        ctx = jnp.einsum('bqk,bkd->bqd', probs, vp)
        return jnp.einsum('bqd,ed->bqe', ctx, Wo) + bo

    def _L0_ffn_ref(x, ln_g, ln_b, wq, wk, wv, wo, gate_w, w1, b1, w2, b2):
        import jax, jax.numpy as jnp
        import numpy as np
        H = 32
        MB = 2
        TOP_K = 2
        B, S, D = x.shape
        E = w1.shape[0]
        hd = D // H
        mu = jnp.mean(x, axis=-1, keepdims=True)
        var = jnp.var(x, axis=-1, keepdims=True)
        xn = (x - mu) / jnp.sqrt(var + 1e-05) * ln_g + ln_b
        q = (xn @ wq).reshape(B, S, H, hd)
        k = (xn @ wk).reshape(B, S, H, hd)
        v = (xn @ wv).reshape(B, S, H, hd)
        att = jnp.einsum('bqhd,bkhd->bhqk', q, k) / np.float32(np.sqrt(hd))
        p = jax.nn.softmax(att, axis=-1)
        o = jnp.einsum('bhqk,bkhd->bqhd', p, v).reshape(B, S, D) @ wo + x
        xf = o.reshape(-1, D)
        logits = xf @ gate_w.T
        _ = jax.lax.top_k(logits, TOP_K)
        tpe = xf.shape[0] // (MB * E)
        xe = xf.reshape(MB, E, tpe, D)
        h = jax.nn.gelu(jnp.einsum('metd,edf->metf', xe, w1) + b1[None, :, None, :], approximate=False)
        y = jnp.einsum('metf,efd->metd', h, w2) + b2[None, :, None, :]
        return y.reshape(B, S, D)

    def _L1_xattn_ref(hidden_states, external_embeddings, Wq, bq, Wk, bk, Wv, bv):
        import jax, jax.numpy as jnp
        import numpy as np
        B, S, E, H = (4, 512, 128, 256)
        q = hidden_states @ Wq + bq
        k_tok = hidden_states @ Wk + bk
        v_tok = hidden_states @ Wv + bv
        k_ext = external_embeddings @ Wk + bk
        v_ext = external_embeddings @ Wv + bv
        s_self = jnp.einsum('bsh,bsh->bs', q, k_tok)[..., None]
        s_ext = jnp.einsum('bsh,beh->bse', q, k_ext)
        scores = jnp.concatenate([s_self, s_ext], axis=-1)
        probs = jax.nn.softmax(scores, axis=-1)
        ctx = probs[..., :1] * v_tok + jnp.einsum('bse,beh->bsh', probs[..., 1:], v_ext)
        return ctx

    def _L1_ffn_ref(x, wq, bq, wk, bk, wv, bv, wo, bo, ln1_g, ln1_b, ln2_g, ln2_b, wr, w1, b1, w2, b2):
        import jax, jax.numpy as jnp
        import numpy as np
        D_MODEL = 256
        N_HEADS = 16
        HEAD_DIM = D_MODEL // N_HEADS
        FFN_DIM = 1024
        N_EXPERTS = 8
        CAP_FRAC = 0.25
        MOE_TOKEN_DROPOUT = 0.2
        LN_EPS = 1e-05
        B, S = (4, 128)

        def _layer_norm(x, g, b):
            mu = x.mean(-1, keepdims=True)
            var = ((x - mu) ** 2).mean(-1, keepdims=True)
            return (x - mu) * jax.lax.rsqrt(var + LN_EPS) * g + b

        def _self_attention(x, wq, bq, wk, bk, wv, bv, wo, bo):
            b, s, d = x.shape
            q = ((x @ wq + bq) * HEAD_DIM ** (-0.5)).reshape(b, s, N_HEADS, HEAD_DIM)
            k = (x @ wk + bk).reshape(b, s, N_HEADS, HEAD_DIM)
            v = (x @ wv + bv).reshape(b, s, N_HEADS, HEAD_DIM)
            scores = jnp.einsum('bqhd,bkhd->bhqk', q, k)
            p = jax.nn.softmax(scores, axis=-1)
            o = jnp.einsum('bhqk,bkhd->bqhd', p, v).reshape(b, s, d)
            return o @ wo + bo

        def _moe_ffn(x, wr, w1, b1, w2, b2):
            T, D = x.shape
            C = int(np.ceil(CAP_FRAC * T))
            logits = x @ wr
            probs = jax.nn.softmax(logits, axis=-1)
            top1 = jnp.argmax(probs, axis=-1)
            m1 = jax.nn.one_hot(top1, N_EXPERTS, dtype=x.dtype)
            top2 = jnp.argmax(jnp.where(m1 > 0, -jnp.inf, logits), axis=-1)
            m2 = jax.nn.one_hot(top2, N_EXPERTS, dtype=x.dtype)
            loc1 = jnp.cumsum(m1, axis=0) - 1.0
            loc2 = jnp.cumsum(m2, axis=0) - 1.0 + m1.sum(0, keepdims=True)
            m1 = m1 * (loc1 < C)
            m2 = m2 * (loc2 < C)
            t1 = (probs * m1).sum(-1)
            t2 = (probs * m2).sum(-1)
            denom = jnp.maximum(t1 + t2, jnp.finfo(x.dtype).eps)
            t1, t2 = (t1 / denom, t2 / denom)
            tok = jnp.arange(T)
            s1 = loc1[tok, top1].astype(jnp.int32)
            s2 = loc2[tok, top2].astype(jnp.int32)
            v1 = m1[tok, top1] > 0
            v2 = m2[tok, top2] > 0
            s1 = jnp.where(v1, s1, C)
            s2 = jnp.where(v2, s2, C)
            buf = jnp.zeros((N_EXPERTS, C, D), x.dtype)
            buf = buf.at[top1, s1].set(x, mode='drop')
            buf = buf.at[top2, s2].set(x, mode='drop')
            h = jax.nn.relu(jnp.einsum('ecd,edf->ecf', buf, w1) + b1[:, None, :])
            y = (jnp.einsum('ecf,efd->ecd', h, w2) + b2[:, None, :]) * (1.0 - MOE_TOKEN_DROPOUT)
            y1 = y[top1, jnp.minimum(s1, C - 1)]
            y2 = y[top2, jnp.minimum(s2, C - 1)]
            g1 = t1 * v1
            g2 = t2 * v2
            return g1[:, None] * y1 + g2[:, None] * y2
        h = _layer_norm(x, ln1_g, ln1_b)
        h = _self_attention(h, wq, bq, wk, bk, wv, bv, wo, bo)
        x = x + h
        h = _layer_norm(x, ln2_g, ln2_b)
        b, s, d = h.shape
        moe = _moe_ffn(h.reshape(b * s, d), wr, w1, b1, w2, b2).reshape(b, s, d)
        return x + moe
    x = x + _L0_xattn_ref(ctx_1024, ctx_1024, _layernorm(x, axis=-1), L0_xattn_Wk, L0_xattn_Wv, L0_xattn_bv, L0_xattn_Wq, L0_xattn_bq, L0_xattn_Wo, L0_xattn_bo)
    x = x + _L0_ffn_ref(_layernorm(x, axis=-1), L0_ffn_ln_g, L0_ffn_ln_b, L0_ffn_wq, L0_ffn_wk, L0_ffn_wv, L0_ffn_wo, L0_ffn_gate_w, L0_ffn_w1, L0_ffn_b1, L0_ffn_w2, L0_ffn_b2)
    x = x + _L1_xattn_ref(_layernorm(x, axis=-1), ctx_1024, L1_xattn_Wq, L1_xattn_bq, L1_xattn_Wk, L1_xattn_bk, L1_xattn_Wv, L1_xattn_bv)
    x = x + _L1_ffn_ref(_layernorm(x, axis=-1), L1_ffn_wq, L1_ffn_bq, L1_ffn_wk, L1_ffn_bk, L1_ffn_wv, L1_ffn_bv, L1_ffn_wo, L1_ffn_bo, L1_ffn_ln1_g, L1_ffn_ln1_b, L1_ffn_ln2_g, L1_ffn_ln2_b, L1_ffn_wr, L1_ffn_w1, L1_ffn_b1, L1_ffn_w2, L1_ffn_b2)
    return x

_drawn_inputs = setup_inputs


def setup_inputs(seed=0):
    import zlib

    import numpy as np

    out = dict(_drawn_inputs(seed))
    spreads = {'L0_xattn_bv': (0.0, 0.1),
     'L0_xattn_bq': (0.0, 0.1),
     'L0_xattn_bo': (0.0, 0.1),
     'L0_ffn_ln_g': (1.0, 0.2),
     'L0_ffn_ln_b': (0.0, 0.1),
     'L0_ffn_b1': (0.0, 0.1),
     'L0_ffn_b2': (0.0, 0.1)}
    factors = {'L1_xattn_bk': 64.0,
     'L1_xattn_bv': 4.779,
     'L1_ffn_wq': 8.0,
     'L1_ffn_bq': 8.0,
     'L1_ffn_wk': 8.0,
     'L1_ffn_bk': 64.0,
     'L1_ffn_wv': 2.744,
     'L1_ffn_bv': 8.0,
     'L1_ffn_bo': 6.249,
     'L1_ffn_ln1_g': 8.0,
     'L1_ffn_ln1_b': 8.0,
     'L1_ffn_ln2_g': 8.0,
     'L1_ffn_ln2_b': 22.791,
     'L1_ffn_b1': 33.083,
     'L1_ffn_b2': 8.0}
    for name, (base, spread) in spreads.items():
        noise = np.random.default_rng([zlib.crc32(name.encode()), seed]).standard_normal(out[name].shape)
        drawn = base * np.exp(spread * noise) if base else spread * noise
        out[name] = jnp.asarray(drawn.astype(out[name].dtype))
    for name, factor in factors.items():
        out[name] = (out[name] * factor).astype(out[name].dtype)
    return out
```

```python
from contextlib import ExitStack

import concourse.bass as bass
from concourse import mybir

F32 = mybir.dt.float32
F32R = mybir.dt.float32r
I32 = mybir.dt.int32
ALU = mybir.AluOpType
ACT = mybir.ActivationFunctionType
AX = mybir.AxisListType.X

P = 128
EPS = 1e-5
SLOT = 32
PARTS = 3
MROW = PARTS * SLOT
C_MASK = {8: 0, 16: 4}
C_SEL, C_HALF, C_EPS, C_FIRST, C_BASE, C_TRI, C_IDENT, C_ALL = 8, 12, 16, 20, 28, 36, 164, 292


def now(eng, value):
    eng.compute_val(value)
    return value


def wait_first(eng, static, sem, value):
    value = now(eng, value)
    eng.wait_ge(*static)
    eng.wait_ge(sem, value)


class Events:

    def __init__(self, sem, names):
        self.sem, self.names, self.done = sem, names.split(), []

    def start(self, eng):
        eng.sem_inc(self.sem, 1)

    def before(self, rnd):
        return rnd * len(self.names) + 1

    def at(self, rnd, name):
        return rnd * len(self.names) + self.names.index(name) + 2

    def tick(self, name):
        assert self.names[len(self.done) % len(self.names)] == name, (self.names, self.done, name)
        self.done.append(name)
        return self.sem, 1


class Heads:

    def __init__(self, name, width, D, sem):
        self.width = width
        self.nh = SLOT // width
        self.slots = D // SLOT
        self.pairs = self.nh // 2
        self.units = 2 * self.pairs
        self.heads = D // width
        self.groups = self.heads // 4
        self.scale = float(width) ** -0.5
        self.scored = sem(f"{name}_scored")
        self.maxed = sem(f"{name}_maxed")
        self.negated = sem(f"{name}_negated")
        self.parted = sem(f"{name}_parted")
        self.turned = sem(f"{name}_turned")
        self.rows = sem(f"{name}_rows")
        self.st = sem(f"{name}_st")
        self.exp = sem(f"{name}_exp")
        self.pv = sem(f"{name}_pv")
        self.os = sem(f"{name}_os")


def layers(nc, a, scratch, sem, ident, ones, cst, logits, bank):
    B, S, D = a["x"].shape
    NE, _, FD = a["L0_ffn_w1"].shape
    DC, FC = D // P, FD // P
    assert S == 2 * P and DC == 2 and FC == 8 and B % NE == 0

    x_d = a["x"].rearrange("b (t p) d -> b p t d", p=P)
    ctx_d = a["ctx_1024"].rearrange("b (t p) d -> b p t d", p=P)
    res_d = scratch["residual"].rearrange("(b t p) d -> b p t d", p=P, t=2)
    tok_d = scratch["tokens"].rearrange("(b t p) d -> b p t d", p=P, t=2)
    w1_d = a["L0_ffn_w1"].rearrange("e (c p) f -> e p c f", p=P)
    w2_d = a["L0_ffn_w2"].rearrange("e (f p) d -> e p f d", p=P)

    with ExitStack() as stack:
        def sb(name, shape, dt=F32):
            return stack.enter_context(nc.sbuf_tensor(name, shape, dt))

        def tile(name, dt=F32):
            return sb(name, [P, 2, D], dt)

        raw = {n: tile(f"raw_{n}") for n in ("WqA", "WkA", "WvA", "WoA", "WqC", "WkC")}
        MA, WA, MC, WvC = tile("MA"), tile("WA"), tile("MC"), tile("WvC")
        wB = {n: tile(f"wB_{n}") for n in ("wq", "wk", "wv", "wo")}
        wD = {n: tile(f"wD_{n}") for n in ("wq", "wk", "wv", "wo")}
        wr = sb("wr", [P, DC, NE])
        vecs = sb("vecs", [32, P])
        cols = sb("cols", [P, 32])
        b1rows, b1T = sb("b1rows", [P, P]), sb("b1T", [P, B, FC])
        rowA, rowbvC, rowu, rowbvD, rowboD, rowg2, rowb2 = (
            sb(n, [P, 1, D]) for n in ("rowA", "rowbvC", "rowu", "rowbvD", "rowboD", "rowg2", "rowb2"))
        qkbias = sb("qkbias", [P, 4])
        bqbk = sb("bqbk", [P, 1])
        X0, CX, XB, X1, X2, X3, XP, N, Y, YB = (tile(n) for n in ("X0", "CX", "XB", "X1", "X2", "X3", "XP", "N", "Y", "YB"))
        nT, cxT, qT, PR, pT, cT = (tile(n) for n in ("nT", "cxT", "qT", "PR", "pT", "cT"))
        AO, AOT, XF, XFT = (tile(n) for n in ("AO", "AOT", "XF", "XFT"))
        zT, prT, H2, H2T, RES = pT, AOT, Y, XFT, XF
        diag = sb("diag", [P, 2, P])
        bn, mv = sb("bn", [P, 2, 6]), sb("mv", [P, 2, 2])
        uw, rr = sb("uw", [P, 4]), sb("rr", [P, 4])
        st = sb("st", [P, 20])
        W1, W2, B2 = sb("W1", [P, DC, FD]), sb("W2", [P, FC, D]), sb("B2", [P, 1, D])
        HT = sb("HT", [P, FC, 2 * P])
        QH, QL, KH, KL = (tile(n, F32R) for n in ("QH", "QL", "KH", "KL"))
        QS, KS = (sb(n, [P, DC, 4, D], F32R) for n in ("QS", "KS"))
        KM = sb("KM", [P, 32, D], F32R)
        MX, MH, MT = sb("MX", [P, 2, 2, 4]), sb("MH", [P, 2, 2, 4], F32R), sb("MT", [P, 2, 2, P])
        PT = sb("PT", [P, 8, 2, D])
        VA = {8: sb("VA0", [P, 2, 32, SLOT]), 16: sb("VA1", [P, 2, 16, SLOT])}
        OS = sb("OS", [P, 8, D])
        rh = sb("rh", [P, 4, 4])
        QSs = QS[:, :, :, :].rearrange("p c g t -> p (c g) t")
        KSs = KS[:, :, :, :].rearrange("p c g t -> p (c g) t")

        def halves(b):
            return bank[b][:, :].rearrange("p (c t) -> p c t", c=2)

        def row(t):
            return t[:, :, :].broadcast_to([P, 2, D])

        COLS = ["L0_xattn_bv", "L0_xattn_bq", "L0_ffn_ln_g", "L0_ffn_ln_b", "L1_xattn_bq", "L1_xattn_bk",
                "L1_ffn_bq", "L1_ffn_bk", "L1_ffn_ln1_g", "L1_ffn_ln1_b"]

        def col(name, c):
            i = 2 * COLS.index(name) + c
            return cols[:, i:i + 1]

        s_load, s_zero, s_cst, s_setpe, s_set = (sem(n) for n in ("s_load", "s_zero", "s_cst", "s_setpe", "s_set"))
        s_x, s_cx, s_w, s_store = (sem(n) for n in ("s_x", "s_cx", "s_w", "s_store"))
        s_stack = {(s, w): sem(f"s_stack_{w}{s}") for s in "BD" for w in "kq"}
        STACKED = 16 * PARTS * 4
        h0, h1 = Heads("h0", 8, D, sem), Heads("h1", 16, D, sem)
        attn_out = "os0 os1 os2 os3"
        pe = {"A": Events(sem("pe_A"), "nT cxT qT s pT cT o"),
              "B": Events(sem("pe_B"), "nT q k v os0 os1 os2 os3 aoT wo xfT f0 f1 f2 f3 y"),
              "C": Events(sem("pe_C"), "nT qT self s pT cT o"),
              "D": Events(sem("pe_D"), "nT q k v os0 os1 aoT wo h2T lg")}
        dve = {"A": Events(sem("dve_A"), "bn mv uw n cxT max nb pT rs x"),
               "B": Events(sem("dve_B"), "bn mv uw y n ql kl v rh0 os0 rh1 os1 rh2 os2 rh3 os3 aoT xf xfT x"),
               "C": Events(sem("dve_C"), "bn mv uw n c0 c max mxs mxc nb z rs diag pT x"),
               "D": Events(sem("dve_D"), "bn mv uw y n ql kl v rh0 os0 rh1 os1 aoT xp bn2 mv2 uw2 n2 h2T lg")}
        pool = {"A": Events(sem("pool_A"), "r xb"),
                "B": Events(sem("pool_B"), "r mask xb"),
                "C": Events(sem("pool_C"), "r xb prT"),
                "D": Events(sem("pool_D"), "r yb mask r2 res g h2")}
        act = {"A": Events(sem("act_A"), "nT qT exp cT"),
               "B": Events(sem("act_B"), "zT qh kh f0 f1 f2 f3"),
               "C": Events(sem("act_C"), "nT qT exp pn cT"),
               "D": Events(sem("act_D"), "zT qh kh")}

        block = stack.enter_context(nc.Block())

        rows = lambda n: a[n].rearrange("(c p) d -> p c d", p=P)
        loads = [(raw[n], rows(f"L0_xattn_{n[:2]}" if n[2] == "A" else f"L1_xattn_{n[:2]}")) for n in raw]
        loads.append((WvC, rows("L1_xattn_Wv")))
        loads += [(w[n], rows(f"{layer}_ffn_{n}")) for w, layer in ((wB, "L0"), (wD, "L1")) for n in w]
        loads = [(t[:, :, :], src) for t, src in loads]
        loads.append((wr[:, :, :], rows("L1_ffn_wr")))
        loads += [(vecs[2 * i:2 * i + 2, :], a[n].rearrange("(c p) -> c p", p=P)) for i, n in enumerate(COLS)]
        loads += [(b1rows[r * NE * FC:(r + 1) * NE * FC, :], a["L0_ffn_b1"].rearrange("e (f p) -> (e f) p", p=P)) for r in range(B // NE)]
        loads += [(t[:, 0, :], a[n].partition_broadcast(P)) for t, n in (
            (rowA, "L0_xattn_bo"), (rowbvC, "L1_xattn_bv"), (rowbvD, "L1_ffn_bv"), (rowboD, "L1_ffn_bo"),
            (rowg2, "L1_ffn_ln2_g"), (rowb2, "L1_ffn_ln2_b"))]
        loads.append((cst[:, :], a["constants"]))
        NLOAD = 16 * len(loads)
        NSET = 12

        @block.sync
        def _(sp):
            for dst, src in loads:
                sp.dma_start(dst, src).then_inc(s_load, 16)
            sp.wait_ge(s_cst, 1)
            slots_d = scratch["slots"].rearrange("(n p r) d -> n p (r d)", p=P, r=8)
            for i in range(slots_d.shape[0]):
                sp.dma_start(slots_d[i], HT[:, :, :].rearrange("p f t -> p (f t)")).then_inc(s_zero, 16)
            sp.wait_ge(s_zero, 16 * slots_d.shape[0])
            sp.sem_inc(s_store, 16)
            with sp.Fori(0, B) as it:
                value = {k: now(sp, v) for k, v in dict(
                    dA=dve["A"].before(it), pA=pool["A"].before(it), pC=pe["C"].before(it), pB=pe["B"].before(it), oB=pool["B"].before(it),
                    qlB=dve["B"].at(it, "ql"), klB=dve["B"].at(it, "kl"), qlD=dve["D"].at(it, "ql"), klD=dve["D"].at(it, "kl"),
                    res=pool["D"].at(it, "res"), h2=pool["D"].at(it, "h2")).items()}
                e = now(sp, it % NE)
                sp.wait_ge(dve["A"].sem, value["dA"])
                sp.wait_ge(pool["A"].sem, value["pA"])
                sp.dma_start(X0[:, :, :], x_d[it]).then_inc(s_x, 16)
                sp.wait_ge(pe["C"].sem, value["pC"])
                sp.dma_start(CX[:, :, :], ctx_d[it]).then_inc(s_cx, 16)
                sp.wait_ge(pe["B"].sem, value["pB"])
                sp.wait_ge(pool["B"].sem, value["oB"])
                sp.dma_start(W1[:, :, :], w1_d[e]).then_inc(s_w, 16)
                sp.dma_start(W2[:, :, :], w2_d[e]).then_inc(s_w, 16)
                sp.dma_start(B2[:, 0, :], a["L0_ffn_b2"][e].partition_broadcast(P)).then_inc(s_w, 16)
                for s, ql, kl in (("B", "qlB", "klB"), ("D", "qlD", "klD")):
                    for w, ready, stack_, parts in (("k", kl, KS, (KH, KH, KL)), ("q", ql, QS, (QH, QL, QH))):
                        sp.wait_ge(dve[s].sem, value[ready])
                        for part, src in enumerate(parts):
                            for g in range(4):
                                sp.dma_start(stack_[part * SLOT:(part + 1) * SLOT, :, g, :].bitcast(F32),
                                             src[g * SLOT:(g + 1) * SLOT, :, :].bitcast(F32)).then_inc(s_stack[s, w], 16)
                sp.wait_ge(pool["D"].sem, value["res"])
                sp.dma_start(res_d[it], RES[:, :, :]).then_inc(s_store, 16)
                sp.wait_ge(pool["D"].sem, value["h2"])
                sp.dma_start(tok_d[it], H2[:, :, :]).then_inc(s_store, 16)
            sp.wait_ge(s_store, 16 + B * 32)

        @block.gpsimd
        def _(g):
            def wait(sem_, value):
                wait_first(g, (s_cst, 1), sem_, value)

            g.memset(HT[:, :, :], 0.0).then_inc(s_cst, 1)
            g.memset(KM[:, :, :].bitcast(F32), 0.0)
            g.memset(MT[:, :, :, :], 0.0)
            for w in VA:
                g.memset(VA[w][:, :, :, :], 0.0)
            g.memset(QS[:, :, :, :].bitcast(F32), 0.0)
            g.memset(ones[:, :], 1.0)
            g.memset(KS[:, :, :, :].bitcast(F32), 0.0).then_inc(s_cst, 1)

            def power(ev, s, name, source, it, n):
                wait(dve[s].sem, dve[s].at(it, source))
                g.tensor_tensor(rr[:, 0:n], uw[:, 0:n], cst[:, C_HALF:C_HALF + n], ALU.pow).then_inc(*ev.tick(name))

            def masks(s, h, it):
                wait(s_stack[s, "k"], it * STACKED + STACKED)
                for slot in range(h.slots):
                    for j in range(h.nh):
                        i = g.tensor_scalar(KM[0:MROW, 4 * slot + j, :], KSs[0:MROW, slot, :].bitcast(F32),
                                            cst[0:MROW, C_MASK[h.width] + j:C_MASK[h.width] + j + 1], None, ALU.mult)
                i.then_inc(*pool[s].tick("mask"))

            g.wait_ge(s_load, NLOAD)
            for events in pool.values():
                events.start(g)
            with g.Fori(0, B) as it:
                power(pool["A"], "A", "r", "uw", it, 4)
                g.tensor_tensor(XB[:, :, :], X0[:, :, :], row(rowA), ALU.add).then_inc(*pool["A"].tick("xb"))
                power(pool["B"], "B", "r", "uw", it, 4)
                masks("B", h0, it)
                wait(s_w, it * 48 + 48)
                g.tensor_tensor(XB[:, :, :], X1[:, :, :], row(B2), ALU.add).then_inc(*pool["B"].tick("xb"))
                power(pool["C"], "C", "r", "uw", it, 4)
                wait(dve["B"].sem, dve["B"].at(it, "x"))
                g.tensor_tensor(XB[:, :, :], X2[:, :, :], row(rowbvC), ALU.add).then_inc(*pool["C"].tick("xb"))
                wait(act["C"].sem, act["C"].at(it, "qT"))
                g.tensor_tensor(prT[:, :, :], qT[:, :, :], nT[:, :, :], ALU.mult).then_inc(*pool["C"].tick("prT"))
                power(pool["D"], "D", "r", "uw", it, 4)
                wait(dve["D"].sem, dve["D"].at(it, "y"))
                g.tensor_tensor(YB[:, :, :], Y[:, :, :], row(rowboD), ALU.add).then_inc(*pool["D"].tick("yb"))
                masks("D", h1, it)
                power(pool["D"], "D", "r2", "uw2", it, 4)
                g.tensor_tensor(RES[:, :, :], X3[:, :, :], XP[:, :, :], ALU.add).then_inc(*pool["D"].tick("res"))
                wait(dve["D"].sem, dve["D"].at(it, "n2"))
                g.tensor_tensor(XB[:, :, :], N[:, :, :], row(rowg2), ALU.mult).then_inc(*pool["D"].tick("g"))
                wait(pool["D"].sem, pool["D"].at(it, "g"))
                g.tensor_tensor(H2[:, :, :], XB[:, :, :], row(rowb2), ALU.add).then_inc(*pool["D"].tick("h2"))

        @block.tensor
        def _(t):
            mm = t.matmul
            t.wait_ge(s_load, NLOAD)
            t.wait_ge(s_cst, 2)

            def turn(b, src):
                for c in range(2):
                    for r in range(2):
                        i = t.transpose(halves(b)[:, c, r * P:(r + 1) * P], src[:, r, c * P:(c + 1) * P], ident)
                return i

            def product(b, lhsT, rhs, m=2, last=True):
                for o in range(m):
                    for c in range(2):
                        i = mm(halves(b)[:, o, :], lhsT[:, c, o * P:(o + 1) * P], rhs[:, c, :], start=c == 0, stop=last and c == 1)
                return i

            t.transpose(bank[0][:, 0:20], vecs[0:20, :], ident[0:20, 0:20])
            t.transpose(bank[1][:, 0:P], b1rows[:, :], ident).then_inc(s_setpe, 1)
            turn(2, raw["WoA"]).then_inc(s_setpe, 1)
            turn(3, raw["WqC"]).then_inc(s_setpe, 1)
            turn(4, raw["WkC"]).then_inc(s_setpe, 1)
            product(5, raw["WqA"], raw["WkA"]).then_inc(s_setpe, 1)
            t.wait_ge(s_set, 4)
            product(6, raw["WvA"], nT).then_inc(s_setpe, 1)
            product(7, qT, cxT).then_inc(s_setpe, 1)
            for o in range(2):
                for c in range(2):
                    mm(bank[0][:, 4 + o:5 + o], raw["WkA"][:, c, o * P:(o + 1) * P], col("L0_xattn_bq", c), start=c == 0, stop=c == 1)
                for c in range(2):
                    i = mm(bank[0][:, 6 + o:7 + o], cxT[:, c, o * P:(o + 1) * P], col("L1_xattn_bq", c), start=c == 0, stop=c == 1)
            i.then_inc(s_setpe, 1)
            for c in range(2):
                i = mm(bank[1][:, 0:1], col("L1_xattn_bq", c).broadcast_to([P, P]), col("L1_xattn_bk", c), start=c == 0, stop=c == 1)
            i.then_inc(s_setpe, 1)
            for c in range(2):
                i = mm(bank[2][:, 0:D], col("L0_xattn_bv", c).broadcast_to([P, P]), nT[:, c, :], start=c == 0, stop=c == 1)
            i.then_inc(s_setpe, 1)
            for c in range(2):
                i = mm(bank[3][:, 0:D], col("L1_xattn_bk", c).broadcast_to([P, P]), qT[:, c, :], start=c == 0, stop=c == 1)
            i.then_inc(s_setpe, 1)
            t.wait_ge(s_set, NSET)

            def heads(s, h, it):
                base = {n: t.snap(it * v) for n, v in dict(scored=h.slots * h.units, head=h.heads, slot=h.slots, group=h.groups).items()}
                V = VA[h.width]
                t.wait_ge(pool[s].sem, pool[s].at(it, "mask"))
                t.wait_ge(s_stack[s, "q"], it * STACKED + STACKED)
                for i in range(h.slots + 3):
                    if i < h.slots:
                        for u in range(h.units):
                            r, pair = divmod(u, h.pairs)
                            n = i * h.units + u
                            if n >= 2:
                                t.wait_ge(h.maxed, base["scored"] + (n - 1))
                            k = 4 * i + 2 * pair
                            mm(halves(n % 2), QSs[0:MROW, i, r * P:(r + 1) * P], KM[0:MROW, k:k + 2, :], start=True, stop=True).then_inc(h.scored, 1)
                    if 1 <= i <= h.slots:
                        t.wait_ge(h.parted, base["slot"] + i)
                        if i >= 2:
                            t.wait_ge(h.rows, base["slot"] + (i - 1))
                        for r in range(2):
                            x = t.transpose(bank[5][:, r * P:(r + 1) * P], MT[:, (i - 1) % 2, r, :], ident)
                        x.then_inc(h.turned, 1)
                    if 2 <= i <= h.slots + 1:
                        slot = i - 2
                        t.wait_ge(h.rows, base["slot"] + (slot + 1))
                        for j in range(h.nh):
                            n = slot * h.nh + j
                            if n >= 2:
                                t.wait_ge(h.exp, base["head"] + (n - 1))
                            for kc in range(2):
                                x = mm(halves(2 + n % 2)[:, kc, :], KM[:, 4 * slot + j, kc * P:(kc + 1) * P], QSs[:, slot, :], start=True, stop=True)
                            x.then_inc(h.st, 1)
                    if i >= 3 and (i - 2) * h.nh % 4 == 0:
                        grp = (i - 2) * h.nh // 4 - 1
                        t.wait_ge(h.exp, base["head"] + 4 * (grp + 1))
                        if grp:
                            t.wait_ge(h.os, base["group"] + grp)
                        for kc in range(2):
                            for j in range(4):
                                x = mm(bank[4][SLOT * j:SLOT * (j + 1), 0:D], V[:, kc, 4 * grp + j, :], PT[:, (4 * grp + j) % 8, kc, :],
                                       start=kc == 0, stop=kc == 1, tile_position=(0, SLOT * j))
                        x.then_inc(h.pv, 1)
                t.wait_ge(h.os, base["group"] + h.groups)
                for q in range(h.groups // 2):
                    half, r = divmod(q, 2)
                    if q >= 2:
                        t.wait_ge(dve[s].sem, dve[s].at(it, f"os{q - 2}"))
                    for k in range(4):
                        x = t.transpose(bank[6 + q % 2][:, k * P:(k + 1) * P], OS[:, 4 * half + k, r * P:(r + 1) * P], ident)
                    x.then_inc(*pe[s].tick(f"os{q}"))
                t.wait_ge(dve[s].sem, dve[s].at(it, f"os{h.groups // 2 - 1}"))
                turn(6, AO).then_inc(*pe[s].tick("aoT"))

            for events in pe.values():
                events.start(t)
            with t.Fori(0, B) as it:
                E = pe["A"]
                t.wait_ge(dve["D"].sem, dve["D"].before(it))
                t.wait_ge(dve["A"].sem, dve["A"].at(it, "n"))
                turn(6, N).then_inc(*E.tick("nT"))
                t.wait_ge(s_cx, it * 16 + 16)
                turn(7, CX).then_inc(*E.tick("cxT"))
                t.wait_ge(act["A"].sem, act["A"].at(it, "nT"))
                product(5, MA, nT).then_inc(*E.tick("qT"))
                t.wait_ge(act["A"].sem, act["A"].at(it, "qT"))
                t.wait_ge(dve["A"].sem, dve["A"].at(it, "cxT"))
                product(6, qT, cxT).then_inc(*E.tick("s"))
                t.wait_ge(act["A"].sem, act["A"].at(it, "exp"))
                turn(7, PR).then_inc(*E.tick("pT"))
                t.wait_ge(dve["A"].sem, dve["A"].at(it, "pT"))
                product(5, CX, pT).then_inc(*E.tick("cT"))
                t.wait_ge(act["A"].sem, act["A"].at(it, "cT"))
                product(6, cT, WA).then_inc(*E.tick("o"))

                E = pe["B"]
                t.wait_ge(dve["B"].sem, dve["B"].at(it, "n"))
                turn(7, N).then_inc(*E.tick("nT"))
                t.wait_ge(act["B"].sem, act["B"].at(it, "zT"))
                product(5, wB["wq"], zT).then_inc(*E.tick("q"))
                product(6, wB["wk"], zT).then_inc(*E.tick("k"))
                product(7, zT, wB["wv"]).then_inc(*E.tick("v"))
                t.wait_ge(dve["B"].sem, dve["B"].at(it, "v"))
                heads("B", h0, it)
                t.wait_ge(dve["B"].sem, dve["B"].at(it, "aoT"))
                product(7, AOT, wB["wo"]).then_inc(*E.tick("wo"))
                t.wait_ge(dve["B"].sem, dve["B"].at(it, "xf"))
                turn(6, XF).then_inc(*E.tick("xfT"))
                t.wait_ge(dve["B"].sem, dve["B"].at(it, "xfT"))
                t.wait_ge(s_w, it * 48 + 48)
                for k in range(4):
                    product(k, W1[:, :, 2 * k * P:], XFT).then_inc(*E.tick(f"f{k}"))
                t.wait_ge(act["B"].sem, act["B"].at(it, "f3"))
                for r in range(2):
                    for f in range(FC):
                        x = mm(halves(6)[:, r, :], HT[:, f, r * P:(r + 1) * P], W2[:, f, :], start=f == 0, stop=f == FC - 1)
                x.then_inc(*E.tick("y"))

                E = pe["C"]
                t.wait_ge(dve["C"].sem, dve["C"].at(it, "n"))
                turn(7, N).then_inc(*E.tick("nT"))
                t.wait_ge(act["C"].sem, act["C"].at(it, "nT"))
                product(6, MC, nT).then_inc(*E.tick("qT"))
                t.wait_ge(pool["C"].sem, pool["C"].at(it, "prT"))
                for r in range(2):
                    for c in range(2):
                        x = mm(bank[5][:, r:r + 1], prT[:, c, r * P:(r + 1) * P], ones[:, 0:1], start=c == 0, stop=c == 1)
                x.then_inc(*E.tick("self"))
                product(7, qT, cxT).then_inc(*E.tick("s"))
                t.wait_ge(act["C"].sem, act["C"].at(it, "exp"))
                turn(6, PR).then_inc(*E.tick("pT"))
                t.wait_ge(dve["C"].sem, dve["C"].at(it, "pT"))
                for o in range(2):
                    for c in range(2):
                        mm(halves(5)[:, o, :], CX[:, c, o * P:(o + 1) * P], pT[:, c, :], start=c == 0, stop=False)
                    for r in range(2):
                        x = mm(halves(5)[:, o, r * P:(r + 1) * P], N[:, r, o * P:(o + 1) * P], diag[:, r, :], start=False, stop=r == 1)
                x.then_inc(*E.tick("cT"))
                t.wait_ge(act["C"].sem, act["C"].at(it, "cT"))
                product(6, cT, WvC).then_inc(*E.tick("o"))

                E = pe["D"]
                t.wait_ge(dve["D"].sem, dve["D"].at(it, "n"))
                turn(7, N).then_inc(*E.tick("nT"))
                t.wait_ge(act["D"].sem, act["D"].at(it, "zT"))
                product(5, wD["wq"], zT).then_inc(*E.tick("q"))
                product(6, wD["wk"], zT).then_inc(*E.tick("k"))
                product(7, zT, wD["wv"]).then_inc(*E.tick("v"))
                t.wait_ge(dve["D"].sem, dve["D"].at(it, "v"))
                heads("D", h1, it)
                t.wait_ge(dve["D"].sem, dve["D"].at(it, "aoT"))
                product(7, AOT, wD["wo"]).then_inc(*E.tick("wo"))
                t.wait_ge(pool["D"].sem, pool["D"].at(it, "h2"))
                turn(6, H2).then_inc(*E.tick("h2T"))
                t.wait_ge(dve["D"].sem, dve["D"].at(it, "h2T"))
                for r in range(2):
                    for c in range(2):
                        x = mm(bank[5][:, r * NE:(r + 1) * NE], H2T[:, c, r * P:(r + 1) * P], wr[:, c, :], start=c == 0, stop=c == 1)
                x.then_inc(*E.tick("lg"))

        @block.vector
        def _(v):
            v.wait_ge(s_load, NLOAD)
            v.wait_ge(s_cst, 2)
            for w in VA:
                v.memset(VA[w][:, :, :, w:w + 1], 1.0)
            for slot in range(8):
                v.tensor_copy(KM[MROW:P, 4 * slot:4 * slot + 4, :], cst[MROW:P, C_SEL:C_SEL + 4].unsqueeze(2).broadcast_to([SLOT, 4, D]))
            v.wait_ge(s_setpe, 1)
            v.tensor_copy(cols[:, 0:20], bank[0][:, 0:20])
            v.tensor_copy(b1T[:, :, :].rearrange("p b f -> p (b f)"), bank[1][:, 0:P]).then_inc(s_set, 1)
            for n, (dst, b) in enumerate(((nT, 2), (qT, 3), (cxT, 4))):
                v.wait_ge(s_setpe, 2 + n)
                v.tensor_copy(dst[:, :, :], halves(b)).then_inc(s_set, 1)
            for n, (dst, b) in enumerate(((MA, 5), (WA, 6), (MC, 7))):
                v.wait_ge(s_setpe, 5 + n)
                v.tensor_copy(dst[:, :, :], halves(b)).then_inc(s_set, 1)
            v.wait_ge(s_setpe, 8)
            v.tensor_copy(qkbias[:, :], bank[0][:, 4:8]).then_inc(s_set, 1)
            v.wait_ge(s_setpe, 9)
            v.tensor_copy(bqbk[:, :], bank[1][:, 0:1]).then_inc(s_set, 1)
            v.wait_ge(s_setpe, 10)
            v.tensor_tensor(rowA[:, 0, :], bank[2][:, 0:D], rowA[:, 0, :], ALU.add).then_inc(s_set, 1)
            v.wait_ge(s_setpe, 11)
            v.tensor_copy(rowu[:, 0, :], bank[3][:, 0:D]).then_inc(s_set, 1)
            v.tensor_scalar(cst[:, C_EPS:C_EPS + 1], cst[:, C_EPS:C_EPS + 1], 1.0, None, ALU.mult).then_inc(s_set, 1)
            v.wait_ge(s_set, NSET)

            def moments(E, X, it, sfx=""):
                for r in range(2):
                    x = v.bn_stats(bn[:, r, :], X[:, r, :])
                x.then_inc(*E.tick("bn" + sfx))
                wait_first(v, (s_cst, 2), E.sem, E.at(it, "bn" + sfx))
                for r in range(2):
                    x = v.bn_aggr(mv[:, r, :], bn[:, r, :])
                x.then_inc(*E.tick("mv" + sfx))
                v.wait_ge(E.sem, E.at(it, "mv" + sfx))
                v.tensor_scalar(uw[:, 0:2], mv[:, :, 1], EPS, None, ALU.add)
                v.tensor_scalar(uw[:, 2:4], mv[:, :, 1], 1.0 + EPS, EPS * EPS, ALU.mult, ALU.add).then_inc(*E.tick("uw" + sfx))

            def norm(dst, X, k):
                for r in range(2):
                    x = v.tensor_scalar(dst[:, r, :], X[:, r, :], mv[:, r, 0:1], rr[:, k + r:k + r + 1], ALU.subtract, ALU.mult)
                return x

            def take(E, s, b, dst, it, name, pe_name):
                v.wait_ge(pe[s].sem, pe[s].at(it, pe_name))
                v.tensor_copy(dst, halves(b)).then_inc(*E.tick(name))

            def rests(E, s, h, it, bias):
                for n, b, head, rest, bn_ in (("q", 5, QH, QL, "L1_ffn_bq"), ("k", 6, KH, KL, "L1_ffn_bk")):
                    v.wait_ge(act[s].sem, act[s].at(it, n + "h"))
                    if bias:
                        for c in range(2):
                            x = v.scalar_tensor_tensor(rest[:, c, :], halves(b)[:, c, :], col(bn_, c), head[:, c, :].bitcast(F32), ALU.add, ALU.subtract)
                    else:
                        x = v.tensor_tensor(rest[:, :, :], halves(b), head[:, :, :].bitcast(F32), ALU.subtract)
                    x.then_inc(*E.tick(n + "l"))
                v.wait_ge(pe[s].sem, pe[s].at(it, "v"))
                for r in range(2):
                    dst = VA[h.width][:, r, :, 0:h.width]
                    src = halves(7)[:, r, :].rearrange("p (h d) -> p h d", d=h.width)
                    if bias:
                        x = v.tensor_tensor(dst, src, rowbvD[:, 0, :].rearrange("p (h d) -> p h d", d=h.width), ALU.add)
                    else:
                        x = v.tensor_copy(dst, src)
                x.then_inc(*E.tick("v"))

            def heads(s, h, it):
                E = dve[s]
                base = {n: v.snap(it * k) for n, k in dict(scored=h.slots * h.units, slot=h.slots).items()}
                for i in range(h.slots + 1):
                    if i < h.slots:
                        for u in range(h.units):
                            r, pair = divmod(u, h.pairs)
                            n = i * h.units + u
                            v.wait_ge(h.scored, base["scored"] + (n + 1))
                            v.tensor_reduce(MX[:, i % 2, r, 2 * pair:2 * pair + 2], halves(n % 2), AX, ALU.max).then_inc(h.maxed, 1)
                        v.wait_ge(h.maxed, base["scored"] + (i + 1) * h.units)
                        v.tensor_scalar(MH[:, i % 2, :, 0:h.nh], MX[:, i % 2, :, 0:h.nh], -1.0, None, ALU.mult).then_inc(h.negated, 1)
                        v.wait_ge(h.negated, base["slot"] + (i + 1))
                        if i >= 2:
                            v.wait_ge(h.turned, base["slot"] + (i - 1))
                        v.tensor_copy(MT[:, i % 2, :, MROW:MROW + h.nh], MH[:, i % 2, :, 0:h.nh].bitcast(F32))
                        v.scalar_tensor_tensor(MT[:, i % 2, :, MROW + 4:MROW + 4 + h.nh], MX[:, i % 2, :, 0:h.nh], -1.0,
                                               MH[:, i % 2, :, 0:h.nh].bitcast(F32), ALU.mult, ALU.subtract).then_inc(h.parted, 1)
                    if i >= 1:
                        v.wait_ge(h.turned, base["slot"] + i)
                        v.tensor_copy(QSs[MROW:P, i - 1, :], bank[5][MROW:P, 0:D]).then_inc(h.rows, 1)
                per = 16 * h.width
                for q in range(h.groups // 2):
                    half, r = divmod(q, 2)
                    ps = bank[6 + q % 2][:, :].rearrange("p (g j d) -> p g j d", g=4, j=4)
                    v.wait_ge(pe[s].sem, pe[s].at(it, f"os{q}"))
                    if q:
                        v.wait_ge(E.sem, E.at(it, f"os{q - 1}"))
                    v.reciprocal(rh[:, :, :], ps[:, :, :, h.width]).then_inc(*E.tick(f"rh{q}"))
                    v.wait_ge(E.sem, E.at(it, f"rh{q}"))
                    v.tensor_tensor(AO[:, r, half * per:(half + 1) * per].rearrange("p (g j d) -> p g j d", g=4, j=4), ps[:, :, :, 0:h.width],
                                    rh[:, :, :].unsqueeze(3).broadcast_to([P, 4, 4, h.width]), ALU.mult).then_inc(*E.tick(f"os{q}"))
                take(E, s, 6, AOT[:, :, :], it, "aoT", "aoT")

            for events in dve.values():
                events.start(v)
            with v.Fori(0, B) as it:
                E = dve["A"]
                v.wait_ge(s_x, it * 16 + 16)
                moments(E, X0, it)
                v.wait_ge(pool["A"].sem, pool["A"].at(it, "r"))
                norm(N, X0, 0).then_inc(*E.tick("n"))
                take(E, "A", 7, cxT[:, :, :], it, "cxT", "cxT")
                v.wait_ge(pe["A"].sem, pe["A"].at(it, "s"))
                v.tensor_reduce(st[:, 0:2], halves(6), AX, ALU.max).then_inc(*E.tick("max"))
                v.wait_ge(E.sem, E.at(it, "max"))
                v.tensor_scalar(st[:, 2:4], st[:, 0:2], -float(D) ** -0.5, None, ALU.mult).then_inc(*E.tick("nb"))
                take(E, "A", 7, pT[:, :, :], it, "pT", "pT")
                v.reciprocal(st[:, 6:8], st[:, 4:6]).then_inc(*E.tick("rs"))
                v.wait_ge(pe["A"].sem, pe["A"].at(it, "o"))
                v.wait_ge(pool["A"].sem, pool["A"].at(it, "xb"))
                v.wait_ge(E.sem, E.at(it, "rs"))
                for r in range(2):
                    x = v.scalar_tensor_tensor(X1[:, r, :], halves(6)[:, r, :], st[:, 6 + r:7 + r], XB[:, r, :], ALU.mult, ALU.add)
                x.then_inc(*E.tick("x"))

                E = dve["B"]
                v.wait_ge(dve["A"].sem, dve["A"].at(it, "x"))
                moments(E, X1, it)
                v.wait_ge(pool["B"].sem, pool["B"].at(it, "r"))
                norm(Y, X1, 0).then_inc(*E.tick("y"))
                norm(N, X1, 2).then_inc(*E.tick("n"))
                rests(E, "B", h0, it, False)
                heads("B", h0, it)
                v.wait_ge(pe["B"].sem, pe["B"].at(it, "wo"))
                v.tensor_tensor(XF[:, :, :], halves(7), Y[:, :, :], ALU.add).then_inc(*E.tick("xf"))
                take(E, "B", 6, XFT[:, :, :], it, "xfT", "xfT")
                v.wait_ge(pe["B"].sem, pe["B"].at(it, "y"))
                v.wait_ge(pool["B"].sem, pool["B"].at(it, "xb"))
                v.tensor_tensor(X2[:, :, :], halves(6), XB[:, :, :], ALU.add).then_inc(*E.tick("x"))

                E = dve["C"]
                v.wait_ge(dve["B"].sem, dve["B"].at(it, "x"))
                moments(E, X2, it)
                v.wait_ge(pool["C"].sem, pool["C"].at(it, "r"))
                norm(N, X2, 0).then_inc(*E.tick("n"))
                v.wait_ge(E.sem, E.at(it, "n"))
                for r in range(2):
                    x = v.tensor_tensor_reduce(out=AO[:, r, :], in0=N[:, r, :], in1=rowu[:, 0, :], scale=1.0, scalar=0.0,
                                               op0=ALU.mult, op1=ALU.add, accum_out=st[:, 10 + r:11 + r])
                x.then_inc(*E.tick("c0"))
                v.wait_ge(E.sem, E.at(it, "c0"))
                v.tensor_scalar(st[:, 10:12], st[:, 10:12], bqbk[:, 0:1], None, ALU.add).then_inc(*E.tick("c"))
                v.wait_ge(pe["C"].sem, pe["C"].at(it, "s"))
                v.tensor_reduce(st[:, 0:2], halves(7), AX, ALU.max).then_inc(*E.tick("max"))
                v.wait_ge(E.sem, E.at(it, "max"))
                v.tensor_tensor(st[:, 12:14], bank[5][:, 0:2], st[:, 0:2], ALU.max).then_inc(*E.tick("mxs"))
                v.wait_ge(E.sem, E.at(it, "mxs"))
                v.tensor_tensor(st[:, 12:14], st[:, 12:14], st[:, 10:12], ALU.add).then_inc(*E.tick("mxc"))
                v.wait_ge(E.sem, E.at(it, "mxc"))
                v.tensor_tensor(st[:, 2:4], st[:, 10:12], st[:, 12:14], ALU.subtract).then_inc(*E.tick("nb"))
                v.wait_ge(act["C"].sem, act["C"].at(it, "pn"))
                v.tensor_tensor(st[:, 14:16], st[:, 4:6], st[:, 8:10], ALU.add).then_inc(*E.tick("z"))
                v.wait_ge(E.sem, E.at(it, "z"))
                v.reciprocal(st[:, 6:8], st[:, 14:16]).then_inc(*E.tick("rs"))
                for r in range(2):
                    x = v.tensor_scalar(diag[:, r, :], ident, st[:, 8 + r:9 + r], None, ALU.mult)
                x.then_inc(*E.tick("diag"))
                take(E, "C", 6, pT[:, :, :], it, "pT", "pT")
                v.wait_ge(pe["C"].sem, pe["C"].at(it, "o"))
                v.wait_ge(pool["C"].sem, pool["C"].at(it, "xb"))
                v.wait_ge(E.sem, E.at(it, "rs"))
                for r in range(2):
                    x = v.scalar_tensor_tensor(X3[:, r, :], halves(6)[:, r, :], st[:, 6 + r:7 + r], XB[:, r, :], ALU.mult, ALU.add)
                x.then_inc(*E.tick("x"))

                E = dve["D"]
                v.wait_ge(dve["C"].sem, dve["C"].at(it, "x"))
                moments(E, X3, it)
                v.wait_ge(pool["D"].sem, pool["D"].at(it, "r"))
                v.wait_ge(s_store, 16 + it * 32)
                norm(Y, X3, 0).then_inc(*E.tick("y"))
                norm(N, X3, 2).then_inc(*E.tick("n"))
                rests(E, "D", h1, it, True)
                heads("D", h1, it)
                v.wait_ge(pe["D"].sem, pe["D"].at(it, "wo"))
                v.wait_ge(pool["D"].sem, pool["D"].at(it, "yb"))
                v.tensor_tensor(XP[:, :, :], halves(7), YB[:, :, :], ALU.add).then_inc(*E.tick("xp"))
                v.wait_ge(E.sem, E.at(it, "xp"))
                moments(E, XP, it, "2")
                v.wait_ge(pool["D"].sem, pool["D"].at(it, "r2"))
                norm(N, XP, 0).then_inc(*E.tick("n2"))
                take(E, "D", 6, H2T[:, :, :], it, "h2T", "h2T")
                v.wait_ge(pe["D"].sem, pe["D"].at(it, "lg"))
                v.tensor_copy(logits[:, bass.ts(it, 2), :], bank[5][:, 0:2 * NE].rearrange("p (t e) -> p t e", t=2)).then_inc(*E.tick("lg"))

        @block.scalar
        def _(s_):
            s_.wait_ge(s_set, NSET)

            def take(E, s, b, dst, it, name):
                s_.wait_ge(pe[s].sem, pe[s].at(it, name))
                s_.activation(dst[:, :, :], halves(b), ACT.Copy).then_inc(*E.tick(name))

            def take_cols(E, s, b, dst, it, name, pe_name, scale=None, bias=None):
                s_.wait_ge(pe[s].sem, pe[s].at(it, pe_name))
                for c in range(2):
                    kw = {} if scale is None else {"scale": col(scale, c)}
                    x = s_.activation(dst[:, c, :], halves(b)[:, c, :], ACT.Identity, bias=bias(c), **kw)
                x.then_inc(*E.tick(name))

            def heads(s, h, it):
                base = {n: s_.snap(it * k) for n, k in dict(head=h.heads, group=h.groups).items()}

                def outputs(grp):
                    s_.wait_ge(h.pv, base["group"] + (grp + 1))
                    s_.activation(OS[:, grp, :], bank[4][:, 0:D], ACT.Copy).then_inc(h.os, 1)

                for n in range(h.heads):
                    s_.wait_ge(h.st, base["head"] + (n + 1))
                    if n >= 8:
                        s_.wait_ge(h.pv, base["group"] + (n // 4 - 1))
                    s_.activation(PT[:, n % 8, :, :], halves(2 + n % 2), ACT.Exp, scale=h.scale).then_inc(h.exp, 1)
                    if n % 4 == 3 and n > 3:
                        outputs(n // 4 - 1)
                outputs(h.groups - 1)

            for events in act.values():
                events.start(s_)
            with s_.Fori(0, B) as it:
                E = act["A"]
                take(E, "A", 6, nT, it, "nT")
                take_cols(E, "A", 5, qT, it, "qT", "qT", bias=lambda c: qkbias[:, c:c + 1])
                s_.wait_ge(dve["A"].sem, dve["A"].at(it, "nb"))
                for r in range(2):
                    x = s_.activation(PR[:, r, :], halves(6)[:, r, :], ACT.Exp, bias=st[:, 2 + r:3 + r], scale=float(D) ** -0.5, accum_out=st[:, 4 + r:5 + r])
                x.then_inc(*E.tick("exp"))
                take(E, "A", 5, cT, it, "cT")

                E = act["B"]
                take_cols(E, "B", 7, zT, it, "zT", "nT", "L0_ffn_ln_g", lambda c: col("L0_ffn_ln_b", c))
                for n, b, dst in (("q", 5, QH), ("k", 6, KH)):
                    s_.wait_ge(pe["B"].sem, pe["B"].at(it, n))
                    s_.activation(dst[:, :, :], halves(b), ACT.Copy).then_inc(*E.tick(n + "h"))
                heads("B", h0, it)
                for k in range(4):
                    wait_first(s_, (s_set, NSET), pe["B"].sem, pe["B"].at(it, f"f{k}"))
                    for f in (2 * k, 2 * k + 1):
                        x = s_.activation(HT[:, f, :], halves(k)[:, f % 2, :], ACT.Gelu, bias=b1T[:, bass.ts(it, 1), f])
                    x.then_inc(*E.tick(f"f{k}"))

                E = act["C"]
                take(E, "C", 7, nT, it, "nT")
                take_cols(E, "C", 6, qT, it, "qT", "qT", bias=lambda c: qkbias[:, 2 + c:3 + c])
                s_.wait_ge(dve["C"].sem, dve["C"].at(it, "nb"))
                for r in range(2):
                    x = s_.activation(PR[:, r, :], halves(7)[:, r, :], ACT.Exp, bias=st[:, 2 + r:3 + r], accum_out=st[:, 4 + r:5 + r])
                x.then_inc(*E.tick("exp"))
                for r in range(2):
                    x = s_.activation(st[:, 8 + r:9 + r], bank[5][:, r:r + 1], ACT.Exp, bias=st[:, 2 + r:3 + r])
                x.then_inc(*E.tick("pn"))
                take(E, "C", 5, cT, it, "cT")

                E = act["D"]
                take_cols(E, "D", 7, zT, it, "zT", "nT", "L1_ffn_ln1_g", lambda c: col("L1_ffn_ln1_b", c))
                take_cols(E, "D", 5, QH, it, "qh", "q", bias=lambda c: col("L1_ffn_bq", c))
                take_cols(E, "D", 6, KH, it, "kh", "k", bias=lambda c: col("L1_ffn_bk", c))
                heads("D", h1, it)


def experts(nc, a, out, scratch, sem, ident, ones, cst, logits, bank):
    B, S, D = a["x"].shape
    T = B * S
    NE, _, FD = a["L1_ffn_w1"].shape
    NT, DC, FC = T // P, D // P, FD // P
    CAP = -(-T // 4)
    GAIN = 1.0 - 0.2
    HALF = 512
    HT4 = HALF // P
    NH = CAP // HALF
    assert NH == 2

    w1_d = a["L1_ffn_w1"].rearrange("e (c p) f -> e p c f", p=P)
    w2_d = a["L1_ffn_w2"].rearrange("e (f p) d -> e p f d", p=P)
    tok_d = scratch["tokens"].rearrange("(n p) d -> n p d", p=P)
    res_d = scratch["residual"].rearrange("(n p) d -> n p d", p=P)
    out_d = out.rearrange("b (t p) d -> (b t) p d", p=P)
    slots_d = scratch["slots"].rearrange("(e h r p) d -> (e h) p r d", h=NH, r=HT4, p=P)
    y_d = scratch["outputs"].rearrange("(e h r p) d -> (e h) p r d", h=NH, r=HT4, p=P)

    with ExitStack() as stack:
        def sb(name, shape, dt=F32):
            return stack.enter_context(nc.sbuf_tensor(name, shape, dt))

        def table(name):
            return sb(name, [P, NT, NE])

        pr, eq, key, m1, m2, l2, cum, tot, run, loc1, loc2, keep = (
            table(n) for n in ("pr", "eq", "key", "m1", "m2", "l2", "cum", "tot", "run", "loc1", "loc2", "keep"))
        mx, zs, kx, t1, t2, den, f1, f2, g1, g2, w = (
            sb(n, [P, NT]) for n in ("mx", "zs", "kx", "t1", "t2", "den", "f1", "f2", "g1", "g2", "wv"))
        put1, put2, get1, get2 = (sb(n, [P, NT], I32) for n in ("put1", "put2", "get1", "get2"))
        tk = sb("tk", [P, 4, D])
        W1 = [sb(f"W1_{i}", [P, DC, FD]) for i in range(2)]
        W2 = [sb(f"W2_{i}", [P, FC, D]) for i in range(2)]
        B2 = [sb(f"B2_{i}", [P, 1, D]) for i in range(2)]
        b1rows, b1T = sb("b1rows2", [NE * FC, P]), sb("b1T2", [P, NE, FC])
        xg = [sb(f"xg{i}", [P, HT4, D]) for i in range(2)]
        xgT = [sb(f"xgT{i}", [P, DC, HALF]) for i in range(2)]
        hT = sb("hT", [P, FC, HALF])
        yo = [sb(f"yo{i}", [P, HT4, D]) for i in range(2)]
        ya, yb, rs, ob = (sb(n, [P, 4, D]) for n in ("ya", "yb", "rs", "ob"))

        s_ld, s_tk = sem("s_ld"), [sem(f"s_tk{i}") for i in range(4)]
        s_d, s_ex, s_cum, s_bt = sem("s_d"), sem("s_ex"), sem("s_cum"), sem("s_bt")
        s_routed, s_sc = sem("s_routed"), [sem(f"s_sc{i}") for i in range(4)]
        s_w = [sem(f"s_w{i}") for i in range(2)]
        s_xg = [sem(f"s_xg{i}") for i in range(2)]
        s_xt, s_xv, s_h, s_hr, s_y, s_yv = (sem(n) for n in ("s_xt", "s_xv", "s_h", "s_hr", "s_y", "s_yv"))
        s_yo = [sem(f"s_yo{i}") for i in range(2)]
        s_ya, s_rs, s_out = ([sem(f"{n}{i}") for i in range(4)] for n in ("s_ya", "s_rs", "s_out"))
        s_a1, s_a2 = sem("s_a1"), sem("s_a2")
        block = stack.enter_context(nc.Block())
        NROUTE = 2

        def load_weights(sp, i, e):
            sp.dma_start(W1[i][:, :, :], w1_d[e]).then_inc(s_w[i], 16)
            sp.dma_start(W2[i][:, :, :], w2_d[e]).then_inc(s_w[i], 16)
            sp.dma_start(B2[i][:, 0, :], a["L1_ffn_b2"][e].partition_broadcast(P)).then_inc(s_w[i], 16)

        @block.sync
        def _(sp):
            sp.dma_start(b1rows[:, :], a["L1_ffn_b1"].rearrange("e (f p) -> (e f) p", p=P)).then_inc(s_ld, 16)
            load_weights(sp, 0, 0)
            load_weights(sp, 1, 1)
            for n in range(NT):
                if n >= 4:
                    sp.wait_ge(s_sc[n % 4], 32 * (n // 4))
                sp.dma_start(tk[:, n % 4, :], tok_d[n]).then_inc(s_tk[n % 4], 16)
            for i in range(4):
                sp.wait_ge(s_sc[i], 32 * (NT // 4))
            for i in range(2):
                sp.sem_inc(s_yo[i], 16)
            with sp.Fori(0, NE // 2) as k:
                half_ = [now(sp, k * 4 + j) for j in range(4)]
                turned = [now(sp, k * 4 + 1 + (0 if j < 2 else j - 1)) for j in range(4)]
                stored = [now(sp, 1 + (k * 4 + (j + 1)) * HT4) for j in range(4)]
                nxt = [now(sp, (k * 2 + 2 + i) % NE) for i in range(2)]
                for j in range(4):
                    sp.wait_ge(s_xt, turned[j])
                    sp.dma_start(xg[j % 2][:, :, :], slots_d[half_[j]]).then_inc(s_xg[j % 2], 16)
                for j in range(4):
                    sp.wait_ge(s_yv, stored[j])
                    sp.dma_start(y_d[half_[j]], yo[j % 2][:, :, :]).then_inc(s_yo[j % 2], 16)
                    if j % 2 == 1:
                        load_weights(sp, j // 2, nxt[j // 2])
            for i in range(2):
                sp.wait_ge(s_yo[i], 16 + 16 * NE)
            for n in range(NT + 2):
                if n < NT:
                    if n >= 4:
                        sp.wait_ge(s_a2, n - 3)
                    sp.dma_start(rs[:, n % 4, :], res_d[n]).then_inc(s_rs[n % 4], 16)
                if n >= 2:
                    sp.wait_ge(s_a2, n - 1)
                    sp.dma_start(out_d[n - 2], ob[:, (n - 2) % 4, :]).then_inc(s_out[(n - 2) % 4], 16)
            for i in range(4):
                sp.wait_ge(s_out[i], 16 * (NT // 4))
            for i in range(2):
                sp.wait_ge(s_w[i], 48 * (NE // 2 + 1))

        @block.gpsimd
        def _(g):
            g.wait_ge(s_routed, 1)
            for n in range(NT):
                g.wait_ge(s_tk[n % 4], 16 * (n // 4 + 1))
                for put in (put1, put2):
                    g.indirect_dma_start(out=scratch["slots"], out_offset=bass.IndirectOffsetOnAxis(ap=put[:, n:n + 1], axis=0),
                                         in_=tk[:, n % 4, :], in_offset=None,
                                         bounds_check=NE * CAP - 1, oob_is_err=False).then_inc(s_sc[n % 4], 16)
            g.wait_ge(s_routed, 2)
            for i in range(2):
                g.wait_ge(s_yo[i], 16 + 16 * NE)
            for n in range(NT):
                if n >= 4:
                    g.wait_ge(s_a2, n - 3)
                for dst, get in ((ya, get1), (yb, get2)):
                    g.indirect_dma_start(out=dst[:, n % 4, :], out_offset=None, in_=scratch["outputs"],
                                         in_offset=bass.IndirectOffsetOnAxis(ap=get[:, n:n + 1], axis=0),
                                         bounds_check=NE * CAP - 1, oob_is_err=False).then_inc(s_ya[n % 4], 16)

        @block.tensor
        def _(t):
            mm = t.matmul
            t.wait_ge(s_ld, 16)
            t.transpose(bank[7][:, 0:NE * FC], b1rows[:, :], ident[0:NE * FC, 0:NE * FC]).then_inc(s_bt, 1)
            flat = lambda x: x[:, :, :].rearrange("p n e -> p (n e)")
            for i, m in enumerate((m1, m2)):
                t.wait_ge(s_ex, 1 + i)
                mm(bank[2 * i][:, 0:NT * NE], cst[:, C_TRI:C_TRI + P], flat(m), start=True, stop=True)
                mm(bank[2 * i + 1][:, 0:NT * NE], ones, flat(m), start=True, stop=True).then_inc(s_cum, 1)
            t.wait_ge(s_routed, 2)

            t.sem_inc(s_xt, 1)
            t.sem_inc(s_y, 1)
            with t.Fori(0, NE // 2) as k:
                for j in range(4):
                    u = k * 4 + j
                    i = j // 2
                    t.wait_ge(s_xg[j % 2], (k * 2 + (j // 2 + 1)) * 16)
                    for c in range(DC):
                        for r in range(HT4):
                            x = t.transpose(bank[c][:, r * P:(r + 1) * P], xg[j % 2][:, r, c * P:(c + 1) * P], ident)
                    x.then_inc(s_xt, 1)
                    t.wait_ge(s_xv, u * DC + DC)
                    t.wait_ge(s_w[i], k * 48 + 48)
                    for f in range(FC):
                        b = 2 + f % 2
                        if f >= 2:
                            t.wait_ge(s_hr, 1 + u * FC + (f - 1))
                        else:
                            t.wait_ge(s_hr, 1 + u * FC)
                        for c in range(DC):
                            x = mm(bank[b][:, :], W1[i][:, c, f * P:(f + 1) * P], xgT[j % 2][:, c, :], start=c == 0, stop=c == DC - 1)
                        x.then_inc(s_h, 1)
                    t.wait_ge(s_hr, 1 + u * FC + FC)
                    for r in range(HT4):
                        if r >= 2:
                            t.wait_ge(s_yv, 1 + u * HT4 + (r - 1))
                        else:
                            t.wait_ge(s_yv, 1 + u * HT4)
                        for f in range(FC):
                            x = mm(bank[4 + r % 2][:, 0:D], hT[:, f, r * P:(r + 1) * P], W2[i][:, f, :], start=f == 0, stop=f == FC - 1)
                        x.then_inc(s_y, 1)

        @block.scalar
        def _(s_):
            s_.wait_ge(s_d, 2)
            s_.activation(pr[:, :, :], pr[:, :, :], ACT.Exp).then_inc(s_a1, 1)
            s_.sem_inc(s_hr, 1)
            with s_.Fori(0, NE // 2) as k:
                for j in range(4):
                    u = k * 4 + j
                    for f in range(FC):
                        if f == 0:
                            s_.wait_ge(s_y, 1 + u * HT4)
                        e = k * 2 + j // 2
                        wait_first(s_, (s_bt, 1), s_h, u * FC + (f + 1))
                        s_.activation(hT[:, f, :], bank[2 + f % 2][:, :], ACT.Relu, bias=b1T[:, bass.ds(e, 1), f]).then_inc(s_hr, 1)

        @block.vector
        def _(v):
            count = [0]

            def link(ins):
                count[0] += 1
                ins.then_inc(s_d, 1)
                v.wait_ge(s_d, count[0])

            def each(x):
                return x[:, :].unsqueeze(2).broadcast_to([P, NT, NE])

            def const(c):
                return cst[:, c:c + NE].unsqueeze(1).broadcast_to([P, NT, NE])

            A = lambda x: x[:, :, :]
            tt, sc = v.tensor_tensor, v.tensor_scalar
            link(v.tensor_reduce(mx[:, :], A(logits), AX, ALU.max))
            link(tt(A(pr), A(logits), each(mx), ALU.subtract))

            def first_max(src, m, dst):
                link(tt(A(eq), A(src), each(m), ALU.is_equal))
                link(tt(A(key), A(eq), const(C_FIRST), ALU.mult))
                link(v.tensor_reduce(kx[:, :], A(key), AX, ALU.max))
                link(tt(A(dst), A(key), each(kx), ALU.is_equal))

            first_max(logits, mx, m1)
            v.tensor_copy(w[:, 0:1], kx[:, 0:1]).then_inc(s_ex, 1)
            link(v.scalar_tensor_tensor(A(l2), A(m1), -3.0e38, A(logits), ALU.mult, ALU.add))
            link(v.tensor_reduce(mx[:, :], A(l2), AX, ALU.max))
            first_max(l2, mx, m2)
            v.tensor_copy(w[:, 0:1], kx[:, 0:1]).then_inc(s_ex, 1)
            v.wait_ge(s_a1, 1)
            link(v.tensor_reduce(zs[:, :], A(pr), AX, ALU.add))
            link(v.reciprocal(zs[:, :], zs[:, :]))
            link(tt(A(pr), A(pr), each(zs), ALU.mult))

            v.wait_ge(s_bt, 1)
            v.tensor_copy(b1T[:, :, :].rearrange("p e f -> p (e f)"), bank[7][:, 0:NE * FC])

            def places(i, m, loc, first_total):
                v.wait_ge(s_cum, i + 1)
                view = lambda b: bank[b][:, 0:NT * NE].rearrange("p (n e) -> p n e", e=NE)
                link(v.tensor_copy(A(tot), view(2 * i + 1)))
                link(sc(A(loc), view(2 * i), -1.0, None, ALU.add))
                link(v.tensor_copy(A(run), A(tot)))
                src, dst, step = run, cum, 1
                while step < NT:
                    v.tensor_copy(dst[:, 0:step, :], src[:, 0:step, :])
                    link(tt(dst[:, step:NT, :], src[:, step:NT, :], src[:, 0:NT - step, :], ALU.add))
                    src, dst, step = dst, src, 2 * step
                link(tt(loc[:, 1:NT, :], loc[:, 1:NT, :], src[:, 0:NT - 1, :], ALU.add))
                if first_total is not None:
                    link(tt(A(loc), A(loc), first_total[:, :, :].broadcast_to([P, NT, NE]), ALU.add))
                return src

            def use(m, loc, t_, g_, f_, put, get):
                link(v.scalar_tensor_tensor(A(keep), A(loc), float(CAP), A(m), ALU.is_lt, ALU.mult))
                link(v.tensor_reduce(g_[:, :], A(keep), AX, ALU.add))
                link(tt(A(key), A(keep), A(pr), ALU.mult))
                link(v.tensor_reduce(t_[:, :], A(key), AX, ALU.add))
                link(sc(A(key), A(loc), float(CAP - 1), None, ALU.min))
                link(tt(A(key), A(key), const(C_BASE), ALU.add))
                link(tt(A(key), A(key), A(m), ALU.mult))
                link(v.tensor_reduce(f_[:, :], A(key), AX, ALU.add))
                v.tensor_copy(get[:, :], f_[:, :])
                link(sc(w[:, :], g_[:, :], -float(NE * CAP), float(NE * CAP), ALU.mult, ALU.add))
                link(tt(w[:, :], w[:, :], f_[:, :], ALU.add))
                link(v.tensor_copy(put[:, :], w[:, :]))

            src = places(0, m1, loc1, None)
            total1 = sb("total1", [P, 1, NE])
            link(v.tensor_copy(total1[:, :, :], src[:, NT - 1:NT, :]))
            places(1, m2, loc2, total1)
            use(m1, loc1, t1, g1, f1, put1, get1)
            use(m2, loc2, t2, g2, f2, put2, get2)
            v.tensor_copy(w[:, 0:1], kx[:, 0:1]).then_inc(s_routed, 1)
            link(tt(den[:, :], t1[:, :], t2[:, :], ALU.add))
            link(sc(den[:, :], den[:, :], 1.1920929e-07, None, ALU.max))
            link(v.reciprocal(den[:, :], den[:, :]))
            for t_, g_ in ((t1, g1), (t2, g2)):
                link(tt(t_[:, :], t_[:, :], den[:, :], ALU.mult))
                link(v.scalar_tensor_tensor(g_[:, :], t_[:, :], GAIN, g_[:, :], ALU.mult, ALU.mult))
            v.tensor_copy(w[:, 0:1], kx[:, 0:1]).then_inc(s_routed, 1)

            v.sem_inc(s_yv, 1)
            with v.Fori(0, NE // 2) as k:
                for j in range(4):
                    u = k * 4 + j
                    v.wait_ge(s_xt, u + 2)
                    for c in range(DC):
                        v.tensor_copy(xgT[j % 2][:, c, :], bank[c][:, :]).then_inc(s_xv, 1)
                    for r in range(HT4):
                        v.wait_ge(s_y, 1 + u * HT4 + (r + 1))
                        if r == 0:
                            v.wait_ge(s_yo[j % 2], 16 + (k * 2 + j // 2) * 16)
                        v.tensor_tensor(yo[j % 2][:, r, :], bank[4 + r % 2][:, 0:D], B2[j // 2][:, 0, :], ALU.add).then_inc(s_yv, 1)
            for n in range(NT):
                v.wait_ge(s_ya[n % 4], 32 * (n // 4 + 1))
                v.wait_ge(s_rs[n % 4], 16 * (n // 4 + 1))
                v.scalar_tensor_tensor(rs[:, n % 4, :], ya[:, n % 4, :], g1[:, n:n + 1], rs[:, n % 4, :], ALU.mult, ALU.add).then_inc(s_a1, 1)
                v.wait_ge(s_a1, n + 2)
                if n >= 4:
                    v.wait_ge(s_out[n % 4], 16 * (n // 4))
                v.scalar_tensor_tensor(ob[:, n % 4, :], yb[:, n % 4, :], g2[:, n:n + 1], rs[:, n % 4, :], ALU.mult, ALU.add).then_inc(s_a2, 1)


def program(nc, a, out):
    B, S, D = a["x"].shape
    T, NE = B * S, a["L1_ffn_w1"].shape[0]
    CAP = -(-T // 4)
    scratch = {n: nc.dram_tensor(f"{n}_dram", (r, D), F32, kind="Internal").ap()
               for n, r in (("residual", T), ("tokens", T), ("slots", NE * CAP), ("outputs", NE * CAP))}
    with ExitStack() as stack:
        def sem(name):
            return stack.enter_context(nc.semaphore(name))

        cst_t = stack.enter_context(nc.sbuf_tensor("cst", [P, C_ALL], F32))
        ones_t = stack.enter_context(nc.sbuf_tensor("ones", [P, P], F32))
        logits = stack.enter_context(nc.sbuf_tensor("logits", [P, T // P, NE], F32))
        bank = [stack.enter_context(nc.psum_tensor(f"bank{i}", [P, 512], F32)) for i in range(8)]
        ident, ones = cst_t[:, C_IDENT:C_IDENT + P], ones_t[:, :]
        layers(nc, a, scratch, sem, ident, ones_t, cst_t, logits, bank)
        experts(nc, a, out, scratch, sem, ident, ones, cst_t, logits, bank)


_UNUSED = ("L0_ffn_gate_w",)


def constants(NE, CAP):
    import numpy as np

    c = np.zeros((P, C_ALL), np.float32)
    p = np.arange(P)
    for width, at in C_MASK.items():
        for j in range(SLOT // width):
            c[:, at + j] = p % SLOT // width == j
    for j in range(4):
        c[MROW + j, C_SEL + j] = c[MROW + 4 + j, C_SEL + j] = 1.0
    c[:, C_HALF:C_HALF + 4] = -0.5
    c[:, C_FIRST:C_FIRST + NE] = NE - np.arange(NE)
    c[:, C_BASE:C_BASE + NE] = CAP * np.arange(NE)
    c[:, C_TRI:C_TRI + P] = p[:, None] <= p[None, :]
    c[:, C_IDENT:C_IDENT + P] = np.eye(P)
    return c


def kernel(**inputs):
    import numpy as _np
    import concourse.bacc as _bacc
    from concourse import mybir as _mybir
    from concourse.bass_utils import run_bass_kernel_spmd as _run

    nc = _bacc.Bacc("TRN2", target_bir_lowering=False, num_devices=1)
    arrays, args = {}, {}
    named = {n: _np.ascontiguousarray(v) for n, v in inputs.items() if n not in _UNUSED}
    B, S, _ = named["x"].shape
    named["constants"] = constants(named["L1_ffn_w1"].shape[0], -(-B * S // 4))
    for name, v in named.items():
        arrays[f"in_{name}_dram"] = v
        args[name] = nc.dram_tensor(f"in_{name}_dram", v.shape, _mybir.dt.from_np(v.dtype), kind="ExternalInput").ap()
    out = nc.dram_tensor("out_0_dram", named["x"].shape, _mybir.dt.from_np(named["x"].dtype), kind="ExternalOutput").ap()
    program(nc, args, out)
    r = _run(nc, [arrays], core_ids=[0])
    return r.results[0]["out_0_dram"]
```

```python
from contextlib import ExitStack
from itertools import product as product_of

import concourse.bass as bass
from concourse import mybir

F32 = mybir.dt.float32
F32R = mybir.dt.float32r
I32 = mybir.dt.int32
ALU = mybir.AluOpType
ACT = mybir.ActivationFunctionType
AX = mybir.AxisListType.X

P = 128
EPS = 1e-5
SLOT = 32
PARTS = 3
MROW = PARTS * SLOT
C_MASK = {8: 0, 16: 4}
C_SEL, C_HALF, C_EPS, C_FIRST, C_BASE, C_TRI, C_IDENT, C_ALL = 8, 12, 16, 20, 28, 36, 164, 292


def now(eng, value):
    eng.compute_val(value)
    return value


def wait_first(eng, static, sem, value):
    value = now(eng, value)
    eng.wait_ge(*static)
    eng.wait_ge(sem, value)


class Events:

    def __init__(self, sem, names):
        self.sem, self.names, self.done = sem, names.split(), []

    def start(self, eng):
        eng.sem_inc(self.sem, 1)

    def before(self, rnd):
        return rnd * len(self.names) + 1

    def at(self, rnd, name):
        return rnd * len(self.names) + self.names.index(name) + 2

    def tick(self, name):
        assert self.names[len(self.done) % len(self.names)] == name, (self.names, self.done, name)
        self.done.append(name)
        return self.sem, 1


class Heads:

    def __init__(self, name, width, D, sem):
        self.width = width
        self.nh = SLOT // width
        self.slots = D // SLOT
        self.pairs = self.nh // 2
        self.units = 2 * self.pairs
        self.heads = D // width
        self.groups = self.heads // 4
        self.scale = float(width) ** -0.5
        self.scored = sem(f"{name}_scored")
        self.maxed = sem(f"{name}_maxed")
        self.negated = sem(f"{name}_negated")
        self.parted = sem(f"{name}_parted")
        self.turned = sem(f"{name}_turned")
        self.rows = sem(f"{name}_rows")
        self.st = sem(f"{name}_st")
        self.exp = sem(f"{name}_exp")
        self.pv = sem(f"{name}_pv")
        self.os = sem(f"{name}_os")


def chain(*threads):
    for thread in threads:
        yield from thread


def steps(thread, n):
    for _ in range(n):
        next(thread)


def weave(main, side, n_main, n_side, tail):
    done = 0
    for i in range(n_main):
        next(main)
        while done < n_side and done * (n_main - tail) < (i + 1) * n_side:
            next(side)
            done += 1
    steps(side, n_side - done)


def idle(n):
    return iter([0] * n)


LIN1, LIN2, POST, HEADS_B, HEADS_D = 12, 18, 5, 26, 13


def schedule(fori, n, lin1, lin2, post, heads_b, heads_d, masks_b, masks_d):
    def round_(r, b=True, p=True, l=True, d=True, ahead=True, last=False):
        nxt = lin1(r + 1) if ahead else iter(())
        side = post(r - 2, last) if p else iter(())
        steps(side, 3 if p else 0)
        if b:
            masks_b(r)
        side = chain(side, lin2(r - 1, ahead) if l else iter(()), (next(nxt) for _ in range(2 * ahead)))
        weave(heads_b(r) if b else iter(()), side, HEADS_B * b, (POST - 3) * p + LIN2 * l + 2 * ahead, TAIL_B)
        steps(nxt, 2 * ahead)
        if d:
            masks_d(r - 1)
        weave(heads_d(r - 1) if d else iter(()), nxt, HEADS_D * d, (LIN1 - 4) * ahead, TAIL_D)

    round_(-1, b=False, p=False, l=False, d=False)
    round_(0, p=False, l=False, d=False)
    round_(1, p=False)
    with fori(2, n - 1) as r:
        round_(r)
    round_(n - 1, ahead=False)
    round_(n, b=False, ahead=False, last=True)
    round_(n + 1, b=False, l=False, d=False, ahead=False, last=True)


TAIL_B, TAIL_D = 2, 3


def layers(nc, a, scratch, sem, ident, ones, cst, logits, bank):
    B, S, D = a["x"].shape
    NE, _, FD = a["L0_ffn_w1"].shape
    DC, FC = D // P, FD // P
    assert S == 2 * P and DC == 2 and FC == 8 and B % NE == 0

    x_d = a["x"].rearrange("b (t p) d -> b p t d", p=P)
    ctx_d = a["ctx_1024"].rearrange("b (t p) d -> b p t d", p=P)
    res_d = scratch["residual"].rearrange("(b t p) d -> b p t d", p=P, t=2)
    tok_d = scratch["tokens"].rearrange("(b t p) d -> b p t d", p=P, t=2)
    w1_d = a["L0_ffn_w1"].rearrange("e (c p) f -> e p c f", p=P)
    w2_d = a["L0_ffn_w2"].rearrange("e (f p) d -> e p f d", p=P)

    with ExitStack() as stack:
        def sb(name, shape, dt=F32):
            return stack.enter_context(nc.sbuf_tensor(name, shape, dt))

        def tile(name, dt=F32):
            return sb(name, [P, 2, D], dt)

        MA, WA, MC, WvC = tile("MA"), tile("WA"), tile("MC"), tile("WvC")
        wB = {n: tile(f"wB_{n}") for n in ("wq", "wk", "wv", "wo")}
        wD = {n: tile(f"wD_{n}") for n in ("wq", "wk", "wv", "wo")}
        wr = sb("wr", [P, DC, NE])
        cols, b1T = sb("cols", [P, 24]), sb("b1T", [P, B, FC])
        rowA, rowbvC, rowu, rowbvD, rowboD, rowg2, rowb2 = (
            sb(n, [P, 1, D]) for n in ("rowA", "rowbvC", "rowu", "rowbvD", "rowboD", "rowg2", "rowb2"))
        qkbias = sb("qkbias", [P, 4])
        bqbk = sb("bqbk", [P, 1])
        X0, CX, XB, X1, X1c, Yc, X2, X3, XF, N, Y, YB = (
            tile(n) for n in ("X0", "CX", "XB", "X1", "X1c", "Yc", "X2", "X3", "XF", "N", "Y", "YB"))
        nT, cxT, qT, PR, pT, cT, AOT, XFT, H2, RES = (
            tile(n) for n in ("nT", "cxT", "qT", "PR", "pT", "cT", "AOT", "XFT", "H2", "RES"))
        AO = {8: tile("AO0"), 16: tile("AO1")}
        zT, prT, AOTD, H2T, XP, YD = pT, AOT, pT, XFT, XF, X2
        QH, QL, KH, KL = (t[:, :, :].bitcast(F32R) for t in (PR, cT, tile("KH"), AOT))
        diag = sb("diag", [P, 2, P])
        bn, mv = sb("bn", [P, 2, 6]), sb("mv", [P, 2, 2])
        uw, rr = sb("uw", [P, 4]), sb("rr", [P, 4])
        st = sb("st", [P, 20])
        W1, W2, B2 = sb("W1", [P, DC, FD]), sb("W2", [P, FC, D]), sb("B2", [P, 1, D])
        HT = sb("HT", [P, FC, 2 * P])
        KS = HT[:, :, :].rearrange("p (c g) t -> p c g t", c=DC)
        KSs = HT
        QS = {8: sb("QS0", [P, 8, D], F32R), 16: sb("QS1", [P, 8, D], F32R)}
        KM = {8: sb("KM0", [P, 8, 4, D], F32R), 16: sb("KM1", [P, 8, 2, D], F32R)}
        MX, MH, MT = sb("MX", [P, 2, 2, 4]), sb("MH", [P, 2, 2, 4], F32R), sb("MT", [P, 2, 2, P])
        PT = sb("PT", [P, 8, 2, D])
        VA = {w: sb(f"VA{w}", [P, 2, D // w * (w + 1) + SLOT - w - 1]) for w in (8, 16)}
        OS = sb("OS", [P, 8, D])
        rh = sb("rh", [P, 4, 4, 4])
        raw = {n: PT[:, i, :, :] for i, n in enumerate(("WqA", "WkA", "WvA", "WoA", "WqC", "WkC"))}
        vecs, b1rows = OS[0:24, 0, 0:P], OS[:, 1, 0:P]

        def halves(b):
            return bank[b][:, :].rearrange("p (c t) -> p c t", c=2)

        def row(t):
            return t[:, :, :].broadcast_to([P, 2, D])

        COLS = ["L0_xattn_bv", "L0_xattn_bq", "L0_ffn_ln_g", "L0_ffn_ln_b", "L1_xattn_bq", "L1_xattn_bk",
                "L1_ffn_bq", "L1_ffn_bk", "L1_ffn_ln1_g", "L1_ffn_ln1_b",
                "L1_ffn_ln2_g", "L1_ffn_ln2_b"]
        NV = 2 * len(COLS)

        def col(name, c):
            i = 2 * COLS.index(name) + c
            return cols[:, i:i + 1]

        s_load, s_zero, s_cst, s_setpe, s_set = (sem(n) for n in ("s_load", "s_zero", "s_cst", "s_setpe", "s_set"))
        s_x, s_cxA, s_cxC, s_w, s_store = (sem(n) for n in ("s_x", "s_cxA", "s_cxC", "s_w", "s_store"))
        s_stack = {(s, w): sem(f"s_stack_{w}{s}") for s in "BD" for w in "kq"}
        STACKED = 16 * PARTS * 4
        h0, h1 = Heads("h0", 8, D, sem), Heads("h1", 16, D, sem)
        pe = {"A": Events(sem("pe_A"), "nT cxT qT s pT cT o"),
              "B1": Events(sem("pe_B1"), "nT k q v"), "HB": Events(sem("pe_HB"), "os0 os1 os2 os3"),
              "B2": Events(sem("pe_B2"), "aoT wo xfT f0 f1 f2 f3 y"),
              "C": Events(sem("pe_C"), "nT cxT qT self s pT cT o"),
              "D1": Events(sem("pe_D1"), "nT k q v"), "HD": Events(sem("pe_HD"), "os0 os1"),
              "D2": Events(sem("pe_D2"), "aoT wo nT lg")}
        dve = {"A": Events(sem("dve_A"), "bn mv uw n cxT max nb pT rs x"),
               "B1": Events(sem("dve_B1"), "bn mv uw y n kl ql v"), "HB": Events(sem("dve_HB"), "rh0 os0 rh1 os1 rh2 os2 rh3 os3"),
               "B2": Events(sem("dve_B2"), "aoT xf xfT x"),
               "C": Events(sem("dve_C"), "bn mv uw n cxT c0 c max mxs mxc nb z rs diag pT x"),
               "D1": Events(sem("dve_D1"), "bn mv uw y n kl ql v"), "HD": Events(sem("dve_HD"), "rh0 os0 rh1 os1"),
               "D2": Events(sem("dve_D2"), "aoT xp bn mv uw n h2T lg")}
        pool = {"A": Events(sem("pool_A"), "r xb"), "B1": Events(sem("pool_B1"), "r"), "HB": Events(sem("pool_HB"), "x1 y"),
                "B2": Events(sem("pool_B2"), "xb"), "C": Events(sem("pool_C"), "r xb prT"), "D1": Events(sem("pool_D1"), "r yb"),
                "D2": Events(sem("pool_D2"), "r g h2 res")}
        act = {"A": Events(sem("act_A"), "nT qT exp cT"), "B1": Events(sem("act_B1"), "zT kh qh mask0 mask1"),
               "B2": Events(sem("act_B2"), "f0 f1 f2 f3"), "C": Events(sem("act_C"), "nT qT exp pn cT"),
               "D1": Events(sem("act_D1"), "zT kh qh mask0 mask1")}

        def wait(eng, table, part, rnd, name):
            eng.wait_ge(table[part].sem, table[part].at(rnd, name))

        block = stack.enter_context(nc.Block())

        rows = lambda n: a[n].rearrange("(c p) d -> p c d", p=P)
        loads = [(raw[n], rows(f"L0_xattn_{n[:2]}" if n[2] == "A" else f"L1_xattn_{n[:2]}")) for n in raw]
        loads += [(WvC[:, :, :], rows("L1_xattn_Wv"))]
        loads += [(w[n][:, :, :], rows(f"{layer}_ffn_{n}")) for w, layer in ((wB, "L0"), (wD, "L1")) for n in w]
        loads.append((wr[:, :, :], rows("L1_ffn_wr")))
        loads += [(vecs[2 * i:2 * i + 2, :], a[n].rearrange("(c p) -> c p", p=P)) for i, n in enumerate(COLS)]
        loads += [(b1rows[r * NE * FC:(r + 1) * NE * FC, :], a["L0_ffn_b1"].rearrange("e (f p) -> (e f) p", p=P)) for r in range(B // NE)]
        loads += [(t[:, 0, :], a[n].partition_broadcast(P)) for t, n in (
            (rowA, "L0_xattn_bo"), (rowbvC, "L1_xattn_bv"), (rowbvD, "L1_ffn_bv"), (rowboD, "L1_ffn_bo"),
            (rowg2, "L1_ffn_ln2_g"), (rowb2, "L1_ffn_ln2_b"))]
        loads.append((cst[:, :], a["constants"]))
        NLOAD = 16 * len(loads)
        NSET = 11

        @block.sync
        def _(sp):
            def load_x(b):
                sp.dma_start(X0[:, :, :], x_d[b]).then_inc(s_x, 16)

            def load_cx(b, s):
                sp.dma_start(CX[:, :, :], ctx_d[b]).then_inc(s, 16)

            def load_w(b):
                e = now(sp, b % NE)
                sp.dma_start(W1[:, :, :], w1_d[e]).then_inc(s_w, 16)
                sp.dma_start(W2[:, :, :], w2_d[e]).then_inc(s_w, 16)
                sp.dma_start(B2[:, 0, :], a["L0_ffn_b2"][e].partition_broadcast(P)).then_inc(s_w, 16)

            def ready(table, part, rnd, name):
                value = now(sp, table[part].at(rnd, name))
                sp.wait_ge(s_cst, 1)
                sp.wait_ge(table[part].sem, value)

            load_x(0)
            load_cx(0, s_cxA)
            for dst, src in loads:
                sp.dma_start(dst, src).then_inc(s_load, 16)
            load_w(0)
            sp.wait_ge(s_cst, 1)
            slots_d = scratch["slots"].rearrange("(n p r) d -> n p (r d)", p=P, r=8)
            for i in range(slots_d.shape[0]):
                sp.dma_start(slots_d[i], HT[:, :, :].rearrange("p f t -> p (f t)")).then_inc(s_zero, 16)
            sp.wait_ge(s_zero, 16 * slots_d.shape[0])
            sp.sem_inc(s_store, 16)

            def stacks(part, s, width, b):
                for w, name, parts, heads_, rests_ in (("k", "kl", (0, 0, 1), KH, KL), ("q", "ql", (0, 1, 0), QH, QL)):
                    now(sp, b)
                    ready(dve, part, b, name)
                    dst = KS if w == "k" else QS[width][:, :, :].rearrange("p (c g) t -> p c g t", c=DC)
                    for k, rest in enumerate(parts):
                        for g in range(4):
                            src = (rests_ if rest else heads_)[g * SLOT:(g + 1) * SLOT, :, :].bitcast(F32)
                            sp.dma_start(dst[k * SLOT:(k + 1) * SLOT, :, g, :].bitcast(F32), src).then_inc(s_stack[s, w], 16)

            def lin1(b):
                first = isinstance(b, int) and b == 0
                yield from idle(6)
                if not first:
                    ready(pe, "A", b, "cT")
                    load_cx(now(sp, b - 1), s_cxC)
                else:
                    ready(pe, "A", b, "cT")
                    load_cx(1, s_cxA)
                    ready(dve, "A", b, "n")
                    ready(pool, "A", b, "xb")
                    load_x(1)
                yield
                yield from idle(3)
                stacks("B1", "B", 8, b)
                yield
                yield

            def lin2(b, more):
                yield from idle(6)
                if not (isinstance(b, int) and b == B - 1):
                    nb = now(sp, b + 1)
                    ready(pe, "B2", b, "y")
                    ready(pool, "B2", b, "xb")
                    load_w(nb)
                yield
                yield from idle(5)
                ready(pe, "C", b, "cT")
                if more:
                    nb = now(sp, b + 2)
                    load_cx(nb, s_cxA)
                    load_x(nb)
                elif b == B - 2:
                    load_cx(B - 1, s_cxC)
                yield
                yield from idle(3)
                stacks("D1", "D", 16, b)
                yield
                yield

            def post(b, last):
                yield from idle(2)
                ready(pool, "D2", b, "h2")
                sp.dma_start(tok_d[now(sp, b)], H2[:, :, :]).then_inc(s_store, 16)
                ready(pool, "D2", b, "res")
                sp.dma_start(res_d[now(sp, b)], RES[:, :, :]).then_inc(s_store, 16)
                yield
                yield from idle(2)

            schedule(sp.Fori, B, lin1, lin2, post, lambda b: idle(HEADS_B), lambda b: idle(HEADS_D), lambda b: None, lambda b: None)
            sp.wait_ge(s_store, 16 + B * 32)

        @block.gpsimd
        def _(g):
            def ready(sem_, value):
                wait_first(g, (s_cst, 1), sem_, value)

            g.memset(HT[:, :, :], 0.0).then_inc(s_cst, 1)
            g.memset(MT[:, :, :, :], 0.0)
            for w in VA:
                g.memset(VA[w][:, :, :], 0.0)
                g.memset(QS[w][:, :, :].bitcast(F32), 0.0)
                g.memset(KM[w][:, :, :, :].bitcast(F32), 0.0)
            g.memset(ones[:, :], 1.0).then_inc(s_cst, 1)

            def power(part, b):
                ready(dve[part].sem, dve[part].at(b, "uw"))
                g.tensor_tensor(rr[:, :], uw[:, :], cst[:, C_HALF:C_HALF + 4], ALU.pow).then_inc(*pool[part].tick("r"))

            g.wait_ge(s_load, NLOAD)
            g.wait_ge(s_set, NSET)
            for events in pool.values():
                events.start(g)

            def lin1(b):
                power("A", b)
                yield
                ready(dve["A"].sem, dve["A"].at(b, "n"))
                g.tensor_tensor(XB[:, :, :], X0[:, :, :], row(rowA), ALU.add).then_inc(*pool["A"].tick("xb"))
                yield
                yield from idle(5)
                power("B1", b)
                yield
                yield from idle(4)

            def heads_b(b):
                yield from idle(HEADS_B - 1)
                if not (isinstance(b, int) and b == 0):
                    ready(dve["B2"].sem, dve["B2"].at(b - 1, "x"))
                ready(dve["B1"].sem, dve["B1"].at(b, "n"))
                g.tensor_copy(X1c[:, :, :], X1[:, :, :]).then_inc(*pool["HB"].tick("x1"))
                g.tensor_copy(Yc[:, :, :], Y[:, :, :]).then_inc(*pool["HB"].tick("y"))
                yield

            def lin2(b, more):
                yield from idle(3)
                ready(s_w, b * 48 + 48)
                ready(pool["HB"].sem, pool["HB"].at(b, "x1"))
                ready(pool["D2"].sem, pool["D2"].before(b))
                g.tensor_tensor(XB[:, :, :], X1c[:, :, :], row(B2), ALU.add).then_inc(*pool["B2"].tick("xb"))
                yield
                yield from idle(2)
                power("C", b)
                yield
                ready(dve["C"].sem, dve["C"].at(b, "n"))
                g.tensor_tensor(XB[:, :, :], X2[:, :, :], row(rowbvC), ALU.add).then_inc(*pool["C"].tick("xb"))
                yield
                yield
                ready(act["C"].sem, act["C"].at(b, "qT"))
                g.tensor_tensor(prT[:, :, :], qT[:, :, :], nT[:, :, :], ALU.mult).then_inc(*pool["C"].tick("prT"))
                yield
                yield from idle(3)
                power("D1", b)
                yield
                ready(dve["D1"].sem, dve["D1"].at(b, "y"))
                g.tensor_tensor(YB[:, :, :], YD[:, :, :], row(rowboD), ALU.add).then_inc(*pool["D1"].tick("yb"))
                yield
                yield from idle(3)

            def post(b, last):
                yield
                power("D2", b)
                yield
                ready(s_store, 16 + b * 32)
                ready(dve["D2"].sem, dve["D2"].at(b, "n"))
                g.tensor_tensor(XB[:, :, :], N[:, :, :], row(rowg2), ALU.mult).then_inc(*pool["D2"].tick("g"))
                ready(pool["D2"].sem, pool["D2"].at(b, "g"))
                g.tensor_tensor(H2[:, :, :], XB[:, :, :], row(rowb2), ALU.add).then_inc(*pool["D2"].tick("h2"))
                g.tensor_tensor(RES[:, :, :], X3[:, :, :], XP[:, :, :], ALU.add).then_inc(*pool["D2"].tick("res"))
                yield
                yield from idle(2)

            schedule(g.Fori, B, lin1, lin2, post, heads_b, lambda b: idle(HEADS_D), lambda b: None, lambda b: None)

        @block.tensor
        def _(t):
            mm = t.matmul
            t.wait_ge(s_load, NLOAD)
            t.wait_ge(s_cst, 2)

            def turn(b, src):
                for c in range(2):
                    for r in range(2):
                        i = t.transpose(halves(b)[:, c, r * P:(r + 1) * P], src[:, r, c * P:(c + 1) * P], ident)
                return i

            def product(b, lhsT, rhs, m=2, last=True):
                for o in range(m):
                    for c in range(2):
                        i = mm(halves(b)[:, o, :], lhsT[:, c, o * P:(o + 1) * P], rhs[:, c, :], start=c == 0, stop=last and c == 1)
                return i

            t.transpose(bank[0][:, 0:NV], vecs, ident[0:NV, 0:NV])
            t.transpose(bank[1][:, 0:P], b1rows, ident).then_inc(s_setpe, 1)
            turn(2, raw["WoA"]).then_inc(s_setpe, 1)
            turn(3, raw["WqC"]).then_inc(s_setpe, 1)
            turn(4, raw["WkC"]).then_inc(s_setpe, 1)
            product(5, raw["WqA"], raw["WkA"]).then_inc(s_setpe, 1)
            t.wait_ge(s_set, 4)
            product(6, raw["WvA"], nT).then_inc(s_setpe, 1)
            product(7, qT, cxT).then_inc(s_setpe, 1)
            for o in range(2):
                for c in range(2):
                    mm(bank[0][:, NV + o:NV + 1 + o], raw["WkA"][:, c, o * P:(o + 1) * P], col("L0_xattn_bq", c), start=c == 0, stop=c == 1)
                for c in range(2):
                    i = mm(bank[0][:, NV + 2 + o:NV + 3 + o], cxT[:, c, o * P:(o + 1) * P], col("L1_xattn_bq", c), start=c == 0, stop=c == 1)
            i.then_inc(s_setpe, 1)
            for c in range(2):
                i = mm(bank[1][:, 0:1], col("L1_xattn_bq", c).broadcast_to([P, P]), col("L1_xattn_bk", c), start=c == 0, stop=c == 1)
            i.then_inc(s_setpe, 1)
            for c in range(2):
                i = mm(bank[2][:, 0:D], col("L0_xattn_bv", c).broadcast_to([P, P]), nT[:, c, :], start=c == 0, stop=c == 1)
            i.then_inc(s_setpe, 1)
            for c in range(2):
                i = mm(bank[3][:, 0:D], col("L1_xattn_bk", c).broadcast_to([P, P]), qT[:, c, :], start=c == 0, stop=c == 1)
            i.then_inc(s_setpe, 1)
            t.wait_ge(s_set, NSET)
            for events in pe.values():
                events.start(t)

            def heads(part, before, s, h, b):
                V, K, Q, per = VA[h.width], KM[h.width], QS[h.width], h.width + 1
                base = {n: now(t, b * v) for n, v in dict(scored=h.slots * h.units, head=h.heads, slot=h.slots, group=h.groups).items()}
                for i, p in product_of(range(h.slots + 3), range(h.pairs)):
                    if (i, p) == (0, 0):
                        wait(t, act, before, b, "mask0")
                        t.wait_ge(s_stack[s, "q"], b * STACKED + STACKED)
                    if (i, p) == (h.slots // 2, 0):
                        wait(t, act, before, b, "mask1")
                    if i < h.slots:
                        for u in range(2 * p, 2 * p + 2):
                            r, pair = divmod(u, h.pairs)
                            n = i * h.units + u
                            if n >= 2:
                                t.wait_ge(h.maxed, base["scored"] + (n - 1))
                            mm(halves(n % 2), Q[0:MROW, i, r * P:(r + 1) * P], K[0:MROW, i, 2 * pair:2 * pair + 2, :], start=True, stop=True).then_inc(h.scored, 1)
                    if 1 <= i <= h.slots and p == 0:
                        t.wait_ge(h.parted, base["slot"] + i)
                        if i >= 2:
                            t.wait_ge(h.rows, base["slot"] + (i - 1))
                        for r in range(2):
                            x = t.transpose(bank[5][:, r * P:(r + 1) * P], MT[:, (i - 1) % 2, r, :], ident)
                        x.then_inc(h.turned, 1)
                    if 2 <= i <= h.slots + 1:
                        slot = i - 2
                        if p == 0:
                            t.wait_ge(h.rows, base["slot"] + (slot + 1))
                        for j in range(2 * p, 2 * p + 2):
                            n = slot * h.nh + j
                            if n >= 2:
                                t.wait_ge(h.exp, base["head"] + (n - 1))
                            for kc in range(2):
                                x = mm(halves(2 + n % 2)[:, kc, :], K[:, slot, j, kc * P:(kc + 1) * P], Q[:, slot, :], start=True, stop=True)
                            x.then_inc(h.st, 1)
                    if i >= 3 and p == h.pairs - 1 and (i - 2) * h.nh % 4 == 0:
                        grp = (i - 2) * h.nh // 4 - 1
                        t.wait_ge(h.exp, base["head"] + 4 * (grp + 1))
                        if grp:
                            t.wait_ge(h.os, base["group"] + grp)
                        for kc in range(2):
                            for j in range(4):
                                n = 4 * grp + j
                                x = mm(bank[4][SLOT * j:SLOT * (j + 1), 0:D], V[:, kc, n * per:n * per + SLOT], PT[:, n % 8, kc, :],
                                       start=kc == 0, stop=kc == 1, tile_position=(0, SLOT * j))
                        x.then_inc(h.pv, 1)
                    yield
                for q in range(h.groups // 2):
                    half, r = divmod(q, 2)
                    if q == 0:
                        t.wait_ge(h.os, base["group"] + h.groups)
                    if q >= 2:
                        wait(t, dve, part, b, f"os{q - 2}")
                    for k in range(4):
                        x = t.transpose(bank[q % 2][:, k * P:(k + 1) * P], OS[:, 4 * half + k, r * P:(r + 1) * P], ident)
                    x.then_inc(*pe[part].tick(f"os{q}"))
                    if q == h.groups // 2 - 1:
                        wait(t, dve, part, b, f"os{q}")
                    yield

            def lin1(b):
                yield from idle(2)
                if isinstance(b, int) and b < 2:
                    if b:
                        wait(t, dve, "B1", 0, "v")
                else:
                    wait(t, dve, "D1", b - 2, "v")
                E = pe["A"]
                wait(t, dve, "A", b, "n")
                turn(6, N).then_inc(*E.tick("nT"))
                t.wait_ge(s_cxA, b * 16 + 16)
                turn(7, CX).then_inc(*E.tick("cxT"))
                yield
                wait(t, act, "A", b, "nT")
                product(6, MA, nT).then_inc(*E.tick("qT"))
                yield
                wait(t, act, "A", b, "qT")
                wait(t, dve, "A", b, "cxT")
                product(7, qT, cxT).then_inc(*E.tick("s"))
                yield
                wait(t, act, "A", b, "exp")
                turn(6, PR).then_inc(*E.tick("pT"))
                yield
                wait(t, dve, "A", b, "pT")
                product(7, CX, pT).then_inc(*E.tick("cT"))
                yield
                wait(t, act, "A", b, "cT")
                product(6, cT, WA).then_inc(*E.tick("o"))
                yield
                yield
                E = pe["B1"]
                wait(t, dve, "B1", b, "n")
                turn(7, N).then_inc(*E.tick("nT"))
                yield
                wait(t, act, "B1", b, "zT")
                product(7, wB["wk"], zT).then_inc(*E.tick("k"))
                product(6, wB["wq"], zT).then_inc(*E.tick("q"))
                yield
                wait(t, dve, "B1", b, "ql")
                product(6, zT, wB["wv"]).then_inc(*E.tick("v"))
                yield

            def lin2(b, more):
                E = pe["B2"]
                if isinstance(b, int) and b == 0:
                    wait(t, dve, "B1", 1, "v")
                else:
                    wait(t, dve, "D2", b - 1, "lg")
                turn(6, AO[8]).then_inc(*E.tick("aoT"))
                yield
                wait(t, dve, "B2", b, "aoT")
                product(7, AOT, wB["wo"]).then_inc(*E.tick("wo"))
                yield
                wait(t, dve, "B2", b, "xf")
                turn(6, XF).then_inc(*E.tick("xfT"))
                yield
                wait(t, dve, "B2", b, "xfT")
                t.wait_ge(s_w, b * 48 + 48)
                for k in range(4):
                    if k >= 2:
                        wait(t, act, "B2", b, f"f{k - 2}")
                    product(7 - k % 2, W1[:, :, 2 * k * P:], XFT).then_inc(*E.tick(f"f{k}"))
                    if k % 2:
                        yield
                wait(t, act, "B2", b, "f3")
                for r in range(2):
                    for f in range(FC):
                        x = mm(halves(7)[:, r, :], HT[:, f, r * P:(r + 1) * P], W2[:, f, :], start=f == 0, stop=f == FC - 1)
                    if r == 0:
                        yield
                x.then_inc(*E.tick("y"))
                yield
                yield

                E = pe["C"]
                wait(t, dve, "C", b, "n")
                turn(6, N).then_inc(*E.tick("nT"))
                t.wait_ge(s_cxC, b * 16 + 16)
                turn(7, CX).then_inc(*E.tick("cxT"))
                yield
                wait(t, act, "C", b, "nT")
                product(6, MC, nT).then_inc(*E.tick("qT"))
                yield
                wait(t, pool, "C", b, "prT")
                wait(t, dve, "C", b, "cxT")
                for r in range(2):
                    for c in range(2):
                        x = mm(bank[7][:, r:r + 1], prT[:, c, r * P:(r + 1) * P], ones[:, 0:1], start=c == 0, stop=c == 1)
                x.then_inc(*E.tick("self"))
                product(6, qT, cxT).then_inc(*E.tick("s"))
                yield
                wait(t, act, "C", b, "pn")
                turn(7, PR).then_inc(*E.tick("pT"))
                yield
                wait(t, dve, "C", b, "pT")
                for o in range(2):
                    for c in range(2):
                        mm(halves(6)[:, o, :], CX[:, c, o * P:(o + 1) * P], pT[:, c, :], start=c == 0, stop=False)
                    for r in range(2):
                        x = mm(halves(6)[:, o, r * P:(r + 1) * P], N[:, r, o * P:(o + 1) * P], diag[:, r, :], start=False, stop=r == 1)
                x.then_inc(*E.tick("cT"))
                yield
                wait(t, act, "C", b, "cT")
                product(7, cT, WvC).then_inc(*E.tick("o"))
                yield
                yield

                E = pe["D1"]
                wait(t, dve, "D1", b, "n")
                turn(6, N).then_inc(*E.tick("nT"))
                yield
                wait(t, act, "D1", b, "zT")
                product(6, wD["wk"], zT).then_inc(*E.tick("k"))
                product(7, wD["wq"], zT).then_inc(*E.tick("q"))
                yield
                wait(t, dve, "D1", b, "ql")
                product(7, zT, wD["wv"]).then_inc(*E.tick("v"))
                yield

            def post(b, last):
                E = pe["D2"]
                if last:
                    wait(t, dve, "D1", b, "v")
                else:
                    wait(t, dve, "B1", b + 2, "v")
                turn(6, AO[16]).then_inc(*E.tick("aoT"))
                yield
                wait(t, dve, "D2", b, "aoT")
                product(7, AOTD, wD["wo"]).then_inc(*E.tick("wo"))
                yield
                yield
                wait(t, dve, "D2", b, "n")
                turn(6, N).then_inc(*E.tick("nT"))
                yield
                wait(t, dve, "D2", b, "h2T")
                for r in range(2):
                    for c in range(2):
                        x = mm(bank[7][:, r * NE:(r + 1) * NE], H2T[:, c, r * P:(r + 1) * P], wr[:, c, :], start=c == 0, stop=c == 1)
                x.then_inc(*E.tick("lg"))
                yield

            schedule(t.Fori, B, lin1, lin2, post, lambda b: heads("HB", "B1", "B", h0, b), lambda b: heads("HD", "D1", "D", h1, b), lambda b: None, lambda b: None)

        @block.vector
        def _(v):
            v.wait_ge(s_load, NLOAD)
            v.wait_ge(s_cst, 2)
            for w in VA:
                v.memset(VA[w][:, :, 0:D // w * (w + 1)].rearrange("p k (h d) -> p k h d", d=w + 1)[:, :, :, w:w + 1], 1.0)
                nh = SLOT // w
                for slot in range(8):
                    v.tensor_copy(KM[w][MROW:P, slot, :, :], cst[MROW:P, C_SEL:C_SEL + nh].unsqueeze(2).broadcast_to([SLOT, nh, D]))
            v.wait_ge(s_setpe, 1)
            v.tensor_copy(cols[:, :], bank[0][:, 0:NV])
            v.tensor_copy(b1T[:, :, :].rearrange("p b f -> p (b f)"), bank[1][:, 0:P]).then_inc(s_set, 1)
            for n, (dst, b) in enumerate(((nT, 2), (qT, 3), (cxT, 4))):
                v.wait_ge(s_setpe, 2 + n)
                v.tensor_copy(dst[:, :, :], halves(b)).then_inc(s_set, 1)
            for n, (dst, b) in enumerate(((MA, 5), (WA, 6), (MC, 7))):
                v.wait_ge(s_setpe, 5 + n)
                v.tensor_copy(dst[:, :, :], halves(b)).then_inc(s_set, 1)
            v.wait_ge(s_setpe, 8)
            v.tensor_copy(qkbias[:, :], bank[0][:, NV:NV + 4]).then_inc(s_set, 1)
            v.wait_ge(s_setpe, 9)
            v.tensor_copy(bqbk[:, :], bank[1][:, 0:1]).then_inc(s_set, 1)
            v.wait_ge(s_setpe, 10)
            v.tensor_tensor(rowA[:, 0, :], bank[2][:, 0:D], rowA[:, 0, :], ALU.add).then_inc(s_set, 1)
            v.wait_ge(s_setpe, 11)
            v.tensor_copy(rowu[:, 0, :], bank[3][:, 0:D]).then_inc(s_set, 1)
            v.wait_ge(s_set, NSET)
            for events in dve.values():
                events.start(v)

            def moments(part, X, b):
                E = dve[part]
                for r in range(2):
                    x = v.bn_stats(bn[:, r, :], X[:, r, :])
                x.then_inc(*E.tick("bn"))
                wait_first(v, (s_cst, 2), E.sem, E.at(b, "bn"))
                for r in range(2):
                    x = v.bn_aggr(mv[:, r, :], bn[:, r, :])
                x.then_inc(*E.tick("mv"))
                wait(v, dve, part, b, "mv")
                v.tensor_scalar(uw[:, 0:2], mv[:, :, 1], EPS, None, ALU.add)
                v.tensor_scalar(uw[:, 2:4], mv[:, :, 1], 1.0 + EPS, EPS * EPS, ALU.mult, ALU.add).then_inc(*E.tick("uw"))

            def norm(dst, X, k):
                for r in range(2):
                    x = v.tensor_scalar(dst[:, r, :], X[:, r, :], mv[:, r, 0:1], rr[:, k + r:k + r + 1], ALU.subtract, ALU.mult)
                return x

            def take(part, bnk, dst, b, name):
                wait(v, pe, part, b, name)
                v.tensor_copy(dst[:, :, :], halves(bnk)).then_inc(*dve[part].tick(name))

            def rests(part, b, qbank, kbank, bias):
                for n, bnk, head, rest, name in (("k", kbank, KH, KL, "L1_ffn_bk"), ("q", qbank, QH, QL, "L1_ffn_bq")):
                    wait(v, act, part, b, n + "h")
                    if bias:
                        for c in range(2):
                            x = v.scalar_tensor_tensor(rest[:, c, :], halves(bnk)[:, c, :], col(name, c), head[:, c, :].bitcast(F32), ALU.add, ALU.subtract)
                    else:
                        x = v.tensor_tensor(rest, halves(bnk), head.bitcast(F32), ALU.subtract)
                    x.then_inc(*dve[part].tick(n + "l"))

            def values(part, b, w, bnk, bias):
                wait(v, pe, part, b, "v")
                for r in range(2):
                    dst = VA[w][:, r, 0:D // w * (w + 1)].rearrange("p (h d) -> p h d", d=w + 1)[:, :, 0:w]
                    src = halves(bnk)[:, r, :].rearrange("p (h d) -> p h d", d=w)
                    if bias:
                        x = v.tensor_tensor(dst, src, rowbvD[:, 0, :].rearrange("p (h d) -> p h d", d=w), ALU.add)
                    else:
                        x = v.tensor_copy(dst, src)
                x.then_inc(*dve[part].tick("v"))

            def heads(part, h, b):
                E, Q = dve[part], QS[h.width]
                base = {n: now(v, b * k) for n, k in dict(scored=h.slots * h.units, slot=h.slots).items()}
                for i, p in product_of(range(h.slots + 3), range(h.pairs)):
                    if i < h.slots:
                        for u in range(2 * p, 2 * p + 2):
                            r, pair = divmod(u, h.pairs)
                            n = i * h.units + u
                            v.wait_ge(h.scored, base["scored"] + (n + 1))
                            v.tensor_reduce(MX[:, i % 2, r, 2 * pair:2 * pair + 2], halves(n % 2), AX, ALU.max).then_inc(h.maxed, 1)
                    if 1 <= i <= h.slots and p == 0:
                        v.wait_ge(h.turned, base["slot"] + i)
                        v.tensor_copy(Q[MROW:P, i - 1, :], bank[5][MROW:P, 0:D]).then_inc(h.rows, 1)
                    if i < h.slots and p == h.pairs - 1:
                        v.wait_ge(h.maxed, base["scored"] + (i + 1) * h.units)
                        v.tensor_scalar(MH[:, i % 2, :, 0:h.nh], MX[:, i % 2, :, 0:h.nh], -1.0, None, ALU.mult).then_inc(h.negated, 1)
                        v.wait_ge(h.negated, base["slot"] + (i + 1))
                        if i >= 2:
                            v.wait_ge(h.turned, base["slot"] + (i - 1))
                        v.tensor_copy(MT[:, i % 2, :, MROW:MROW + h.nh], MH[:, i % 2, :, 0:h.nh].bitcast(F32))
                        v.scalar_tensor_tensor(MT[:, i % 2, :, MROW + 4:MROW + 4 + h.nh], MX[:, i % 2, :, 0:h.nh], -1.0,
                                               MH[:, i % 2, :, 0:h.nh].bitcast(F32), ALU.mult, ALU.subtract).then_inc(h.parted, 1)
                    yield
                per = 16 * h.width
                for q in range(h.groups // 2):
                    half, r = divmod(q, 2)
                    ps = bank[q % 2][:, :].rearrange("p (g j d) -> p g j d", g=4, j=4)
                    wait(v, pe, part, b, f"os{q}")
                    v.reciprocal(rh[:, q, :, :], ps[:, :, :, h.width]).then_inc(*E.tick(f"rh{q}"))
                    wait(v, dve, part, b, f"rh{q}")
                    v.tensor_tensor(AO[h.width][:, r, half * per:(half + 1) * per].rearrange("p (g j d) -> p g j d", g=4, j=4), ps[:, :, :, 0:h.width],
                                    rh[:, q, :, :].unsqueeze(3).broadcast_to([P, 4, 4, h.width]), ALU.mult).then_inc(*E.tick(f"os{q}"))
                    yield

            def lin1(b):
                E = dve["A"]
                v.wait_ge(s_x, b * 16 + 16)
                moments("A", X0, b)
                yield
                wait(v, pool, "A", b, "r")
                norm(N, X0, 0).then_inc(*E.tick("n"))
                yield
                take("A", 7, cxT, b, "cxT")
                yield
                yield
                wait(v, pe, "A", b, "s")
                v.tensor_reduce(st[:, 0:2], halves(7), AX, ALU.max).then_inc(*E.tick("max"))
                wait(v, dve, "A", b, "max")
                v.tensor_scalar(st[:, 2:4], st[:, 0:2], -float(D) ** -0.5, None, ALU.mult).then_inc(*E.tick("nb"))
                yield
                take("A", 6, pT, b, "pT")
                v.reciprocal(st[:, 6:8], st[:, 4:6]).then_inc(*E.tick("rs"))
                yield
                yield
                v.wait_ge(pool["HB"].sem, pool["HB"].before(b))
                wait(v, pe, "A", b, "o")
                wait(v, pool, "A", b, "xb")
                wait(v, dve, "A", b, "rs")
                for r in range(2):
                    x = v.scalar_tensor_tensor(X1[:, r, :], halves(6)[:, r, :], st[:, 6 + r:7 + r], XB[:, r, :], ALU.mult, ALU.add)
                x.then_inc(*E.tick("x"))
                wait(v, dve, "A", b, "x")
                moments("B1", X1, b)
                yield
                E = dve["B1"]
                wait(v, pool, "B1", b, "r")
                norm(Y, X1, 0).then_inc(*E.tick("y"))
                norm(N, X1, 2).then_inc(*E.tick("n"))
                yield
                yield
                rests("B1", b, 6, 7, False)
                yield
                values("B1", b, 8, 6, False)
                yield

            def lin2(b, more):
                E = dve["B2"]
                take("B2", 6, AOT, b, "aoT")
                yield
                wait(v, pe, "B2", b, "wo")
                wait(v, pool, "HB", b, "y")
                v.wait_ge(pool["D2"].sem, pool["D2"].before(b))
                v.tensor_tensor(XF[:, :, :], halves(7), Yc[:, :, :], ALU.add).then_inc(*E.tick("xf"))
                yield
                take("B2", 6, XFT, b, "xfT")
                yield
                yield from idle(3)
                wait(v, pe, "B2", b, "y")
                wait(v, pool, "B2", b, "xb")
                v.tensor_tensor(X2[:, :, :], halves(7), XB[:, :, :], ALU.add).then_inc(*E.tick("x"))
                wait(v, dve, "B2", b, "x")
                moments("C", X2, b)
                yield

                E = dve["C"]
                wait(v, pool, "C", b, "r")
                norm(N, X2, 0).then_inc(*E.tick("n"))
                yield
                take("C", 7, cxT, b, "cxT")
                yield
                wait(v, dve, "C", b, "n")
                for r in range(2):
                    x = v.tensor_tensor_reduce(out=PR[:, r, :], in0=N[:, r, :], in1=rowu[:, 0, :], scale=1.0, scalar=0.0,
                                               op0=ALU.mult, op1=ALU.add, accum_out=st[:, 10 + r:11 + r])
                x.then_inc(*E.tick("c0"))
                wait(v, dve, "C", b, "c0")
                v.tensor_scalar(st[:, 10:12], st[:, 10:12], bqbk[:, 0:1], None, ALU.add).then_inc(*E.tick("c"))
                yield
                wait(v, pe, "C", b, "s")
                v.tensor_reduce(st[:, 0:2], halves(6), AX, ALU.max).then_inc(*E.tick("max"))
                wait(v, dve, "C", b, "max")
                v.tensor_tensor(st[:, 12:14], bank[7][:, 0:2], st[:, 0:2], ALU.max).then_inc(*E.tick("mxs"))
                wait(v, dve, "C", b, "mxs")
                v.tensor_tensor(st[:, 12:14], st[:, 12:14], st[:, 10:12], ALU.add).then_inc(*E.tick("mxc"))
                wait(v, dve, "C", b, "mxc")
                v.tensor_tensor(st[:, 2:4], st[:, 10:12], st[:, 12:14], ALU.subtract).then_inc(*E.tick("nb"))
                yield
                wait(v, act, "C", b, "pn")
                v.tensor_tensor(st[:, 14:16], st[:, 4:6], st[:, 8:10], ALU.add).then_inc(*E.tick("z"))
                wait(v, dve, "C", b, "z")
                v.reciprocal(st[:, 6:8], st[:, 14:16]).then_inc(*E.tick("rs"))
                for r in range(2):
                    x = v.tensor_scalar(diag[:, r, :], ident, st[:, 8 + r:9 + r], None, ALU.mult)
                x.then_inc(*E.tick("diag"))
                take("C", 7, pT, b, "pT")
                yield
                yield
                wait(v, pe, "C", b, "o")
                wait(v, pool, "C", b, "xb")
                wait(v, dve, "C", b, "rs")
                for r in range(2):
                    x = v.scalar_tensor_tensor(X3[:, r, :], halves(7)[:, r, :], st[:, 6 + r:7 + r], XB[:, r, :], ALU.mult, ALU.add)
                x.then_inc(*E.tick("x"))
                wait(v, dve, "C", b, "x")
                moments("D1", X3, b)
                yield

                E = dve["D1"]
                wait(v, pool, "D1", b, "r")
                norm(YD, X3, 0).then_inc(*E.tick("y"))
                norm(N, X3, 2).then_inc(*E.tick("n"))
                yield
                yield
                rests("D1", b, 7, 6, True)
                yield
                values("D1", b, 16, 7, True)
                yield

            def post(b, last):
                E = dve["D2"]
                take("D2", 6, AOTD, b, "aoT")
                yield
                wait(v, pe, "D2", b, "wo")
                wait(v, pool, "D1", b, "yb")
                v.tensor_tensor(XP[:, :, :], halves(7), YB[:, :, :], ALU.add).then_inc(*E.tick("xp"))
                wait(v, dve, "D2", b, "xp")
                moments("D2", XP, b)
                yield
                wait(v, pool, "D2", b, "r")
                norm(N, XP, 0).then_inc(*E.tick("n"))
                yield
                wait(v, pe, "D2", b, "nT")
                for c in range(2):
                    x = v.tensor_scalar(H2T[:, c, :], halves(6)[:, c, :], col("L1_ffn_ln2_g", c), col("L1_ffn_ln2_b", c), ALU.mult, ALU.add)
                x.then_inc(*E.tick("h2T"))
                yield
                wait(v, pe, "D2", b, "lg")
                v.tensor_copy(logits[:, bass.ts(b, 2), :], bank[7][:, 0:2 * NE].rearrange("p (t e) -> p t e", t=2)).then_inc(*E.tick("lg"))
                yield

            schedule(v.Fori, B, lin1, lin2, post, lambda b: heads("HB", h0, b), lambda b: heads("HD", h1, b), lambda b: None, lambda b: None)

        @block.scalar
        def _(s_):
            s_.wait_ge(s_set, NSET)
            for events in act.values():
                events.start(s_)

            def take(part, bnk, dst, b, name, tick=None):
                wait(s_, pe, part, b, name)
                s_.activation(dst[:, :, :], halves(bnk), ACT.Copy).then_inc(*act[part].tick(tick or name))

            def take_cols(part, bnk, dst, b, name, tick, scale=None, bias=None):
                wait(s_, pe, part, b, name)
                for c in range(2):
                    kw = {} if scale is None else {"scale": col(scale, c)}
                    x = s_.activation(dst[:, c, :], halves(bnk)[:, c, :], ACT.Identity, bias=bias(c), **kw)
                x.then_inc(*act[part].tick(tick))

            def masks(part, s, w, b):
                s_.wait_ge(s_stack[s, "k"], b * STACKED + STACKED)
                for half in range(2):
                    for j in range(SLOT // w):
                        x = s_.activation(KM[w][0:MROW, 4 * half:4 * half + 4, j, :], KSs[0:MROW, 4 * half:4 * half + 4, :], ACT.Copy,
                                          scale=cst[0:MROW, C_MASK[w] + j:C_MASK[w] + j + 1])
                    x.then_inc(*act[part].tick(f"mask{half}"))

            def heads(n_steps, h, b):
                base = {n: now(s_, b * k) for n, k in dict(head=h.heads, group=h.groups).items()}

                def outputs(grp):
                    s_.wait_ge(h.pv, base["group"] + (grp + 1))
                    s_.activation(OS[:, grp, :], bank[4][:, 0:D], ACT.Copy).then_inc(h.os, 1)

                for i, p in product_of(range(h.slots + 3), range(h.pairs)):
                    for j in range(2 * p, 2 * p + 2) if 2 <= i <= h.slots + 1 else ():
                        n = (i - 2) * h.nh + j
                        s_.wait_ge(h.st, base["head"] + (n + 1))
                        if n >= 8:
                            s_.wait_ge(h.pv, base["group"] + (n // 4 - 1))
                        s_.activation(PT[:, n % 8, :, :], halves(2 + n % 2), ACT.Exp, scale=h.scale).then_inc(h.exp, 1)
                    if i >= 3 and p == h.pairs - 1 and (i - 2) * h.nh % 4 == 0:
                        outputs((i - 2) * h.nh // 4 - 1)
                    yield
                yield from idle(n_steps - (h.slots + 3) * h.pairs)

            def lin1(b):
                yield from idle(2)
                take("A", 6, nT, b, "nT")
                yield
                take_cols("A", 6, qT, b, "qT", "qT", bias=lambda c: qkbias[:, c:c + 1])
                yield
                wait(s_, dve, "A", b, "nb")
                for r in range(2):
                    x = s_.activation(PR[:, r, :], halves(7)[:, r, :], ACT.Exp, bias=st[:, 2 + r:3 + r], scale=float(D) ** -0.5, accum_out=st[:, 4 + r:5 + r])
                x.then_inc(*act["A"].tick("exp"))
                yield
                yield
                take("A", 7, cT, b, "cT")
                yield
                yield from idle(2)
                take_cols("B1", 7, zT, b, "nT", "zT", "L0_ffn_ln_g", lambda c: col("L0_ffn_ln_b", c))
                yield
                take("B1", 7, KH, b, "k", "kh")
                take("B1", 6, QH, b, "q", "qh")
                yield
                yield

            def lin2(b, more):
                yield from idle(3)
                for k in range(4):
                    for f in (2 * k, 2 * k + 1):
                        if f % 2 == 0:
                            wait_first(s_, (s_set, NSET), pe["B2"].sem, pe["B2"].at(b, f"f{k}"))
                        x = s_.activation(HT[:, f, :], halves(7 - k % 2)[:, f % 2, :], ACT.Gelu, bias=b1T[:, bass.ts(b, 1), f])
                    x.then_inc(*act["B2"].tick(f"f{k}"))
                    if k % 2:
                        yield
                yield from idle(3)
                take("C", 6, nT, b, "nT")
                yield
                take_cols("C", 6, qT, b, "qT", "qT", bias=lambda c: qkbias[:, 2 + c:3 + c])
                yield
                wait(s_, dve, "C", b, "nb")
                for r in range(2):
                    x = s_.activation(PR[:, r, :], halves(6)[:, r, :], ACT.Exp, bias=st[:, 2 + r:3 + r], accum_out=st[:, 4 + r:5 + r])
                x.then_inc(*act["C"].tick("exp"))
                for r in range(2):
                    x = s_.activation(st[:, 8 + r:9 + r], bank[7][:, r:r + 1], ACT.Exp, bias=st[:, 2 + r:3 + r])
                x.then_inc(*act["C"].tick("pn"))
                yield
                yield
                take("C", 6, cT, b, "cT")
                yield
                yield from idle(2)
                take_cols("D1", 6, zT, b, "nT", "zT", "L1_ffn_ln1_g", lambda c: col("L1_ffn_ln1_b", c))
                yield
                take_cols("D1", 6, KH, b, "k", "kh", bias=lambda c: col("L1_ffn_bk", c))
                take_cols("D1", 7, QH, b, "q", "qh", bias=lambda c: col("L1_ffn_bq", c))
                yield
                yield

            schedule(s_.Fori, B, lin1, lin2, lambda b, last: idle(POST), lambda b: heads(HEADS_B, h0, b), lambda b: heads(HEADS_D, h1, b),
                     lambda b: masks("B1", "B", 8, b), lambda b: masks("D1", "D", 16, b))


def experts(nc, a, out, scratch, sem, ident, ones, cst, logits, bank):
    B, S, D = a["x"].shape
    T = B * S
    NE, _, FD = a["L1_ffn_w1"].shape
    NT, DC, FC = T // P, D // P, FD // P
    CAP = -(-T // 4)
    GAIN = 1.0 - 0.2
    HALF = 512
    HT4 = HALF // P
    NH = CAP // HALF
    assert NH == 2

    w1_d = a["L1_ffn_w1"].rearrange("e (c p) f -> e p c f", p=P)
    w2_d = a["L1_ffn_w2"].rearrange("e (f p) d -> e p f d", p=P)
    tok_d = scratch["tokens"].rearrange("(n p) d -> n p d", p=P)
    res_d = scratch["residual"].rearrange("(n p) d -> n p d", p=P)
    out_d = out.rearrange("b (t p) d -> (b t) p d", p=P)
    slots_d = scratch["slots"].rearrange("(e h r p) d -> (e h) p r d", h=NH, r=HT4, p=P)
    y_d = scratch["outputs"].rearrange("(e h r p) d -> (e h) p r d", h=NH, r=HT4, p=P)

    with ExitStack() as stack:
        def sb(name, shape, dt=F32):
            return stack.enter_context(nc.sbuf_tensor(name, shape, dt))

        def table(name):
            return sb(name, [P, NT, NE])

        pr, eq, key, m1, m2, l2, cum, tot, run, loc1, loc2, keep = (
            table(n) for n in ("pr", "eq", "key", "m1", "m2", "l2", "cum", "tot", "run", "loc1", "loc2", "keep"))
        mx, zs, kx, t1, t2, den, f1, f2, g1, g2, w = (
            sb(n, [P, NT]) for n in ("mx", "zs", "kx", "t1", "t2", "den", "f1", "f2", "g1", "g2", "wv"))
        put1, put2, get1, get2 = (sb(n, [P, NT], I32) for n in ("put1", "put2", "get1", "get2"))
        tk = sb("tk", [P, 4, D])
        W1 = [sb(f"W1_{i}", [P, DC, FD]) for i in range(2)]
        W2 = [sb(f"W2_{i}", [P, FC, D]) for i in range(2)]
        B2 = [sb(f"B2_{i}", [P, 1, D]) for i in range(2)]
        b1rows, b1T = sb("b1rows2", [NE * FC, P]), sb("b1T2", [P, NE, FC])
        xg = [sb(f"xg{i}", [P, HT4, D]) for i in range(2)]
        xgT = [sb(f"xgT{i}", [P, DC, HALF]) for i in range(2)]
        hT = sb("hT", [P, FC, HALF])
        yo = [sb(f"yo{i}", [P, HT4, D]) for i in range(2)]
        ya, yb, rs, ob = (sb(n, [P, 4, D]) for n in ("ya", "yb", "rs", "ob"))

        s_ld, s_tk = sem("s_ld"), [sem(f"s_tk{i}") for i in range(4)]
        s_d, s_ex, s_cum, s_bt = sem("s_d"), sem("s_ex"), sem("s_cum"), sem("s_bt")
        s_routed, s_sc = sem("s_routed"), [sem(f"s_sc{i}") for i in range(4)]
        s_w = [sem(f"s_w{i}") for i in range(2)]
        s_xg = [sem(f"s_xg{i}") for i in range(2)]
        s_xt, s_xv, s_h, s_hr, s_y, s_yv = (sem(n) for n in ("s_xt", "s_xv", "s_h", "s_hr", "s_y", "s_yv"))
        s_yo = [sem(f"s_yo{i}") for i in range(2)]
        s_ya, s_rs, s_out = ([sem(f"{n}{i}") for i in range(4)] for n in ("s_ya", "s_rs", "s_out"))
        s_a1, s_a2 = sem("s_a1"), sem("s_a2")
        block = stack.enter_context(nc.Block())
        NROUTE = 2

        def load_weights(sp, i, e):
            sp.dma_start(W1[i][:, :, :], w1_d[e]).then_inc(s_w[i], 16)
            sp.dma_start(W2[i][:, :, :], w2_d[e]).then_inc(s_w[i], 16)
            sp.dma_start(B2[i][:, 0, :], a["L1_ffn_b2"][e].partition_broadcast(P)).then_inc(s_w[i], 16)

        @block.sync
        def _(sp):
            sp.dma_start(b1rows[:, :], a["L1_ffn_b1"].rearrange("e (f p) -> (e f) p", p=P)).then_inc(s_ld, 16)
            load_weights(sp, 0, 0)
            load_weights(sp, 1, 1)
            for n in range(NT):
                if n >= 4:
                    sp.wait_ge(s_sc[n % 4], 32 * (n // 4))
                sp.dma_start(tk[:, n % 4, :], tok_d[n]).then_inc(s_tk[n % 4], 16)
            for i in range(4):
                sp.wait_ge(s_sc[i], 32 * (NT // 4))
            for i in range(2):
                sp.sem_inc(s_yo[i], 16)
            with sp.Fori(0, NE // 2) as k:
                half_ = [now(sp, k * 4 + j) for j in range(4)]
                turned = [now(sp, k * 4 + 1 + (0 if j < 2 else j - 1)) for j in range(4)]
                stored = [now(sp, 1 + (k * 4 + (j + 1)) * HT4) for j in range(4)]
                nxt = [now(sp, (k * 2 + 2 + i) % NE) for i in range(2)]
                for j in range(4):
                    sp.wait_ge(s_xt, turned[j])
                    sp.dma_start(xg[j % 2][:, :, :], slots_d[half_[j]]).then_inc(s_xg[j % 2], 16)
                for j in range(4):
                    sp.wait_ge(s_yv, stored[j])
                    sp.dma_start(y_d[half_[j]], yo[j % 2][:, :, :]).then_inc(s_yo[j % 2], 16)
                    if j % 2 == 1:
                        load_weights(sp, j // 2, nxt[j // 2])
            for i in range(2):
                sp.wait_ge(s_yo[i], 16 + 16 * NE)
            for n in range(NT + 2):
                if n < NT:
                    if n >= 4:
                        sp.wait_ge(s_a2, n - 3)
                    sp.dma_start(rs[:, n % 4, :], res_d[n]).then_inc(s_rs[n % 4], 16)
                if n >= 2:
                    sp.wait_ge(s_a2, n - 1)
                    sp.dma_start(out_d[n - 2], ob[:, (n - 2) % 4, :]).then_inc(s_out[(n - 2) % 4], 16)
            for i in range(4):
                sp.wait_ge(s_out[i], 16 * (NT // 4))
            for i in range(2):
                sp.wait_ge(s_w[i], 48 * (NE // 2 + 1))

        @block.gpsimd
        def _(g):
            g.wait_ge(s_routed, 1)
            for n in range(NT):
                g.wait_ge(s_tk[n % 4], 16 * (n // 4 + 1))
                for put in (put1, put2):
                    g.indirect_dma_start(out=scratch["slots"], out_offset=bass.IndirectOffsetOnAxis(ap=put[:, n:n + 1], axis=0),
                                         in_=tk[:, n % 4, :], in_offset=None,
                                         bounds_check=NE * CAP - 1, oob_is_err=False).then_inc(s_sc[n % 4], 16)
            g.wait_ge(s_routed, 2)
            for i in range(2):
                g.wait_ge(s_yo[i], 16 + 16 * NE)
            for n in range(NT):
                if n >= 4:
                    g.wait_ge(s_a2, n - 3)
                for dst, get in ((ya, get1), (yb, get2)):
                    g.indirect_dma_start(out=dst[:, n % 4, :], out_offset=None, in_=scratch["outputs"],
                                         in_offset=bass.IndirectOffsetOnAxis(ap=get[:, n:n + 1], axis=0),
                                         bounds_check=NE * CAP - 1, oob_is_err=False).then_inc(s_ya[n % 4], 16)

        @block.tensor
        def _(t):
            mm = t.matmul
            t.wait_ge(s_ld, 16)
            t.transpose(bank[7][:, 0:NE * FC], b1rows[:, :], ident[0:NE * FC, 0:NE * FC]).then_inc(s_bt, 1)
            flat = lambda x: x[:, :, :].rearrange("p n e -> p (n e)")
            for i, m in enumerate((m1, m2)):
                t.wait_ge(s_ex, 1 + i)
                mm(bank[2 * i][:, 0:NT * NE], cst[:, C_TRI:C_TRI + P], flat(m), start=True, stop=True)
                mm(bank[2 * i + 1][:, 0:NT * NE], ones, flat(m), start=True, stop=True).then_inc(s_cum, 1)
            t.wait_ge(s_routed, 2)

            t.sem_inc(s_xt, 1)
            t.sem_inc(s_y, 1)
            with t.Fori(0, NE // 2) as k:
                for j in range(4):
                    u = k * 4 + j
                    i = j // 2
                    t.wait_ge(s_xg[j % 2], (k * 2 + (j // 2 + 1)) * 16)
                    for c in range(DC):
                        for r in range(HT4):
                            x = t.transpose(bank[c][:, r * P:(r + 1) * P], xg[j % 2][:, r, c * P:(c + 1) * P], ident)
                    x.then_inc(s_xt, 1)
                    t.wait_ge(s_xv, u * DC + DC)
                    t.wait_ge(s_w[i], k * 48 + 48)
                    for f in range(FC):
                        b = 2 + f % 2
                        if f >= 2:
                            t.wait_ge(s_hr, 1 + u * FC + (f - 1))
                        else:
                            t.wait_ge(s_hr, 1 + u * FC)
                        for c in range(DC):
                            x = mm(bank[b][:, :], W1[i][:, c, f * P:(f + 1) * P], xgT[j % 2][:, c, :], start=c == 0, stop=c == DC - 1)
                        x.then_inc(s_h, 1)
                    t.wait_ge(s_hr, 1 + u * FC + FC)
                    for r in range(HT4):
                        if r >= 2:
                            t.wait_ge(s_yv, 1 + u * HT4 + (r - 1))
                        else:
                            t.wait_ge(s_yv, 1 + u * HT4)
                        for f in range(FC):
                            x = mm(bank[4 + r % 2][:, 0:D], hT[:, f, r * P:(r + 1) * P], W2[i][:, f, :], start=f == 0, stop=f == FC - 1)
                        x.then_inc(s_y, 1)

        @block.scalar
        def _(s_):
            s_.wait_ge(s_d, 2)
            s_.activation(pr[:, :, :], pr[:, :, :], ACT.Exp).then_inc(s_a1, 1)
            s_.sem_inc(s_hr, 1)
            with s_.Fori(0, NE // 2) as k:
                for j in range(4):
                    u = k * 4 + j
                    for f in range(FC):
                        if f == 0:
                            s_.wait_ge(s_y, 1 + u * HT4)
                        e = k * 2 + j // 2
                        wait_first(s_, (s_bt, 1), s_h, u * FC + (f + 1))
                        s_.activation(hT[:, f, :], bank[2 + f % 2][:, :], ACT.Relu, bias=b1T[:, bass.ds(e, 1), f]).then_inc(s_hr, 1)

        @block.vector
        def _(v):
            count = [0]

            def link(ins):
                count[0] += 1
                ins.then_inc(s_d, 1)
                v.wait_ge(s_d, count[0])

            def each(x):
                return x[:, :].unsqueeze(2).broadcast_to([P, NT, NE])

            def const(c):
                return cst[:, c:c + NE].unsqueeze(1).broadcast_to([P, NT, NE])

            A = lambda x: x[:, :, :]
            tt, sc = v.tensor_tensor, v.tensor_scalar
            link(v.tensor_reduce(mx[:, :], A(logits), AX, ALU.max))
            link(tt(A(pr), A(logits), each(mx), ALU.subtract))

            def first_max(src, m, dst):
                link(tt(A(eq), A(src), each(m), ALU.is_equal))
                link(tt(A(key), A(eq), const(C_FIRST), ALU.mult))
                link(v.tensor_reduce(kx[:, :], A(key), AX, ALU.max))
                link(tt(A(dst), A(key), each(kx), ALU.is_equal))

            first_max(logits, mx, m1)
            v.tensor_copy(w[:, 0:1], kx[:, 0:1]).then_inc(s_ex, 1)
            link(v.scalar_tensor_tensor(A(l2), A(m1), -3.0e38, A(logits), ALU.mult, ALU.add))
            link(v.tensor_reduce(mx[:, :], A(l2), AX, ALU.max))
            first_max(l2, mx, m2)
            v.tensor_copy(w[:, 0:1], kx[:, 0:1]).then_inc(s_ex, 1)
            v.wait_ge(s_a1, 1)
            link(v.tensor_reduce(zs[:, :], A(pr), AX, ALU.add))
            link(v.reciprocal(zs[:, :], zs[:, :]))
            link(tt(A(pr), A(pr), each(zs), ALU.mult))

            v.wait_ge(s_bt, 1)
            v.tensor_copy(b1T[:, :, :].rearrange("p e f -> p (e f)"), bank[7][:, 0:NE * FC])

            def places(i, m, loc, first_total):
                v.wait_ge(s_cum, i + 1)
                view = lambda b: bank[b][:, 0:NT * NE].rearrange("p (n e) -> p n e", e=NE)
                link(v.tensor_copy(A(tot), view(2 * i + 1)))
                link(sc(A(loc), view(2 * i), -1.0, None, ALU.add))
                link(v.tensor_copy(A(run), A(tot)))
                src, dst, step = run, cum, 1
                while step < NT:
                    v.tensor_copy(dst[:, 0:step, :], src[:, 0:step, :])
                    link(tt(dst[:, step:NT, :], src[:, step:NT, :], src[:, 0:NT - step, :], ALU.add))
                    src, dst, step = dst, src, 2 * step
                link(tt(loc[:, 1:NT, :], loc[:, 1:NT, :], src[:, 0:NT - 1, :], ALU.add))
                if first_total is not None:
                    link(tt(A(loc), A(loc), first_total[:, :, :].broadcast_to([P, NT, NE]), ALU.add))
                return src

            def use(m, loc, t_, g_, f_, put, get):
                link(v.scalar_tensor_tensor(A(keep), A(loc), float(CAP), A(m), ALU.is_lt, ALU.mult))
                link(v.tensor_reduce(g_[:, :], A(keep), AX, ALU.add))
                link(tt(A(key), A(keep), A(pr), ALU.mult))
                link(v.tensor_reduce(t_[:, :], A(key), AX, ALU.add))
                link(sc(A(key), A(loc), float(CAP - 1), None, ALU.min))
                link(tt(A(key), A(key), const(C_BASE), ALU.add))
                link(tt(A(key), A(key), A(m), ALU.mult))
                link(v.tensor_reduce(f_[:, :], A(key), AX, ALU.add))
                v.tensor_copy(get[:, :], f_[:, :])
                link(sc(w[:, :], g_[:, :], -float(NE * CAP), float(NE * CAP), ALU.mult, ALU.add))
                link(tt(w[:, :], w[:, :], f_[:, :], ALU.add))
                link(v.tensor_copy(put[:, :], w[:, :]))

            src = places(0, m1, loc1, None)
            total1 = sb("total1", [P, 1, NE])
            link(v.tensor_copy(total1[:, :, :], src[:, NT - 1:NT, :]))
            places(1, m2, loc2, total1)
            use(m1, loc1, t1, g1, f1, put1, get1)
            use(m2, loc2, t2, g2, f2, put2, get2)
            v.tensor_copy(w[:, 0:1], kx[:, 0:1]).then_inc(s_routed, 1)
            link(tt(den[:, :], t1[:, :], t2[:, :], ALU.add))
            link(sc(den[:, :], den[:, :], 1.1920929e-07, None, ALU.max))
            link(v.reciprocal(den[:, :], den[:, :]))
            for t_, g_ in ((t1, g1), (t2, g2)):
                link(tt(t_[:, :], t_[:, :], den[:, :], ALU.mult))
                link(v.scalar_tensor_tensor(g_[:, :], t_[:, :], GAIN, g_[:, :], ALU.mult, ALU.mult))
            v.tensor_copy(w[:, 0:1], kx[:, 0:1]).then_inc(s_routed, 1)

            v.sem_inc(s_yv, 1)
            with v.Fori(0, NE // 2) as k:
                for j in range(4):
                    u = k * 4 + j
                    v.wait_ge(s_xt, u + 2)
                    for c in range(DC):
                        v.tensor_copy(xgT[j % 2][:, c, :], bank[c][:, :]).then_inc(s_xv, 1)
                    for r in range(HT4):
                        v.wait_ge(s_y, 1 + u * HT4 + (r + 1))
                        if r == 0:
                            v.wait_ge(s_yo[j % 2], 16 + (k * 2 + j // 2) * 16)
                        v.tensor_tensor(yo[j % 2][:, r, :], bank[4 + r % 2][:, 0:D], B2[j // 2][:, 0, :], ALU.add).then_inc(s_yv, 1)
            for n in range(NT):
                v.wait_ge(s_ya[n % 4], 32 * (n // 4 + 1))
                v.wait_ge(s_rs[n % 4], 16 * (n // 4 + 1))
                v.scalar_tensor_tensor(rs[:, n % 4, :], ya[:, n % 4, :], g1[:, n:n + 1], rs[:, n % 4, :], ALU.mult, ALU.add).then_inc(s_a1, 1)
                v.wait_ge(s_a1, n + 2)
                if n >= 4:
                    v.wait_ge(s_out[n % 4], 16 * (n // 4))
                v.scalar_tensor_tensor(ob[:, n % 4, :], yb[:, n % 4, :], g2[:, n:n + 1], rs[:, n % 4, :], ALU.mult, ALU.add).then_inc(s_a2, 1)


def program(nc, a, out):
    B, S, D = a["x"].shape
    T, NE = B * S, a["L1_ffn_w1"].shape[0]
    CAP = -(-T // 4)
    scratch = {n: nc.dram_tensor(f"{n}_dram", (r, D), F32, kind="Internal").ap()
               for n, r in (("residual", T), ("tokens", T), ("slots", NE * CAP), ("outputs", NE * CAP))}
    with ExitStack() as stack:
        def sem(name):
            return stack.enter_context(nc.semaphore(name))

        cst_t = stack.enter_context(nc.sbuf_tensor("cst", [P, C_ALL], F32))
        ones_t = stack.enter_context(nc.sbuf_tensor("ones", [P, P], F32))
        logits = stack.enter_context(nc.sbuf_tensor("logits", [P, T // P, NE], F32))
        bank = [stack.enter_context(nc.psum_tensor(f"bank{i}", [P, 512], F32)) for i in range(8)]
        ident, ones = cst_t[:, C_IDENT:C_IDENT + P], ones_t[:, :]
        layers(nc, a, scratch, sem, ident, ones_t, cst_t, logits, bank)
        experts(nc, a, out, scratch, sem, ident, ones, cst_t, logits, bank)


_UNUSED = ("L0_ffn_gate_w",)


def constants(NE, CAP):
    import numpy as np

    c = np.zeros((P, C_ALL), np.float32)
    p = np.arange(P)
    for width, at in C_MASK.items():
        for j in range(SLOT // width):
            c[:, at + j] = p % SLOT // width == j
    for j in range(4):
        c[MROW + j, C_SEL + j] = c[MROW + 4 + j, C_SEL + j] = 1.0
    c[:, C_HALF:C_HALF + 4] = -0.5
    c[:, C_FIRST:C_FIRST + NE] = NE - np.arange(NE)
    c[:, C_BASE:C_BASE + NE] = CAP * np.arange(NE)
    c[:, C_TRI:C_TRI + P] = p[:, None] <= p[None, :]
    c[:, C_IDENT:C_IDENT + P] = np.eye(P)
    return c


def kernel(**inputs):
    import numpy as _np
    import concourse.bacc as _bacc
    from concourse import mybir as _mybir
    from concourse.bass_utils import run_bass_kernel_spmd as _run

    nc = _bacc.Bacc("TRN2", target_bir_lowering=False, num_devices=1)
    arrays, args = {}, {}
    named = {n: _np.ascontiguousarray(v) for n, v in inputs.items() if n not in _UNUSED}
    B, S, _ = named["x"].shape
    named["constants"] = constants(named["L1_ffn_w1"].shape[0], -(-B * S // 4))
    for name, v in named.items():
        arrays[f"in_{name}_dram"] = v
        args[name] = nc.dram_tensor(f"in_{name}_dram", v.shape, _mybir.dt.from_np(v.dtype), kind="ExternalInput").ap()
    out = nc.dram_tensor("out_0_dram", named["x"].shape, _mybir.dt.from_np(named["x"].dtype), kind="ExternalOutput").ap()
    program(nc, args, out)
    r = _run(nc, [arrays], core_ids=[0])
    return r.results[0]["out_0_dram"]
```

```python
from contextlib import ExitStack
from itertools import product as product_of

import concourse.bass as bass
from concourse import mybir

F32 = mybir.dt.float32
F32R = mybir.dt.float32r
I32 = mybir.dt.int32
ALU = mybir.AluOpType
ACT = mybir.ActivationFunctionType
AX = mybir.AxisListType.X

P = 128
EPS = 1e-5
SLOT = 32
PARTS = 3
MROW = PARTS * SLOT
C_MASK = {8: 0, 16: 4}
C_SEL, C_HALF, C_EPS, C_FIRST, C_BASE, C_TRI, C_IDENT, C_PAST, C_ID, C_ALL = 8, 12, 16, 20, 28, 36, 164, 292, 296, 328
ROW = 256 + 4


def now(eng, value):
    eng.compute_val(value)
    return value


def wait_first(eng, static, sem, value):
    value = now(eng, value)
    eng.wait_ge(*static)
    eng.wait_ge(sem, value)


class Events:

    def __init__(self, sem, names):
        self.sem, self.names, self.done = sem, names.split(), []

    def start(self, eng):
        eng.sem_inc(self.sem, 1)

    def before(self, rnd):
        return rnd * len(self.names) + 1

    def at(self, rnd, name):
        return rnd * len(self.names) + self.names.index(name) + 2

    def tick(self, name):
        assert self.names[len(self.done) % len(self.names)] == name, (self.names, self.done, name)
        self.done.append(name)
        return self.sem, 1


class Heads:

    def __init__(self, name, width, D, sem):
        self.width = width
        self.nh = SLOT // width
        self.slots = D // SLOT
        self.pairs = self.nh // 2
        self.units = 2 * self.pairs
        self.heads = D // width
        self.groups = self.heads // 4
        self.scale = float(width) ** -0.5
        self.scored = sem(f"{name}_scored")
        self.maxed = sem(f"{name}_maxed")
        self.negated = sem(f"{name}_negated")
        self.parted = sem(f"{name}_parted")
        self.turned = sem(f"{name}_turned")
        self.rows = sem(f"{name}_rows")
        self.st = sem(f"{name}_st")
        self.exp = sem(f"{name}_exp")
        self.pv = sem(f"{name}_pv")
        self.os = sem(f"{name}_os")


def chain(*threads):
    for thread in threads:
        yield from thread


def steps(thread, n):
    for _ in range(n):
        next(thread)


def weave(main, side, n_main, n_side, beside, masks=None, masks_at=0):
    for i in range(n_main):
        if masks and i == masks_at:
            masks()
        next(main)
        n = min(beside[i], n_side)
        steps(side, n)
        n_side -= n
    steps(side, n_side)
    if masks and not n_main:
        masks()


def idle(n):
    return iter([0] * n)


LIN1, LIN2, POST, HEADS_B, HEADS_D = 12, 18, 5, 26, 13
LEAD_POST, LEAD_LIN1, AHEAD = 2, 2, 2
BEGUN = 5
BESIDE_B = [1, 2, 1, 1, 1, 1, 1, 1, 1, 1, 2, 1, 1, 1, 1, 1, 1, 1, 1, 0, 1, 0, 1, 0, 0, 0]
MASKS_D, MASKS_B = 22, 11
BESIDE_D = [1, 1, 1, 1, 0, 1, 1, 1, 1, 0, 0, 0, 0]


def schedule(fori, n, lin1, lin2, post, heads_b, heads_d, masks_b, masks_d):
    def round_(r, b=True, p=True, l=True, d=True, ahead=True, last=False, n_ahead=AHEAD, begun=None, begin=None):
        nxt = lin1(r + 1) if ahead else iter(())
        n_ahead, n_lead = n_ahead * ahead, LEAD_LIN1 * ahead
        side = post(r - 2, last) if p else iter(())
        steps(side, LEAD_POST * p)
        n_lin2 = LIN2 * l
        if begun:
            n_lin2 -= BEGUN
        side = chain(side, begun or (lin2(r - 1, ahead) if l else iter(())), (next(nxt) for _ in range(n_ahead)))
        weave(heads_b(r) if b else iter(()), side, HEADS_B * b, (POST - LEAD_POST) * p + n_lin2 + n_ahead, BESIDE_B,
              (lambda: masks_d(r - 1)) if d else None, MASKS_D)
        steps(nxt, n_lead)
        weave(heads_d(r - 1) if d else iter(()), begin or nxt, HEADS_D * d, BEGUN if begin else (LIN1 - n_ahead - n_lead) * ahead, BESIDE_D,
              (lambda: masks_b(r + 1)) if ahead else None, MASKS_B)

    round_(-1, b=False, p=False, l=False, d=False)
    round_(0, p=False, l=False, d=False, n_ahead=7)
    round_(1, p=False)
    with fori(2, n - 1) as r:
        round_(r)
    last_lin2 = lin2(n - 1, False)
    round_(n - 1, ahead=False, begin=last_lin2)
    round_(n, b=False, ahead=False, last=True, begun=last_lin2)
    round_(n + 1, b=False, l=False, d=False, ahead=False, last=True)


def layers(nc, a, out, scratch, sem, ident, ones, cst, logits, bank):
    B, S, D = a["x"].shape
    NE, _, FD = a["L0_ffn_w1"].shape
    DC, FC = D // P, FD // P
    assert S == 2 * P and DC == 2 and FC == 8 and B % NE == 0

    x_d = a["x"].rearrange("b (t p) d -> b p t d", p=P)
    ctx_d = a["ctx_1024"].rearrange("b (t p) d -> b p t d", p=P)
    res_d = out[0:B * S, :].rearrange("(b t p) d -> b p t d", p=P, t=2)
    tok_d = scratch["tokens"].rearrange("(b t p) d -> b p t d", p=P, t=2)
    w1_d = a["L0_ffn_w1"].rearrange("e (c p) f -> e p c f", p=P)
    w2_d = a["L0_ffn_w2"].rearrange("e (f p) d -> e p f d", p=P)

    with ExitStack() as stack:
        def sb(name, shape, dt=F32):
            return stack.enter_context(nc.sbuf_tensor(name, shape, dt))

        def tile(name, dt=F32):
            return sb(name, [P, 2, D], dt)

        MA, WA, MC, WvC = tile("MA"), tile("WA"), tile("MC"), tile("WvC")
        wB = {n: tile(f"wB_{n}") for n in ("wq", "wk", "wv", "wo")}
        wD = {n: tile(f"wD_{n}") for n in ("wq", "wk", "wv", "wo")}
        wr = sb("wr", [P, DC, NE])
        cols, b1T = sb("cols", [P, 24]), sb("b1T", [P, B, FC])
        rowA, rowbvC, rowu, rowbvD, rowboD, rowg2, rowb2 = (
            sb(n, [P, 1, D]) for n in ("rowA", "rowbvC", "rowu", "rowbvD", "rowboD", "rowg2", "rowb2"))
        qkbias = sb("qkbias", [P, 4])
        bqbk = sb("bqbk", [P, 1])
        X0, CX, XB, X1, X1c, Yc, X2, X3, XF, N, Y, YB = (
            tile(n) for n in ("X0", "CX", "XB", "X1", "X1c", "Yc", "X2", "X3", "XF", "N", "Y", "YB"))
        nT, cxT, qT, PR, pT, cT, AOT, XFT, H2, RES = (
            tile(n) for n in ("nT", "cxT", "qT", "PR", "pT", "cT", "AOT", "XFT", "H2", "RES"))
        AO = {8: tile("AO0"), 16: tile("AO1")}
        zT, prT, AOTD, H2T, XP, YD = pT, AOT, pT, XFT, XF, X2
        QH, QL, KH, KL = (t[:, :, :].bitcast(F32R) for t in (PR, cT, tile("KH"), AOT))
        diag = sb("diag", [P, 2, P])
        bn, mv = sb("bn", [P, 2, 6]), sb("mv", [P, 2, 2])
        uw, rr = sb("uw", [P, 4]), sb("rr", [P, 4])
        st = sb("st", [P, 20])
        W1, W2, B2 = sb("W1", [P, DC, FD]), sb("W2", [P, FC, D]), sb("B2", [P, 1, D])
        HT = sb("HT", [P, FC, 2 * P])
        KS = HT[:, :, :].rearrange("p (c g) t -> p c g t", c=DC)
        KSs = HT
        QS = {8: sb("QS0", [P, 8, D], F32R), 16: sb("QS1", [P, 8, D], F32R)}
        KM = {8: sb("KM0", [P, 8, 4, D], F32R), 16: sb("KM1", [P, 8, 2, D], F32R)}
        MX, MH, MT = sb("MX", [P, 2, 2, 4]), sb("MH", [P, 2, 2, 4], F32R), sb("MT", [P, 2, 2, P])
        PT = sb("PT", [P, 8, 2, D])
        VA = {w: sb(f"VA{w}", [P, 2, D // w * (w + 1) + SLOT - w - 1]) for w in (8, 16)}
        OS = sb("OS", [P, 8, D])
        rh = sb("rh", [P, 4, 4, 4])
        raw = {n: PT[:, i, :, :] for i, n in enumerate(("WqA", "WkA", "WvA", "WoA", "WqC", "WkC"))}
        vecs, b1rows = OS[0:24, 0, 0:P], OS[:, 1, 0:P]

        PART_RESTS = {"k": (False, False, True), "q": (False, True, False)}

        def stacked(width, w, part, g):
            stack_ = KS if w == "k" else QS[width][:, :, :].rearrange("p (c g) t -> p c g t", c=DC)
            src = {"k": (KH, KL), "q": (QH, QL)}[w][PART_RESTS[w][part]]
            return (stack_[part * SLOT:(part + 1) * SLOT, :, g, :].bitcast(F32),
                    src[g * SLOT:(g + 1) * SLOT, :, :].bitcast(F32))

        slots_d = scratch["slots"].rearrange("(n p r) d -> n p (r d)", p=P, r=4)
        NZERO = 16 * slots_d.shape[0]

        def final(b):
            return isinstance(b, int) and b == B - 1

        def halves(b):
            return bank[b][:, :].rearrange("p (c t) -> p c t", c=2)

        def row(t):
            return t[:, :, :].broadcast_to([P, 2, D])

        COLS = ["L0_xattn_bv", "L0_xattn_bq", "L0_ffn_ln_g", "L0_ffn_ln_b", "L1_xattn_bq", "L1_xattn_bk",
                "L1_ffn_bq", "L1_ffn_bk", "L1_ffn_ln1_g", "L1_ffn_ln1_b",
                "L1_ffn_ln2_g", "L1_ffn_ln2_b"]
        NV = 2 * len(COLS)

        def col(name, c):
            i = 2 * COLS.index(name) + c
            return cols[:, i:i + 1]

        s_load, s_zero, s_cst, s_setpe, s_set = (sem(n) for n in ("s_load", "s_zero", "s_cst", "s_setpe", "s_set"))
        s_x, s_cxA, s_cxC, s_w, s_store = (sem(n) for n in ("s_x", "s_cxA", "s_cxC", "s_w", "s_store"))
        s_stack = {(s, w): sem(f"s_stack_{w}{s}") for s in "BD" for w in "kq"}
        s_rests = {(s, w): sem(f"s_rests_{w}{s}") for s in "BD" for w in "kq"}
        STACKED, RESTED = 16 * (PARTS - 1) * 4, 16 * 4
        h0, h1 = Heads("h0", 8, D, sem), Heads("h1", 16, D, sem)
        pe = {"A": Events(sem("pe_A"), "nT cxT qT s pT cT o"),
              "B1": Events(sem("pe_B1"), "nT k q v"), "HB": Events(sem("pe_HB"), "os0 os1 os2 os3"),
              "B2": Events(sem("pe_B2"), "aoT wo xfT f0 f1 f2 f3 y"),
              "C": Events(sem("pe_C"), "nT cxT qT self s pT cT o"),
              "D1": Events(sem("pe_D1"), "nT k q v"), "HD": Events(sem("pe_HD"), "os0 os1"),
              "D2": Events(sem("pe_D2"), "aoT wo nT lg")}
        dve = {"A": Events(sem("dve_A"), "bn mv uw n cxT max nb pT rs x"),
               "B1": Events(sem("dve_B1"), "bn mv uw y n kl ql v"), "HB": Events(sem("dve_HB"), "rh0 os0 rh1 os1 rh2 os2 rh3 os3"),
               "B2": Events(sem("dve_B2"), "aoT xf xfT x"),
               "C": Events(sem("dve_C"), "bn mv uw n cxT c0 c max mxs mxc nb z rs diag pT x"),
               "D1": Events(sem("dve_D1"), "bn mv uw y n kl ql v"), "HD": Events(sem("dve_HD"), "rh0 os0 rh1 os1"),
               "D2": Events(sem("dve_D2"), "aoT xp bn mv uw n h2T lg")}
        pool = {"A": Events(sem("pool_A"), "r xb"), "B1": Events(sem("pool_B1"), "r"), "HB": Events(sem("pool_HB"), "x1 y"),
                "B2": Events(sem("pool_B2"), "xb"), "C": Events(sem("pool_C"), "r xb prT"), "D1": Events(sem("pool_D1"), "r yb"),
                "D2": Events(sem("pool_D2"), "r g h2 res")}
        act = {"A": Events(sem("act_A"), "nT qT exp cT"), "B1": Events(sem("act_B1"), "zT kh qh mask0 mask1"),
               "B2": Events(sem("act_B2"), "f0 f1 f2 f3"), "C": Events(sem("act_C"), "nT qT exp pn cT"),
               "D1": Events(sem("act_D1"), "zT kh qh mask0 mask1")}

        def wait(eng, table, part, rnd, name):
            eng.wait_ge(table[part].sem, table[part].at(rnd, name))

        block = stack.enter_context(nc.Block())

        rows = lambda n: a[n].rearrange("(c p) d -> p c d", p=P)
        loads = [(raw[n], rows(f"L0_xattn_{n[:2]}" if n[2] == "A" else f"L1_xattn_{n[:2]}")) for n in raw]
        loads += [(WvC[:, :, :], rows("L1_xattn_Wv"))]
        loads += [(w[n][:, :, :], rows(f"{layer}_ffn_{n}")) for w, layer in ((wB, "L0"), (wD, "L1")) for n in w]
        loads.append((wr[:, :, :], rows("L1_ffn_wr")))
        loads += [(vecs[2 * i:2 * i + 2, :], a[n].rearrange("(c p) -> c p", p=P)) for i, n in enumerate(COLS)]
        loads += [(b1rows[r * NE * FC:(r + 1) * NE * FC, :], a["L0_ffn_b1"].rearrange("e (f p) -> (e f) p", p=P)) for r in range(B // NE)]
        loads += [(t[:, 0, :], a[n].partition_broadcast(P)) for t, n in (
            (rowA, "L0_xattn_bo"), (rowbvC, "L1_xattn_bv"), (rowbvD, "L1_ffn_bv"), (rowboD, "L1_ffn_bo"),
            (rowg2, "L1_ffn_ln2_g"), (rowb2, "L1_ffn_ln2_b"))]
        loads.append((cst[:, :], a["constants"]))
        NLOAD = 16 * len(loads)
        NSET = 11

        @block.sync
        def _(sp):
            def load_x(b):
                sp.dma_start(X0[:, :, :], x_d[b]).then_inc(s_x, 16)

            def load_cx(b, s):
                sp.dma_start(CX[:, :, :], ctx_d[b]).then_inc(s, 16)

            def load_w(b):
                e = now(sp, b % NE)
                sp.dma_start(W1[:, :, :], w1_d[e]).then_inc(s_w, 16)
                sp.dma_start(W2[:, :, :], w2_d[e]).then_inc(s_w, 16)
                sp.dma_start(B2[:, 0, :], a["L0_ffn_b2"][e].partition_broadcast(P)).then_inc(s_w, 16)

            def ready(table, part, rnd, name):
                value = now(sp, table[part].at(rnd, name))
                sp.wait_ge(s_cst, 1)
                sp.wait_ge(table[part].sem, value)

            load_x(0)
            load_cx(0, s_cxA)
            for dst, src in loads:
                sp.dma_start(dst, src).then_inc(s_load, 16)
            load_w(0)
            sp.wait_ge(s_cst, 1)
            zeros = HT[:, :, :].rearrange("p f t -> p (f t)")
            for i in range(slots_d.shape[0]):
                sp.dma_start(slots_d[i], zeros[:, 0:4 * ROW]).then_inc(s_zero, 16)
            sp.wait_ge(s_zero, NZERO)
            sp.sem_inc(s_store, 16)

            def stacks(part, s, width, b):
                for w in "kq":
                    now(sp, b)
                    ready(act, part, b, w + "h")
                    for part_, rest in enumerate(PART_RESTS[w]):
                        for g in range(4) if not rest else ():
                            dst, src = stacked(width, w, part_, g)
                            sp.dma_start(dst, src).then_inc(s_stack[s, w], 16)
                now(sp, b)
                ready(dve, part, b, "ql")
                for g in range(4):
                    dst, src = stacked(width, "q", PART_RESTS["q"].index(True), g)
                    sp.dma_start(dst, src).then_inc(s_rests[s, "q"], 16)

            def lin1(b):
                first = isinstance(b, int) and b == 0
                yield from idle(6)
                if not first:
                    ready(pe, "A", b, "cT")
                    load_cx(now(sp, b - 1), s_cxC)
                else:
                    ready(pe, "A", b, "cT")
                    load_cx(1, s_cxA)
                    ready(dve, "A", b, "n")
                    ready(pool, "A", b, "xb")
                    load_x(1)
                yield
                yield from idle(3)
                stacks("B1", "B", 8, b)
                yield
                yield

            def lin2(b, more):
                yield from idle(6)
                if not (isinstance(b, int) and b == B - 1):
                    nb = now(sp, b + 1)
                    ready(pe, "B2", b, "y")
                    ready(pool, "B2", b, "xb")
                    load_w(nb)
                yield
                yield from idle(5)
                ready(pe, "C", b, "cT")
                if more:
                    nb = now(sp, b + 2)
                    load_cx(nb, s_cxA)
                    load_x(nb)
                elif b == B - 2:
                    load_cx(B - 1, s_cxC)
                yield
                yield from idle(3)
                stacks("D1", "D", 16, b)
                yield
                yield

            def post(b, last):
                yield from idle(2)
                ready(pool, "D2", b, "h2")
                sp.dma_start(tok_d[now(sp, b)], H2[:, :, :]).then_inc(s_store, 16)
                ready(pool, "D2", b, "res")
                sp.dma_start(res_d[now(sp, b)], RES[:, :, :]).then_inc(s_store, 16)
                yield
                yield from idle(2)

            schedule(sp.Fori, B, lin1, lin2, post, lambda b: idle(HEADS_B), lambda b: idle(HEADS_D), lambda b: None, lambda b: None)
            sp.wait_ge(s_store, 16 + B * 32)

        @block.gpsimd
        def _(g):
            def ready(sem_, value):
                wait_first(g, (s_cst, 1), sem_, value)

            g.memset(HT[:, :, :], 0.0).then_inc(s_cst, 1)
            g.memset(MT[:, :, :, :], 0.0)
            for w in VA:
                g.memset(VA[w][:, :, :], 0.0)
                g.memset(QS[w][:, :, :].bitcast(F32), 0.0)
                g.memset(KM[w][:, :, :, :].bitcast(F32), 0.0)
            g.memset(ones[:, :], 1.0).then_inc(s_cst, 1)

            def power(part, b):
                ready(dve[part].sem, dve[part].at(b, "uw"))
                g.tensor_tensor(rr[:, :], uw[:, :], cst[:, C_HALF:C_HALF + 4], ALU.pow).then_inc(*pool[part].tick("r"))

            def rests(part, s, width, b):
                if isinstance(b, int) and b == 0 and s == "B":
                    g.wait_ge(s_zero, NZERO)
                ready(dve[part].sem, dve[part].at(b, "kl"))
                for i in range(4):
                    dst, src = stacked(width, "k", PART_RESTS["k"].index(True), i)
                    g.dma_start(dst, src).then_inc(s_rests[s, "k"], 16)

            g.wait_ge(s_load, NLOAD)
            g.wait_ge(s_set, NSET)
            for events in pool.values():
                events.start(g)

            def lin1(b):
                power("A", b)
                yield
                ready(dve["A"].sem, dve["A"].at(b, "n"))
                g.tensor_tensor(XB[:, :, :], X0[:, :, :], row(rowA), ALU.add).then_inc(*pool["A"].tick("xb"))
                yield
                yield from idle(5)
                power("B1", b)
                yield
                yield from idle(2)
                rests("B1", "B", 8, b)
                yield
                yield

            def heads_b(b):
                yield from idle(HEADS_B - 1)
                if not (isinstance(b, int) and b == 0):
                    ready(dve["B2"].sem, dve["B2"].at(b - 1, "x"))
                ready(dve["B1"].sem, dve["B1"].at(b, "n"))
                g.tensor_copy(X1c[:, :, :], X1[:, :, :]).then_inc(*pool["HB"].tick("x1"))
                g.tensor_copy(Yc[:, :, :], Y[:, :, :]).then_inc(*pool["HB"].tick("y"))
                yield

            def lin2(b, more):
                yield from idle(3)
                ready(s_w, b * 48 + 48)
                ready(pool["HB"].sem, pool["HB"].at(b, "x1"))
                g.tensor_tensor(XB[:, :, :], X1c[:, :, :], row(B2), ALU.add).then_inc(*pool["B2"].tick("xb"))
                yield
                yield from idle(2)
                power("C", b)
                yield
                ready(dve["C"].sem, dve["C"].at(b, "n"))
                g.tensor_tensor(XB[:, :, :], X2[:, :, :], row(rowbvC), ALU.add).then_inc(*pool["C"].tick("xb"))
                yield
                yield
                ready(act["C"].sem, act["C"].at(b, "qT"))
                g.tensor_tensor(prT[:, :, :], qT[:, :, :], nT[:, :, :], ALU.mult).then_inc(*pool["C"].tick("prT"))
                yield
                yield from idle(3)
                power("D1", b)
                yield
                ready(dve["D1"].sem, dve["D1"].at(b, "y"))
                g.tensor_tensor(YB[:, :, :], YD[:, :, :], row(rowboD), ALU.add).then_inc(*pool["D1"].tick("yb"))
                yield
                yield
                rests("D1", "D", 16, b)
                yield
                yield

            def post(b, last):
                yield
                power("D2", b)
                yield
                ready(s_store, 16 + b * 32)
                ready(dve["D2"].sem, dve["D2"].at(b, "n"))
                g.tensor_tensor(H2[:, :, :], N[:, :, :], row(rowg2), ALU.mult).then_inc(*pool["D2"].tick("g"))
                ready(pool["D2"].sem, pool["D2"].at(b, "g"))
                g.tensor_tensor(H2[:, :, :], H2[:, :, :], row(rowb2), ALU.add).then_inc(*pool["D2"].tick("h2"))
                g.tensor_tensor(RES[:, :, :], X3[:, :, :], XP[:, :, :], ALU.add).then_inc(*pool["D2"].tick("res"))
                yield
                yield from idle(2)

            schedule(g.Fori, B, lin1, lin2, post, heads_b, lambda b: idle(HEADS_D), lambda b: None, lambda b: None)

        @block.tensor
        def _(t):
            mm = t.matmul
            t.wait_ge(s_load, NLOAD)
            t.wait_ge(s_cst, 2)

            def turn(b, src):
                for c in range(2):
                    for r in range(2):
                        i = t.transpose(halves(b)[:, c, r * P:(r + 1) * P], src[:, r, c * P:(c + 1) * P], ident)
                return i

            def product(b, lhsT, rhs, m=2, last=True):
                for o in range(m):
                    for c in range(2):
                        i = mm(halves(b)[:, o, :], lhsT[:, c, o * P:(o + 1) * P], rhs[:, c, :], start=c == 0, stop=last and c == 1)
                return i

            t.transpose(bank[0][:, 0:NV], vecs, ident[0:NV, 0:NV])
            t.transpose(bank[1][:, 0:P], b1rows, ident).then_inc(s_setpe, 1)
            turn(2, raw["WoA"]).then_inc(s_setpe, 1)
            turn(3, raw["WqC"]).then_inc(s_setpe, 1)
            turn(4, raw["WkC"]).then_inc(s_setpe, 1)
            product(5, raw["WqA"], raw["WkA"]).then_inc(s_setpe, 1)
            t.wait_ge(s_set, 4)
            product(6, raw["WvA"], nT).then_inc(s_setpe, 1)
            product(7, qT, cxT).then_inc(s_setpe, 1)
            for o in range(2):
                for c in range(2):
                    mm(bank[0][:, NV + o:NV + 1 + o], raw["WkA"][:, c, o * P:(o + 1) * P], col("L0_xattn_bq", c), start=c == 0, stop=c == 1)
                for c in range(2):
                    i = mm(bank[0][:, NV + 2 + o:NV + 3 + o], cxT[:, c, o * P:(o + 1) * P], col("L1_xattn_bq", c), start=c == 0, stop=c == 1)
            i.then_inc(s_setpe, 1)
            for c in range(2):
                i = mm(bank[1][:, 0:1], col("L1_xattn_bq", c).broadcast_to([P, P]), col("L1_xattn_bk", c), start=c == 0, stop=c == 1)
            i.then_inc(s_setpe, 1)
            for c in range(2):
                i = mm(bank[2][:, 0:D], col("L0_xattn_bv", c).broadcast_to([P, P]), nT[:, c, :], start=c == 0, stop=c == 1)
            i.then_inc(s_setpe, 1)
            for c in range(2):
                i = mm(bank[3][:, 0:D], col("L1_xattn_bk", c).broadcast_to([P, P]), qT[:, c, :], start=c == 0, stop=c == 1)
            i.then_inc(s_setpe, 1)
            t.wait_ge(s_set, NSET)
            for events in pe.values():
                events.start(t)

            def heads(part, before, s, h, b):
                V, K, Q, per = VA[h.width], KM[h.width], QS[h.width], h.width + 1
                base = {n: now(t, b * v) for n, v in dict(scored=h.slots * h.units, head=h.heads, slot=h.slots, group=h.groups).items()}
                for i, p in product_of(range(h.slots + 3), range(h.pairs)):
                    if (i, p) == (0, 0):
                        wait(t, act, before, b, "mask0")
                        t.wait_ge(s_stack[s, "q"], b * STACKED + STACKED)
                        t.wait_ge(s_rests[s, "q"], b * RESTED + RESTED)
                    if (i, p) == (h.slots // 2, 0):
                        wait(t, act, before, b, "mask1")
                    if i < h.slots:
                        for u in range(2 * p, 2 * p + 2):
                            r, pair = divmod(u, h.pairs)
                            n = i * h.units + u
                            if n >= 2:
                                t.wait_ge(h.maxed, base["scored"] + (n - 1))
                            mm(halves(n % 2), Q[0:MROW, i, r * P:(r + 1) * P], K[0:MROW, i, 2 * pair:2 * pair + 2, :], start=True, stop=True).then_inc(h.scored, 1)
                    if 1 <= i <= h.slots and p == 0:
                        t.wait_ge(h.parted, base["slot"] + i)
                        if i >= 2:
                            t.wait_ge(h.rows, base["slot"] + (i - 1))
                        for r in range(2):
                            x = t.transpose(bank[5][:, r * P:(r + 1) * P], MT[:, (i - 1) % 2, r, :], ident)
                        x.then_inc(h.turned, 1)
                    if 2 <= i <= h.slots + 1:
                        slot = i - 2
                        if p == 0:
                            t.wait_ge(h.rows, base["slot"] + (slot + 1))
                        for j in range(2 * p, 2 * p + 2):
                            n = slot * h.nh + j
                            if n >= 2:
                                t.wait_ge(h.exp, base["head"] + (n - 1))
                            for kc in range(2):
                                x = mm(halves(2 + n % 2)[:, kc, :], K[:, slot, j, kc * P:(kc + 1) * P], Q[:, slot, :], start=True, stop=True)
                            x.then_inc(h.st, 1)
                    if i >= 3 and p == h.pairs - 1 and (i - 2) * h.nh % 4 == 0:
                        grp = (i - 2) * h.nh // 4 - 1
                        t.wait_ge(h.exp, base["head"] + 4 * (grp + 1))
                        if grp:
                            t.wait_ge(h.os, base["group"] + grp)
                        for kc in range(2):
                            for j in range(4):
                                n = 4 * grp + j
                                x = mm(bank[4][SLOT * j:SLOT * (j + 1), 0:D], V[:, kc, n * per:n * per + SLOT], PT[:, n % 8, kc, :],
                                       start=kc == 0, stop=kc == 1, tile_position=(0, SLOT * j))
                        x.then_inc(h.pv, 1)
                    yield
                for q in range(h.groups // 2):
                    half, r = divmod(q, 2)
                    if q == 0:
                        t.wait_ge(h.os, base["group"] + h.groups)
                    if q >= 2:
                        wait(t, dve, part, b, f"os{q - 2}")
                    for k in range(4):
                        x = t.transpose(bank[q % 2][:, k * P:(k + 1) * P], OS[:, 4 * half + k, r * P:(r + 1) * P], ident)
                    x.then_inc(*pe[part].tick(f"os{q}"))
                    if q == h.groups // 2 - 1:
                        wait(t, dve, part, b, f"os{q}")
                    yield

            def lin1(b):
                yield from idle(2)
                if isinstance(b, int) and b < 2:
                    if b:
                        wait(t, dve, "B1", 0, "v")
                else:
                    wait(t, dve, "D1", b - 2, "v")
                E = pe["A"]
                wait(t, dve, "A", b, "n")
                turn(6, N).then_inc(*E.tick("nT"))
                t.wait_ge(s_cxA, b * 16 + 16)
                turn(7, CX).then_inc(*E.tick("cxT"))
                yield
                wait(t, act, "A", b, "nT")
                product(6, MA, nT).then_inc(*E.tick("qT"))
                yield
                wait(t, act, "A", b, "qT")
                wait(t, dve, "A", b, "cxT")
                product(7, qT, cxT).then_inc(*E.tick("s"))
                yield
                wait(t, act, "A", b, "exp")
                turn(6, PR).then_inc(*E.tick("pT"))
                yield
                wait(t, dve, "A", b, "pT")
                product(7, CX, pT).then_inc(*E.tick("cT"))
                yield
                wait(t, act, "A", b, "cT")
                product(6, cT, WA).then_inc(*E.tick("o"))
                yield
                yield
                E = pe["B1"]
                wait(t, dve, "B1", b, "n")
                turn(7, N).then_inc(*E.tick("nT"))
                yield
                wait(t, act, "B1", b, "zT")
                product(7, wB["wk"], zT).then_inc(*E.tick("k"))
                product(6, wB["wq"], zT).then_inc(*E.tick("q"))
                yield
                wait(t, dve, "B1", b, "ql")
                product(6, zT, wB["wv"]).then_inc(*E.tick("v"))
                yield

            def lin2(b, more):
                E = pe["B2"]
                if isinstance(b, int) and b == 0:
                    wait(t, dve, "B1", 1, "v")
                elif final(b):
                    wait(t, dve, "D1", b - 1, "v")
                else:
                    wait(t, dve, "D2", b - 1, "lg")
                turn(6, AO[8]).then_inc(*E.tick("aoT"))
                yield
                wait(t, dve, "B2", b, "aoT")
                product(7, AOT, wB["wo"]).then_inc(*E.tick("wo"))
                yield
                wait(t, dve, "B2", b, "xf")
                turn(6, XF).then_inc(*E.tick("xfT"))
                yield
                wait(t, dve, "B2", b, "xfT")
                t.wait_ge(s_w, b * 48 + 48)
                for k in range(4):
                    if k >= 2:
                        wait(t, act, "B2", b, f"f{k - 2}")
                    product(7 - k % 2, W1[:, :, 2 * k * P:], XFT).then_inc(*E.tick(f"f{k}"))
                    if k % 2:
                        yield
                wait(t, act, "B2", b, "f3")
                if final(b):
                    wait(t, dve, "D2", b - 1, "lg")
                for r in range(2):
                    for f in range(FC):
                        x = mm(halves(7)[:, r, :], HT[:, f, r * P:(r + 1) * P], W2[:, f, :], start=f == 0, stop=f == FC - 1)
                    if r == 0:
                        yield
                x.then_inc(*E.tick("y"))
                yield
                yield

                E = pe["C"]
                wait(t, dve, "C", b, "n")
                turn(6, N).then_inc(*E.tick("nT"))
                t.wait_ge(s_cxC, b * 16 + 16)
                turn(7, CX).then_inc(*E.tick("cxT"))
                yield
                wait(t, act, "C", b, "nT")
                product(6, MC, nT).then_inc(*E.tick("qT"))
                yield
                wait(t, pool, "C", b, "prT")
                wait(t, dve, "C", b, "cxT")
                for r in range(2):
                    for c in range(2):
                        x = mm(bank[7][:, r:r + 1], prT[:, c, r * P:(r + 1) * P], ones[:, 0:1], start=c == 0, stop=c == 1)
                x.then_inc(*E.tick("self"))
                product(6, qT, cxT).then_inc(*E.tick("s"))
                yield
                wait(t, act, "C", b, "pn")
                turn(7, PR).then_inc(*E.tick("pT"))
                yield
                wait(t, dve, "C", b, "pT")
                for o in range(2):
                    for c in range(2):
                        mm(halves(6)[:, o, :], CX[:, c, o * P:(o + 1) * P], pT[:, c, :], start=c == 0, stop=False)
                    for r in range(2):
                        x = mm(halves(6)[:, o, r * P:(r + 1) * P], N[:, r, o * P:(o + 1) * P], diag[:, r, :], start=False, stop=r == 1)
                x.then_inc(*E.tick("cT"))
                yield
                wait(t, act, "C", b, "cT")
                product(7, cT, WvC).then_inc(*E.tick("o"))
                yield
                yield

                E = pe["D1"]
                wait(t, dve, "D1", b, "n")
                turn(6, N).then_inc(*E.tick("nT"))
                yield
                wait(t, act, "D1", b, "zT")
                product(6, wD["wk"], zT).then_inc(*E.tick("k"))
                product(7, wD["wq"], zT).then_inc(*E.tick("q"))
                yield
                wait(t, dve, "D1", b, "ql")
                product(7, zT, wD["wv"]).then_inc(*E.tick("v"))
                yield

            def post(b, last):
                E = pe["D2"]
                if last and final(b + 1):
                    wait(t, act, "B2", b + 1, "f3")
                elif last:
                    wait(t, dve, "D1", b, "v")
                else:
                    wait(t, dve, "B1", b + 2, "v")
                turn(6, AO[16]).then_inc(*E.tick("aoT"))
                yield
                wait(t, dve, "D2", b, "aoT")
                product(7, AOTD, wD["wo"]).then_inc(*E.tick("wo"))
                yield
                yield
                wait(t, dve, "D2", b, "n")
                turn(6, N).then_inc(*E.tick("nT"))
                yield
                wait(t, dve, "D2", b, "h2T")
                for r in range(2):
                    for c in range(2):
                        x = mm(bank[7][:, r * NE:(r + 1) * NE], H2T[:, c, r * P:(r + 1) * P], wr[:, c, :], start=c == 0, stop=c == 1)
                x.then_inc(*E.tick("lg"))
                yield

            schedule(t.Fori, B, lin1, lin2, post, lambda b: heads("HB", "B1", "B", h0, b), lambda b: heads("HD", "D1", "D", h1, b), lambda b: None, lambda b: None)

        @block.vector
        def _(v):
            v.wait_ge(s_load, NLOAD)
            v.wait_ge(s_cst, 2)
            for w in VA:
                v.memset(VA[w][:, :, 0:D // w * (w + 1)].rearrange("p k (h d) -> p k h d", d=w + 1)[:, :, :, w:w + 1], 1.0)
                nh = SLOT // w
                for slot in range(8):
                    v.tensor_copy(KM[w][MROW:P, slot, :, :], cst[MROW:P, C_SEL:C_SEL + nh].unsqueeze(2).broadcast_to([SLOT, nh, D]))
            v.wait_ge(s_setpe, 1)
            v.tensor_copy(cols[:, :], bank[0][:, 0:NV])
            v.tensor_copy(b1T[:, :, :].rearrange("p b f -> p (b f)"), bank[1][:, 0:P]).then_inc(s_set, 1)
            for n, (dst, b) in enumerate(((nT, 2), (qT, 3), (cxT, 4))):
                v.wait_ge(s_setpe, 2 + n)
                v.tensor_copy(dst[:, :, :], halves(b)).then_inc(s_set, 1)
            for n, (dst, b) in enumerate(((MA, 5), (WA, 6), (MC, 7))):
                v.wait_ge(s_setpe, 5 + n)
                v.tensor_copy(dst[:, :, :], halves(b)).then_inc(s_set, 1)
            v.wait_ge(s_setpe, 8)
            v.tensor_copy(qkbias[:, :], bank[0][:, NV:NV + 4]).then_inc(s_set, 1)
            v.wait_ge(s_setpe, 9)
            v.tensor_copy(bqbk[:, :], bank[1][:, 0:1]).then_inc(s_set, 1)
            v.wait_ge(s_setpe, 10)
            v.tensor_tensor(rowA[:, 0, :], bank[2][:, 0:D], rowA[:, 0, :], ALU.add).then_inc(s_set, 1)
            v.wait_ge(s_setpe, 11)
            v.tensor_copy(rowu[:, 0, :], bank[3][:, 0:D]).then_inc(s_set, 1)
            v.wait_ge(s_set, NSET)
            for events in dve.values():
                events.start(v)

            def moments(part, X, b):
                E = dve[part]
                for r in range(2):
                    x = v.bn_stats(bn[:, r, :], X[:, r, :])
                x.then_inc(*E.tick("bn"))
                wait_first(v, (s_cst, 2), E.sem, E.at(b, "bn"))
                for r in range(2):
                    x = v.bn_aggr(mv[:, r, :], bn[:, r, :])
                x.then_inc(*E.tick("mv"))
                wait(v, dve, part, b, "mv")
                v.tensor_scalar(uw[:, 0:2], mv[:, :, 1], EPS, None, ALU.add)
                v.tensor_scalar(uw[:, 2:4], mv[:, :, 1], 1.0 + EPS, EPS * EPS, ALU.mult, ALU.add).then_inc(*E.tick("uw"))

            def norm(dst, X, k):
                for r in range(2):
                    x = v.tensor_scalar(dst[:, r, :], X[:, r, :], mv[:, r, 0:1], rr[:, k + r:k + r + 1], ALU.subtract, ALU.mult)
                return x

            def take(part, bnk, dst, b, name):
                wait(v, pe, part, b, name)
                v.tensor_copy(dst[:, :, :], halves(bnk)).then_inc(*dve[part].tick(name))

            def rests(part, b, qbank, kbank, bias):
                for n, bnk, head, rest, name in (("k", kbank, KH, KL, "L1_ffn_bk"), ("q", qbank, QH, QL, "L1_ffn_bq")):
                    wait(v, act, part, b, n + "h")
                    if bias:
                        for c in range(2):
                            x = v.scalar_tensor_tensor(rest[:, c, :], halves(bnk)[:, c, :], col(name, c), head[:, c, :].bitcast(F32), ALU.add, ALU.subtract)
                    else:
                        x = v.tensor_tensor(rest, halves(bnk), head.bitcast(F32), ALU.subtract)
                    x.then_inc(*dve[part].tick(n + "l"))

            def values(part, b, w, bnk, bias):
                wait(v, pe, part, b, "v")
                for r in range(2):
                    dst = VA[w][:, r, 0:D // w * (w + 1)].rearrange("p (h d) -> p h d", d=w + 1)[:, :, 0:w]
                    src = halves(bnk)[:, r, :].rearrange("p (h d) -> p h d", d=w)
                    if bias:
                        x = v.tensor_tensor(dst, src, rowbvD[:, 0, :].rearrange("p (h d) -> p h d", d=w), ALU.add)
                    else:
                        x = v.tensor_copy(dst, src)
                x.then_inc(*dve[part].tick("v"))

            def heads(part, h, b):
                E, Q = dve[part], QS[h.width]
                base = {n: now(v, b * k) for n, k in dict(scored=h.slots * h.units, slot=h.slots).items()}
                for i, p in product_of(range(h.slots + 3), range(h.pairs)):
                    if i < h.slots:
                        for u in range(2 * p, 2 * p + 2):
                            r, pair = divmod(u, h.pairs)
                            n = i * h.units + u
                            v.wait_ge(h.scored, base["scored"] + (n + 1))
                            v.tensor_reduce(MX[:, i % 2, r, 2 * pair:2 * pair + 2], halves(n % 2), AX, ALU.max).then_inc(h.maxed, 1)
                    if 1 <= i <= h.slots and p == 0:
                        v.wait_ge(h.turned, base["slot"] + i)
                        v.tensor_copy(Q[MROW:P, i - 1, :], bank[5][MROW:P, 0:D]).then_inc(h.rows, 1)
                    if i < h.slots and p == h.pairs - 1:
                        v.wait_ge(h.maxed, base["scored"] + (i + 1) * h.units)
                        v.tensor_scalar(MH[:, i % 2, :, 0:h.nh], MX[:, i % 2, :, 0:h.nh], -1.0, None, ALU.mult).then_inc(h.negated, 1)
                        v.wait_ge(h.negated, base["slot"] + (i + 1))
                        if i >= 2:
                            v.wait_ge(h.turned, base["slot"] + (i - 1))
                        v.tensor_copy(MT[:, i % 2, :, MROW:MROW + h.nh], MH[:, i % 2, :, 0:h.nh].bitcast(F32))
                        v.scalar_tensor_tensor(MT[:, i % 2, :, MROW + 4:MROW + 4 + h.nh], MX[:, i % 2, :, 0:h.nh], -1.0,
                                               MH[:, i % 2, :, 0:h.nh].bitcast(F32), ALU.mult, ALU.subtract).then_inc(h.parted, 1)
                    yield
                per = 16 * h.width
                for q in range(h.groups // 2):
                    half, r = divmod(q, 2)
                    ps = bank[q % 2][:, :].rearrange("p (g j d) -> p g j d", g=4, j=4)
                    wait(v, pe, part, b, f"os{q}")
                    v.reciprocal(rh[:, q, :, :], ps[:, :, :, h.width]).then_inc(*E.tick(f"rh{q}"))
                    wait(v, dve, part, b, f"rh{q}")
                    v.tensor_tensor(AO[h.width][:, r, half * per:(half + 1) * per].rearrange("p (g j d) -> p g j d", g=4, j=4), ps[:, :, :, 0:h.width],
                                    rh[:, q, :, :].unsqueeze(3).broadcast_to([P, 4, 4, h.width]), ALU.mult).then_inc(*E.tick(f"os{q}"))
                    yield

            def lin1(b):
                E = dve["A"]
                v.wait_ge(s_x, b * 16 + 16)
                moments("A", X0, b)
                yield
                wait(v, pool, "A", b, "r")
                norm(N, X0, 0).then_inc(*E.tick("n"))
                yield
                take("A", 7, cxT, b, "cxT")
                yield
                yield
                wait(v, pe, "A", b, "s")
                v.tensor_reduce(st[:, 0:2], halves(7), AX, ALU.max).then_inc(*E.tick("max"))
                wait(v, dve, "A", b, "max")
                v.tensor_scalar(st[:, 2:4], st[:, 0:2], -float(D) ** -0.5, None, ALU.mult).then_inc(*E.tick("nb"))
                yield
                take("A", 6, pT, b, "pT")
                v.reciprocal(st[:, 6:8], st[:, 4:6]).then_inc(*E.tick("rs"))
                yield
                yield
                v.wait_ge(pool["HB"].sem, pool["HB"].before(b))
                wait(v, pe, "A", b, "o")
                wait(v, pool, "A", b, "xb")
                wait(v, dve, "A", b, "rs")
                for r in range(2):
                    x = v.scalar_tensor_tensor(X1[:, r, :], halves(6)[:, r, :], st[:, 6 + r:7 + r], XB[:, r, :], ALU.mult, ALU.add)
                x.then_inc(*E.tick("x"))
                wait(v, dve, "A", b, "x")
                moments("B1", X1, b)
                yield
                E = dve["B1"]
                wait(v, pool, "B1", b, "r")
                norm(Y, X1, 0).then_inc(*E.tick("y"))
                norm(N, X1, 2).then_inc(*E.tick("n"))
                yield
                yield
                rests("B1", b, 6, 7, False)
                yield
                values("B1", b, 8, 6, False)
                yield

            def lin2(b, more):
                E = dve["B2"]
                take("B2", 6, AOT, b, "aoT")
                yield
                wait(v, pe, "B2", b, "wo")
                wait(v, pool, "HB", b, "y")
                v.wait_ge(pool["D2"].sem, pool["D2"].before(b - 1 if final(b) else b))
                v.tensor_tensor(XF[:, :, :], halves(7), Yc[:, :, :], ALU.add).then_inc(*E.tick("xf"))
                yield
                take("B2", 6, XFT, b, "xfT")
                yield
                yield from idle(3)
                wait(v, pe, "B2", b, "y")
                wait(v, pool, "B2", b, "xb")
                v.tensor_tensor(X2[:, :, :], halves(7), XB[:, :, :], ALU.add).then_inc(*E.tick("x"))
                wait(v, dve, "B2", b, "x")
                moments("C", X2, b)
                yield

                E = dve["C"]
                wait(v, pool, "C", b, "r")
                norm(N, X2, 0).then_inc(*E.tick("n"))
                yield
                take("C", 7, cxT, b, "cxT")
                yield
                wait(v, dve, "C", b, "n")
                for r in range(2):
                    x = v.tensor_tensor_reduce(out=PR[:, r, :], in0=N[:, r, :], in1=rowu[:, 0, :], scale=1.0, scalar=0.0,
                                               op0=ALU.mult, op1=ALU.add, accum_out=st[:, 10 + r:11 + r])
                x.then_inc(*E.tick("c0"))
                wait(v, dve, "C", b, "c0")
                v.tensor_scalar(st[:, 10:12], st[:, 10:12], bqbk[:, 0:1], None, ALU.add).then_inc(*E.tick("c"))
                yield
                wait(v, pe, "C", b, "s")
                v.tensor_reduce(st[:, 0:2], halves(6), AX, ALU.max).then_inc(*E.tick("max"))
                wait(v, dve, "C", b, "max")
                v.tensor_tensor(st[:, 12:14], bank[7][:, 0:2], st[:, 0:2], ALU.max).then_inc(*E.tick("mxs"))
                wait(v, dve, "C", b, "mxs")
                v.tensor_tensor(st[:, 12:14], st[:, 12:14], st[:, 10:12], ALU.add).then_inc(*E.tick("mxc"))
                wait(v, dve, "C", b, "mxc")
                v.tensor_tensor(st[:, 2:4], st[:, 10:12], st[:, 12:14], ALU.subtract).then_inc(*E.tick("nb"))
                yield
                wait(v, act, "C", b, "pn")
                v.tensor_tensor(st[:, 14:16], st[:, 4:6], st[:, 8:10], ALU.add).then_inc(*E.tick("z"))
                wait(v, dve, "C", b, "z")
                v.reciprocal(st[:, 6:8], st[:, 14:16]).then_inc(*E.tick("rs"))
                for r in range(2):
                    x = v.tensor_scalar(diag[:, r, :], ident, st[:, 8 + r:9 + r], None, ALU.mult)
                x.then_inc(*E.tick("diag"))
                take("C", 7, pT, b, "pT")
                yield
                yield
                v.wait_ge(pool["D2"].sem, pool["D2"].before(b))
                wait(v, pe, "C", b, "o")
                wait(v, pool, "C", b, "xb")
                wait(v, dve, "C", b, "rs")
                for r in range(2):
                    x = v.scalar_tensor_tensor(X3[:, r, :], halves(7)[:, r, :], st[:, 6 + r:7 + r], XB[:, r, :], ALU.mult, ALU.add)
                x.then_inc(*E.tick("x"))
                wait(v, dve, "C", b, "x")
                moments("D1", X3, b)
                yield

                E = dve["D1"]
                wait(v, pool, "D1", b, "r")
                norm(YD, X3, 0).then_inc(*E.tick("y"))
                norm(N, X3, 2).then_inc(*E.tick("n"))
                yield
                yield
                rests("D1", b, 7, 6, True)
                yield
                values("D1", b, 16, 7, True)
                yield

            def post(b, last):
                E = dve["D2"]
                take("D2", 6, AOTD, b, "aoT")
                yield
                wait(v, pe, "D2", b, "wo")
                wait(v, pool, "D1", b, "yb")
                v.tensor_tensor(XP[:, :, :], halves(7), YB[:, :, :], ALU.add).then_inc(*E.tick("xp"))
                wait(v, dve, "D2", b, "xp")
                moments("D2", XP, b)
                yield
                wait(v, pool, "D2", b, "r")
                norm(N, XP, 0).then_inc(*E.tick("n"))
                yield
                wait(v, pe, "D2", b, "nT")
                for c in range(2):
                    x = v.tensor_scalar(H2T[:, c, :], halves(6)[:, c, :], col("L1_ffn_ln2_g", c), col("L1_ffn_ln2_b", c), ALU.mult, ALU.add)
                x.then_inc(*E.tick("h2T"))
                yield
                wait(v, pe, "D2", b, "lg")
                v.tensor_copy(logits[:, bass.ts(b, 2), :], bank[7][:, 0:2 * NE].rearrange("p (t e) -> p t e", t=2)).then_inc(*E.tick("lg"))
                yield

            schedule(v.Fori, B, lin1, lin2, post, lambda b: heads("HB", h0, b), lambda b: heads("HD", h1, b), lambda b: None, lambda b: None)

        @block.scalar
        def _(s_):
            s_.wait_ge(s_set, NSET)
            for events in act.values():
                events.start(s_)

            def take(part, bnk, dst, b, name, tick=None):
                wait(s_, pe, part, b, name)
                s_.activation(dst[:, :, :], halves(bnk), ACT.Copy).then_inc(*act[part].tick(tick or name))

            def take_cols(part, bnk, dst, b, name, tick, scale=None, bias=None):
                wait(s_, pe, part, b, name)
                for c in range(2):
                    kw = {} if scale is None else {"scale": col(scale, c)}
                    x = s_.activation(dst[:, c, :], halves(bnk)[:, c, :], ACT.Identity, bias=bias(c), **kw)
                x.then_inc(*act[part].tick(tick))

            def masks(part, s, w, b):
                s_.wait_ge(s_stack[s, "k"], b * STACKED + STACKED)
                s_.wait_ge(s_rests[s, "k"], b * RESTED + RESTED)
                for half in range(2):
                    for j in range(SLOT // w):
                        x = s_.activation(KM[w][0:MROW, 4 * half:4 * half + 4, j, :], KSs[0:MROW, 4 * half:4 * half + 4, :], ACT.Copy,
                                          scale=cst[0:MROW, C_MASK[w] + j:C_MASK[w] + j + 1])
                    x.then_inc(*act[part].tick(f"mask{half}"))

            def heads(n_steps, h, b):
                base = {n: now(s_, b * k) for n, k in dict(head=h.heads, group=h.groups).items()}

                def outputs(grp):
                    s_.wait_ge(h.pv, base["group"] + (grp + 1))
                    s_.activation(OS[:, grp, :], bank[4][:, 0:D], ACT.Copy).then_inc(h.os, 1)

                for i, p in product_of(range(h.slots + 3), range(h.pairs)):
                    for j in range(2 * p, 2 * p + 2) if 2 <= i <= h.slots + 1 else ():
                        n = (i - 2) * h.nh + j
                        s_.wait_ge(h.st, base["head"] + (n + 1))
                        if n >= 8:
                            s_.wait_ge(h.pv, base["group"] + (n // 4 - 1))
                        s_.activation(PT[:, n % 8, :, :], halves(2 + n % 2), ACT.Exp, scale=h.scale).then_inc(h.exp, 1)
                    if i >= 3 and p == h.pairs - 1 and (i - 2) * h.nh % 4 == 0:
                        outputs((i - 2) * h.nh // 4 - 1)
                    yield
                yield from idle(n_steps - (h.slots + 3) * h.pairs)

            def lin1(b):
                yield from idle(2)
                take("A", 6, nT, b, "nT")
                yield
                take_cols("A", 6, qT, b, "qT", "qT", bias=lambda c: qkbias[:, c:c + 1])
                yield
                wait(s_, dve, "A", b, "nb")
                for r in range(2):
                    x = s_.activation(PR[:, r, :], halves(7)[:, r, :], ACT.Exp, bias=st[:, 2 + r:3 + r], scale=float(D) ** -0.5, accum_out=st[:, 4 + r:5 + r])
                x.then_inc(*act["A"].tick("exp"))
                yield
                yield
                take("A", 7, cT, b, "cT")
                yield
                yield from idle(2)
                take_cols("B1", 7, zT, b, "nT", "zT", "L0_ffn_ln_g", lambda c: col("L0_ffn_ln_b", c))
                yield
                take("B1", 7, KH, b, "k", "kh")
                take("B1", 6, QH, b, "q", "qh")
                yield
                yield

            def lin2(b, more):
                yield from idle(3)
                for k in range(4):
                    for f in (2 * k, 2 * k + 1):
                        if f % 2 == 0:
                            wait_first(s_, (s_set, NSET), pe["B2"].sem, pe["B2"].at(b, f"f{k}"))
                        x = s_.activation(HT[:, f, :], halves(7 - k % 2)[:, f % 2, :], ACT.Gelu, bias=b1T[:, bass.ts(b, 1), f])
                    x.then_inc(*act["B2"].tick(f"f{k}"))
                    if k % 2:
                        yield
                yield from idle(3)
                take("C", 6, nT, b, "nT")
                yield
                take_cols("C", 6, qT, b, "qT", "qT", bias=lambda c: qkbias[:, 2 + c:3 + c])
                yield
                wait(s_, dve, "C", b, "nb")
                for r in range(2):
                    x = s_.activation(PR[:, r, :], halves(6)[:, r, :], ACT.Exp, bias=st[:, 2 + r:3 + r], accum_out=st[:, 4 + r:5 + r])
                x.then_inc(*act["C"].tick("exp"))
                for r in range(2):
                    x = s_.activation(st[:, 8 + r:9 + r], bank[7][:, r:r + 1], ACT.Exp, bias=st[:, 2 + r:3 + r])
                x.then_inc(*act["C"].tick("pn"))
                yield
                yield
                take("C", 6, cT, b, "cT")
                yield
                yield from idle(2)
                take_cols("D1", 6, zT, b, "nT", "zT", "L1_ffn_ln1_g", lambda c: col("L1_ffn_ln1_b", c))
                yield
                take_cols("D1", 6, KH, b, "k", "kh", bias=lambda c: col("L1_ffn_bk", c))
                take_cols("D1", 7, QH, b, "q", "qh", bias=lambda c: col("L1_ffn_bq", c))
                yield
                yield

            schedule(s_.Fori, B, lin1, lin2, lambda b, last: idle(POST), lambda b: heads(HEADS_B, h0, b), lambda b: heads(HEADS_D, h1, b),
                     lambda b: masks("B1", "B", 8, b), lambda b: masks("D1", "D", 16, b))


def experts(nc, a, out, scratch, sem, ident, ones, cst, logits, bank):
    B, S, D = a["x"].shape
    T = B * S
    NE, _, FD = a["L1_ffn_w1"].shape
    NT, DC, FC = T // P, D // P, FD // P
    CAP = -(-T // 4)
    GAIN = 1.0 - 0.2
    HALF = 512
    HT4 = HALF // P
    NH = CAP // HALF
    assert NH == 2

    w1_d = a["L1_ffn_w1"].rearrange("e (c p) f -> e p c f", p=P)
    w2_d = a["L1_ffn_w2"].rearrange("e (f p) d -> e p f d", p=P)
    tok_d = scratch["tokens"].rearrange("(n p) d -> n p d", p=P)
    slots_d = scratch["slots"].rearrange("(e h r p) d -> (e h) p r d", h=NH, r=HT4, p=P)

    with ExitStack() as stack:
        def sb(name, shape, dt=F32):
            return stack.enter_context(nc.sbuf_tensor(name, shape, dt))

        def table(name):
            return sb(name, [P, NT, NE])

        pr, eq, key, m1, m2, l2, cum, tot, run, loc1, loc2, keep = (
            table(n) for n in ("pr", "eq", "key", "m1", "m2", "l2", "cum", "tot", "run", "loc1", "loc2", "keep"))
        mx, zs, kx, kx1, t1, t2, den, f1, f2, g1, g2, w = (
            sb(n, [P, NT]) for n in ("mx", "zs", "kx", "kx1", "t1", "t2", "den", "f1", "f2", "g1", "g2", "wv"))
        put1, put2 = (sb(n, [P, NT], I32) for n in ("put1", "put2"))
        pay = sb("pay", [P, NT, ROW - D])
        RING = 8
        tk = sb("tk", [P, RING, ROW])
        W1 = [sb(f"W1_{i}", [P, DC, FD]) for i in range(2)]
        W2 = [sb(f"W2_{i}", [P, FC, D]) for i in range(2)]
        B2 = sb("B2_all", [P, NE, D])
        W1S = [[sb(f"W1{x}{i}", [P, DC, FD], F32R) for x in "hl"] for i in range(2)]
        W2S = [[sb(f"W2{x}{i}", [P, FC, D], F32R) for x in "hl"] for i in range(2)]
        b1rows, b1T = sb("b1rows2", [NE * FC, P]), sb("b1T2", [P, NE, FC])
        xg = [sb(f"xg{i}", [P, HT4, ROW]) for i in range(2)]
        xgT = [[sb(f"xgT{x}{i}", [P, DC, HALF], F32R) for x in "hl"] for i in range(2)]
        hT = [sb(f"hT{x}", [P, FC, HALF], F32R) for x in "hl"]
        hid = sb("hid", [P, 4, HALF])
        yo = [sb(f"yo{i}", [P, HT4, D]) for i in range(2)]
        where = [sb(f"where{i}", [P, HT4]) for i in range(2)]
        rows_ = [sb(f"rows{i}", [P, HT4], I32) for i in range(2)]
        gate = [sb(f"gate{i}", [P, HT4]) for i in range(2)]

        s_ld, s_tk, s_pay = sem("s_ld"), [sem(f"s_tk{i}") for i in range(RING)], sem("s_pay")
        s_d, s_ex, s_cum, s_bt = sem("s_d"), sem("s_ex"), sem("s_cum"), sem("s_bt")
        s_routed, s_sc = sem("s_routed"), [sem(f"s_sc{i}") for i in range(RING)]
        s_w = [sem(f"s_w{i}") for i in range(2)]
        s_xg = [sem(f"s_xg{i}") for i in range(2)]
        s_xt, s_xh, s_xl, s_h, s_hh, s_hid, s_hl, s_y, s_yv = (
            sem(n) for n in ("s_xt", "s_xh", "s_xl", "s_h", "s_hh", "s_hid", "s_hl", "s_y", "s_yv"))
        s_wh, s_wl = ([sem(f"{n}{i}") for i in range(2)] for n in ("s_wh", "s_wl"))
        s_meta, s_yb, s_add, s_added, s_a1 = sem("s_meta"), sem("s_yb"), sem("s_add"), sem("s_added"), sem("s_a1")
        block = stack.enter_context(nc.Block())
        HB = (2, 3, 6, 7)
        PIECES = 4
        TERMS = ((0, 0), (0, 1), (1, 0))

        def pieces(i):
            for W, parts in ((W1[i], W1S[i]), (W2[i], W2S[i])):
                n = W.shape[1] // 2
                for k in range(2):
                    yield [x[:, k * n:(k + 1) * n, :] for x in (W, *parts)]

        def load_weights(sp, i, e):
            sp.dma_start(W1[i][:, :, :], w1_d[e]).then_inc(s_w[i], 16)
            sp.dma_start(W2[i][:, :, :], w2_d[e]).then_inc(s_w[i], 16)

        @block.sync
        def _(sp):
            sp.dma_start(b1rows[:, :], a["L1_ffn_b1"].rearrange("e (f p) -> (e f) p", p=P)).then_inc(s_ld, 16)
            for e in range(NE):
                sp.dma_start(B2[:, e, :], a["L1_ffn_b2"][e].partition_broadcast(P)).then_inc(s_ld, 16)
            load_weights(sp, 0, 0)
            load_weights(sp, 1, 1)
            for n in range(NT):
                if n >= RING:
                    sp.wait_ge(s_sc[n % RING], 32 * (n // RING))
                sp.dma_start(tk[:, n % RING, 0:D], tok_d[n]).then_inc(s_tk[n % RING], 16)
            for i in range(RING):
                sp.wait_ge(s_sc[i], 32 * (NT // RING))
            for i in range(2):
                sp.dma_start(xg[i][:, :, :], slots_d[i]).then_inc(s_xg[i], 16)
            sp.wait_ge(s_wh[0], PIECES)
            sp.wait_ge(s_wl[0], PIECES)
            load_weights(sp, 0, 2)
            with sp.Fori(0, NE // 2) as k:
                ahead = [now(sp, (k * 4 + j + 2) % (NE * NH)) for j in range(4)]
                turned = [now(sp, 1 + (k * 4 + (j + 1))) for j in range(4)]
                known = [now(sp, (k * 4 + (j + 1)) * 3) for j in range(4)]
                split = [now(sp, (k + 1) * PIECES), now(sp, (k + 2) * PIECES)]
                nxt = [now(sp, (k * 2 + 3 + i) % NE) for i in range(2)]
                for j in range(4):
                    sp.wait_ge(s_xt, turned[j])
                    sp.wait_ge(s_meta, known[j])
                    sp.dma_start(xg[j % 2][:, :, :], slots_d[ahead[j]]).then_inc(s_xg[j % 2], 16)
                    if j % 2 == 0:
                        i = 1 - j // 2
                        sp.wait_ge(s_wh[i], split[j // 2])
                        sp.wait_ge(s_wl[i], split[j // 2])
                        load_weights(sp, i, nxt[j // 2])
            for i in range(2):
                sp.wait_ge(s_w[i], 32 * (NE // 2 + 2 - i))
                sp.wait_ge(s_xg[i], 16 * (NE + 1))
            sp.wait_ge(s_add, 16 + 16 * NE * NH * HT4)

        @block.gpsimd
        def _(g):
            g.dma_start(out[T:T + P, :], cst[:, 0:D]).then_inc(s_add, 16)
            g.wait_ge(s_routed, 1)
            for n in range(NT):
                g.wait_ge(s_tk[n % RING], 16 * (n // RING + 1))
                g.wait_ge(s_pay, n + 1)
                for put in (put1, put2):
                    g.indirect_dma_start(out=scratch["slots"], out_offset=bass.IndirectOffsetOnAxis(ap=put[:, n:n + 1], axis=0),
                                         in_=tk[:, n % RING, :], in_offset=None,
                                         bounds_check=NE * CAP - 1, oob_is_err=False).then_inc(s_sc[n % RING], 16)
            g.sem_inc(s_added, 1)
            with g.Fori(0, NE // 2) as k:
                for j in range(4):
                    for r in range(HT4):
                        n = (k * 4 + j) * HT4 + r
                        before = now(g, n * 16 + 16)
                        wait_first(g, (s_routed, 1), s_yv, 1 + (n + 1))
                        g.wait_ge(s_add, before)
                        if r == 0:
                            g.sem_inc(s_added, 1)
                        g.indirect_dma_start(out=out, out_offset=bass.IndirectOffsetOnAxis(ap=rows_[j % 2][:, r:r + 1], axis=0),
                                             in_=yo[j % 2][:, r, :], in_offset=None,
                                             bounds_check=T + P - 1, oob_is_err=True, compute_op=ALU.add).then_inc(s_add, 16)

        @block.tensor
        def _(t):
            mm = t.matmul
            t.wait_ge(s_ld, 16 * (NE + 1))
            t.transpose(bank[7][:, 0:NE * FC], b1rows[:, :], ident[0:NE * FC, 0:NE * FC]).then_inc(s_bt, 1)
            flat = lambda x: x[:, :, :].rearrange("p n e -> p (n e)")
            for i, m in enumerate((m1, m2)):
                t.wait_ge(s_ex, 1 + i)
                mm(bank[2 * i][:, 0:NT * NE], cst[:, C_TRI:C_TRI + P], flat(m), start=True, stop=True)
                mm(bank[2 * i + 1][:, 0:NT * NE], ones, flat(m), start=True, stop=True).then_inc(s_cum, 1)
            t.wait_ge(s_routed, 1)

            t.sem_inc(s_xt, 1)
            t.sem_inc(s_y, 1)

            def turn(i):
                for c in range(DC):
                    for r in range(HT4):
                        x = t.transpose(bank[c][:, r * P:(r + 1) * P], xg[i][:, r, c * P:(c + 1) * P], ident)
                x.then_inc(s_xt, 1)

            t.wait_ge(s_xg[0], 16)
            turn(0)
            with t.Fori(0, NE // 2) as k:
                for j in range(4):
                    u = k * 4 + j
                    i = j // 2
                    t.wait_ge(s_xh, u * DC + DC)
                    t.wait_ge(s_xl, u * DC + DC)
                    t.wait_ge(s_wh[i], k * PIECES + PIECES)
                    t.wait_ge(s_wl[i], k * PIECES + PIECES)
                    for f in range(FC):
                        t.wait_ge(s_hid, u * FC + (f + 1))
                        for n, (p, q) in enumerate(TERMS):
                            for c in range(DC):
                                x = mm(bank[HB[f % 4]][:, :], W1S[i][p][:, c, f * P:(f + 1) * P], xgT[j % 2][q][:, c, :],
                                       start=(n, c) == (0, 0), stop=(n, c) == (len(TERMS) - 1, DC - 1))
                        x.then_inc(s_h, 1)
                    t.wait_ge(s_xg[(j + 1) % 2], (k * 2 + ((j + 1) // 2 + 1)) * 16)
                    turn((j + 1) % 2)
                    t.wait_ge(s_hl, u * FC + (FC + 4))
                    for r in range(HT4):
                        if r >= 2:
                            t.wait_ge(s_yb, 1 + u * HT4 + (r - 1))
                        else:
                            t.wait_ge(s_yb, 1 + u * HT4)
                        for n, (p, q) in enumerate(TERMS):
                            for f in range(FC):
                                x = mm(bank[4 + r % 2][:, 0:D], hT[p][:, f, r * P:(r + 1) * P], W2S[i][q][:, f, :],
                                       start=(n, f) == (0, 0), stop=(n, f) == (len(TERMS) - 1, FC - 1))
                        x.then_inc(s_y, 1)

        @block.scalar
        def _(s_):
            s_.wait_ge(s_d, 2)
            s_.activation(pr[:, :, :], pr[:, :, :], ACT.Exp).then_inc(s_a1, 1)
            s_.sem_inc(s_hid, 4)

            def split(i, piece):
                W, head, rest = piece
                s_.activation(head, W, ACT.Copy).then_inc(s_wh[i], 1)

            def take(i):
                for c in range(DC):
                    s_.activation(xgT[i][0][:, c, :], bank[c][:, :], ACT.Copy).then_inc(s_xh, 1)

            s_.wait_ge(s_w[0], 32)
            for piece in pieces(0):
                split(0, piece)
            s_.wait_ge(s_xt, 2)
            take(0)
            with s_.Fori(0, NE // 2) as k:
                for j in range(4):
                    u, e, other = k * 4 + j, k * 2 + j // 2, 1 - j // 2
                    piece = pieces(other)
                    for f in range(FC):
                        free = now(s_, u * FC + (f + 1))
                        wait_first(s_, (s_bt, 1), s_h, u * FC + (f + 1))
                        s_.wait_ge(s_hl, free)
                        s_.activation(hid[:, f % 4, :], bank[HB[f % 4]][:, :], ACT.Relu, bias=b1T[:, bass.ds(e, 1), f]).then_inc(s_hid, 1)
                        if j % 2 == 0 and f % 2:
                            if f == 1:
                                s_.wait_ge(s_w[other], (k + (1 if other else 2)) * 32)
                            split(other, next(piece))
                    s_.wait_ge(s_xt, u + 3)
                    take((j + 1) % 2)

        @block.vector
        def _(v):
            count = [0]

            def link(ins):
                count[0] += 1
                ins.then_inc(s_d, 1)
                v.wait_ge(s_d, count[0])

            def each(x):
                return x[:, :].unsqueeze(2).broadcast_to([P, NT, NE])

            def const(c):
                return cst[:, c:c + NE].unsqueeze(1).broadcast_to([P, NT, NE])

            A = lambda x: x[:, :, :]
            tt, sc = v.tensor_tensor, v.tensor_scalar
            link(v.tensor_reduce(mx[:, :], A(logits), AX, ALU.max))
            link(tt(A(pr), A(logits), each(mx), ALU.subtract))

            def first_max(src, m, dst):
                link(tt(A(eq), A(src), each(m), ALU.is_equal))
                link(tt(A(key), A(eq), const(C_FIRST), ALU.mult))
                link(v.tensor_reduce(kx[:, :], A(key), AX, ALU.max))
                link(tt(A(dst), A(key), each(kx), ALU.is_equal))

            first_max(logits, mx, m1)
            v.tensor_copy(kx1[:, :], kx[:, :])
            v.tensor_copy(w[:, 0:1], kx[:, 0:1]).then_inc(s_ex, 1)
            link(v.scalar_tensor_tensor(A(l2), A(m1), -3.0e38, A(logits), ALU.mult, ALU.add))
            link(v.tensor_reduce(mx[:, :], A(l2), AX, ALU.max))
            first_max(l2, mx, m2)
            v.tensor_copy(w[:, 0:1], kx[:, 0:1]).then_inc(s_ex, 1)
            v.wait_ge(s_a1, 1)
            link(v.tensor_reduce(zs[:, :], A(pr), AX, ALU.add))
            link(v.reciprocal(zs[:, :], zs[:, :]))
            link(tt(A(pr), A(pr), each(zs), ALU.mult))

            v.wait_ge(s_bt, 1)
            v.tensor_copy(b1T[:, :, :].rearrange("p e f -> p (e f)"), bank[7][:, 0:NE * FC])

            def places(i, m, loc, first_total):
                v.wait_ge(s_cum, i + 1)
                view = lambda b: bank[b][:, 0:NT * NE].rearrange("p (n e) -> p n e", e=NE)
                link(v.tensor_copy(A(tot), view(2 * i + 1)))
                link(sc(A(loc), view(2 * i), -1.0, None, ALU.add))
                link(v.tensor_copy(A(run), A(tot)))
                src, dst, step = run, cum, 1
                while step < NT:
                    v.tensor_copy(dst[:, 0:step, :], src[:, 0:step, :])
                    link(tt(dst[:, step:NT, :], src[:, step:NT, :], src[:, 0:NT - step, :], ALU.add))
                    src, dst, step = dst, src, 2 * step
                link(tt(loc[:, 1:NT, :], loc[:, 1:NT, :], src[:, 0:NT - 1, :], ALU.add))
                if first_total is not None:
                    link(tt(A(loc), A(loc), first_total[:, :, :].broadcast_to([P, NT, NE]), ALU.add))
                return src

            def use(m, loc, t_, g_, f_, put):
                link(v.scalar_tensor_tensor(A(keep), A(loc), float(CAP), A(m), ALU.is_lt, ALU.mult))
                link(v.tensor_reduce(g_[:, :], A(keep), AX, ALU.add))
                link(tt(A(key), A(keep), A(pr), ALU.mult))
                link(v.tensor_reduce(t_[:, :], A(key), AX, ALU.add))
                link(sc(A(key), A(loc), float(CAP - 1), None, ALU.min))
                link(tt(A(key), A(key), const(C_BASE), ALU.add))
                link(tt(A(key), A(key), A(m), ALU.mult))
                link(v.tensor_reduce(f_[:, :], A(key), AX, ALU.add))
                link(sc(w[:, :], g_[:, :], -float(NE * CAP), float(NE * CAP), ALU.mult, ALU.add))
                link(tt(w[:, :], w[:, :], f_[:, :], ALU.add))
                link(v.tensor_copy(put[:, :], w[:, :]))

            src = places(0, m1, loc1, None)
            total1 = sb("total1", [P, 1, NE])
            link(v.tensor_copy(total1[:, :, :], src[:, NT - 1:NT, :]))
            places(1, m2, loc2, total1)
            use(m1, loc1, t1, g1, f1, put1)
            use(m2, loc2, t2, g2, f2, put2)
            v.tensor_copy(w[:, 0:1], kx[:, 0:1]).then_inc(s_routed, 1)
            link(tt(den[:, :], t1[:, :], t2[:, :], ALU.add))
            link(sc(den[:, :], den[:, :], 1.1920929e-07, None, ALU.max))
            link(v.reciprocal(den[:, :], den[:, :]))
            for t_, g_ in ((t1, g1), (t2, g2)):
                link(tt(t_[:, :], t_[:, :], den[:, :], ALU.mult))
                link(v.scalar_tensor_tensor(g_[:, :], t_[:, :], GAIN, g_[:, :], ALU.mult, ALU.mult))
            def split(i, piece, done):
                W, head, rest = piece
                v.wait_ge(s_wh[i], done)
                v.tensor_tensor(rest, W, head.bitcast(F32), ALU.subtract).then_inc(s_wl[i], 1)

            for n, piece in enumerate(pieces(0)):
                split(0, piece, n + 1)
            v.tensor_copy(pay[:, :, 0], cst[:, C_ID:C_ID + NT])
            v.tensor_copy(pay[:, :, 1], kx1[:, :])
            v.tensor_copy(pay[:, :, 2], g1[:, :])
            link(v.tensor_copy(pay[:, :, 3], g2[:, :]))
            for n in range(NT):
                if n >= RING:
                    v.wait_ge(s_sc[n % RING], 32 * (n // RING))
                v.tensor_copy(tk[:, n % RING, D:ROW], pay[:, n, :]).then_inc(s_pay, 1)

            v.sem_inc(s_yv, 1)
            v.sem_inc(s_yb, 1)

            v.sem_inc(s_hl, 4)

            def take(i, first):
                for c in range(DC):
                    v.wait_ge(s_xh, first + (c + 1))
                    v.tensor_tensor(xgT[i][1][:, c, :], bank[c][:, :], xgT[i][0][:, c, :].bitcast(F32), ALU.subtract).then_inc(s_xl, 1)

            take(0, 0)
            with v.Fori(0, NE // 2) as k:
                for j in range(4):
                    u, b, e = k * 4 + j, j % 2, k * 2 + j // 2
                    v.wait_ge(s_xg[b], (k * 2 + (j // 2 + 1)) * 16)
                    v.wait_ge(s_added, u + 1)
                    v.scalar_tensor_tensor(where[b][:, :], xg[b][:, :, D], 0.0, cst[:, C_PAST:C_PAST + HT4], ALU.is_equal, ALU.mult)
                    v.tensor_scalar(gate[b][:, :], xg[b][:, :, D + 1], cst[:, bass.ds(C_FIRST + e, 1)], None, ALU.is_equal)
                    v.tensor_tensor(xg[b][:, :, D + 2], xg[b][:, :, D + 2], xg[b][:, :, D + 3], ALU.subtract).then_inc(s_meta, 1)
                    v.wait_ge(s_meta, u * 3 + 1)
                    v.scalar_tensor_tensor(rows_[b][:, :], xg[b][:, :, D], -1.0, where[b][:, :], ALU.add, ALU.add)
                    v.tensor_tensor(gate[b][:, :], gate[b][:, :], xg[b][:, :, D + 2], ALU.mult).then_inc(s_meta, 1)
                    v.wait_ge(s_meta, u * 3 + 2)
                    v.tensor_tensor(gate[b][:, :], gate[b][:, :], xg[b][:, :, D + 3], ALU.add).then_inc(s_meta, 1)
                    other, piece = 1 - j // 2, pieces(1 - j // 2)
                    for f in range(FC):
                        v.wait_ge(s_hid, u * FC + (f + 5))
                        v.tensor_copy(hT[0][:, f, :], hid[:, f % 4, :]).then_inc(s_hh, 1)
                        v.wait_ge(s_hh, u * FC + (f + 1))
                        v.tensor_tensor(hT[1][:, f, :], hid[:, f % 4, :], hT[0][:, f, :].bitcast(F32), ALU.subtract).then_inc(s_hl, 1)
                        if j % 2 == 0 and f % 2:
                            split(other, next(piece), (k + (0 if other else 1)) * PIECES + ((f + 1) // 2))
                    take((j + 1) % 2, u * DC + DC)
                    for r in range(HT4):
                        v.wait_ge(s_y, 1 + u * HT4 + (r + 1))
                        v.tensor_tensor(yo[b][:, r, :], bank[4 + r % 2][:, 0:D], B2[:, bass.ds(e, 1), :].squeeze(1), ALU.add).then_inc(s_yb, 1)
                        v.wait_ge(s_yb, 1 + u * HT4 + (r + 1))
                        v.tensor_scalar(yo[b][:, r, :], yo[b][:, r, :], gate[b][:, r:r + 1], None, ALU.mult).then_inc(s_yv, 1)


def program(nc, a, out):
    B, S, D = a["x"].shape
    T, NE = B * S, a["L1_ffn_w1"].shape[0]
    CAP = -(-T // 4)
    scratch = {n: nc.dram_tensor(f"{n}_dram", shape, F32, kind="Internal").ap()
               for n, shape in (("tokens", (T, D)), ("slots", (NE * CAP, ROW)))}
    with ExitStack() as stack:
        def sem(name):
            return stack.enter_context(nc.semaphore(name))

        cst_t = stack.enter_context(nc.sbuf_tensor("cst", [P, C_ALL], F32))
        ones_t = stack.enter_context(nc.sbuf_tensor("ones", [P, P], F32))
        logits = stack.enter_context(nc.sbuf_tensor("logits", [P, T // P, NE], F32))
        bank = [stack.enter_context(nc.psum_tensor(f"bank{i}", [P, 512], F32)) for i in range(8)]
        ident, ones = cst_t[:, C_IDENT:C_IDENT + P], ones_t[:, :]
        layers(nc, a, out, scratch, sem, ident, ones_t, cst_t, logits, bank)
        experts(nc, a, out, scratch, sem, ident, ones, cst_t, logits, bank)


_UNUSED = ("L0_ffn_gate_w",)


def constants(NE, CAP, T):
    import numpy as np

    c = np.zeros((P, C_ALL), np.float32)
    p = np.arange(P)
    for width, at in C_MASK.items():
        for j in range(SLOT // width):
            c[:, at + j] = p % SLOT // width == j
    for j in range(4):
        c[MROW + j, C_SEL + j] = c[MROW + 4 + j, C_SEL + j] = 1.0
    c[:, C_HALF:C_HALF + 4] = -0.5
    c[:, C_FIRST:C_FIRST + NE] = NE - np.arange(NE)
    c[:, C_BASE:C_BASE + NE] = CAP * np.arange(NE)
    c[:, C_TRI:C_TRI + P] = p[:, None] <= p[None, :]
    c[:, C_IDENT:C_IDENT + P] = np.eye(P)
    c[:, C_PAST:C_PAST + 4] = T + p[:, None] + 1
    c[:, C_ID:C_ID + T // P] = np.arange(T).reshape(-1, P).T + 1
    return c


def kernel(**inputs):
    import numpy as _np
    import concourse.bacc as _bacc
    from concourse import mybir as _mybir
    from concourse.bass_utils import run_bass_kernel_spmd as _run

    nc = _bacc.Bacc("TRN2", target_bir_lowering=False, num_devices=1)
    arrays, args = {}, {}
    named = {n: _np.ascontiguousarray(v) for n, v in inputs.items() if n not in _UNUSED}
    B, S, D = named["x"].shape
    named["constants"] = constants(named["L1_ffn_w1"].shape[0], -(-B * S // 4), B * S)
    for name, v in named.items():
        arrays[f"in_{name}_dram"] = v
        args[name] = nc.dram_tensor(f"in_{name}_dram", v.shape, _mybir.dt.from_np(v.dtype), kind="ExternalInput").ap()
    out = nc.dram_tensor("out_0_dram", (B * S + P, D), _mybir.dt.from_np(named["x"].dtype), kind="ExternalOutput").ap()
    program(nc, args, out)
    r = _run(nc, [arrays], core_ids=[0])
    return r.results[0]["out_0_dram"][:B * S].reshape(B, S, D)
```
